# Optimizing a Trainium2 kernel written in Bass

```python
import numpy as np
import jax
import jax.numpy as jnp

def _softmax(x, axis=-1):
    return jax.nn.softmax(x, axis=axis)

def _gelu(x):
    return jax.nn.gelu(x, approximate=True)

def _silu(x):
    return jax.nn.silu(x)

def _sigmoid(x):
    return jax.nn.sigmoid(x)

def _layernorm(x, axis=-1, eps=1e-05):
    m = jnp.mean(x, axis=axis, keepdims=True)
    v = jnp.var(x, axis=axis, keepdims=True)
    return (x - m) / jnp.sqrt(v + eps)

def _scatter_add(tgt, idx, src, axis=0):
    return tgt.at[idx].add(src)

def _segment_sum(src, seg, n):
    return jax.ops.segment_sum(src, seg, n)
kernel_name = 'mk_seq_preln_d2_jaxref_r4_a45f63'

def setup_inputs(seed: int=0):
    np.random.seed(seed)
    _w = jnp.asarray

    def _L0_attn_setup():
        import jax, jax.numpy as jnp
        import numpy as np
        DIM = 256
        HEADS = 16
        HEAD_DIM = DIM // HEADS
        B, N = (2, 512)
        SCALE = 1.0 / np.float32(np.sqrt(DIM))

        def _split_heads(t):
            b, n, _ = t.shape
            return jnp.moveaxis(t.reshape(b, n, HEADS, HEAD_DIM), 2, 0)
        key = jax.random.key(seed)
        ks = jax.random.split(key, 9)
        s = 0.02
        return {'x': jax.random.normal(ks[0], (B, N, DIM), dtype=jnp.float32), 'Wq': jax.random.normal(ks[1], (DIM, DIM), dtype=jnp.float32) * s, 'bq': jax.random.normal(ks[2], (DIM,), dtype=jnp.float32) * s, 'Wk': jax.random.normal(ks[3], (DIM, DIM), dtype=jnp.float32) * s, 'bk': jax.random.normal(ks[4], (DIM,), dtype=jnp.float32) * s, 'Wv': jax.random.normal(ks[5], (DIM, DIM), dtype=jnp.float32) * s, 'bv': jax.random.normal(ks[6], (DIM,), dtype=jnp.float32) * s, 'Wo': jax.random.normal(ks[7], (DIM, DIM), dtype=jnp.float32) * s, 'bo': jax.random.normal(ks[8], (DIM,), dtype=jnp.float32) * s}
    _L0_attn_in = _L0_attn_setup()

    def _L0_ffn_setup():
        import jax, jax.numpy as jnp
        import numpy as np
        D_MODEL = 256
        HIDDEN = 1024
        N_ROUTING = 2
        key = jax.random.key(seed)
        ks = jax.random.split(key, 10)
        s = 0.02
        x = jax.random.normal(ks[0], (4, 1024, D_MODEL), dtype=jnp.float32)
        gate_w = jax.random.normal(ks[1], (N_ROUTING, D_MODEL), dtype=jnp.float32) * s
        w1 = jax.random.normal(ks[2], (N_ROUTING, D_MODEL, HIDDEN), dtype=jnp.float32) * s
        b1 = jax.random.normal(ks[3], (N_ROUTING, HIDDEN), dtype=jnp.float32) * s
        w2 = jax.random.normal(ks[4], (N_ROUTING, HIDDEN, D_MODEL), dtype=jnp.float32) * s
        b2 = jax.random.normal(ks[5], (N_ROUTING, D_MODEL), dtype=jnp.float32) * s
        sw1 = jax.random.normal(ks[6], (D_MODEL, HIDDEN), dtype=jnp.float32) * s
        sb1 = jax.random.normal(ks[7], (HIDDEN,), dtype=jnp.float32) * s
        sw2 = jax.random.normal(ks[8], (HIDDEN, D_MODEL), dtype=jnp.float32) * s
        sb2 = jax.random.normal(ks[9], (D_MODEL,), dtype=jnp.float32) * s
        return {'x': x, 'gate_w': gate_w, 'w1': w1, 'b1': b1, 'w2': w2, 'b2': b2, 'sw1': sw1, 'sb1': sb1, 'sw2': sw2, 'sb2': sb2}
    _L0_ffn_in = _L0_ffn_setup()

    def _L1_attn_setup():
        import jax, jax.numpy as jnp
        import numpy as np
        B, N, H = (4, 1024, 256)
        NUM_HEADS = 16
        HEAD_DIM = H // NUM_HEADS
        EPS = 1e-05

        def _layernorm(x, g, b):
            mu = jnp.mean(x, axis=-1, keepdims=True)
            var = jnp.mean(jnp.square(x - mu), axis=-1, keepdims=True)
            return (x - mu) * jax.lax.rsqrt(var + EPS) * g + b
        key = jax.random.key(seed)
        ks = jax.random.split(key, 12)
        s = 0.02
        return {'x': jax.random.normal(ks[0], (B, N, H), dtype=jnp.float32), 'w_qkv': jax.random.normal(ks[1], (3 * H, H), dtype=jnp.float32) * s, 'b_qkv': jax.random.normal(ks[2], (3 * H,), dtype=jnp.float32) * s, 'w_g1': jax.random.normal(ks[3], (HEAD_DIM, H), dtype=jnp.float32) * s, 'b_g1': jax.random.normal(ks[4], (HEAD_DIM,), dtype=jnp.float32) * s, 'w_g2': jax.random.normal(ks[5], (H, HEAD_DIM), dtype=jnp.float32) * s, 'b_g2': jax.random.normal(ks[6], (H,), dtype=jnp.float32) * s, 'w_out': jax.random.normal(ks[7], (H, H), dtype=jnp.float32) * s, 'b_out': jax.random.normal(ks[8], (H,), dtype=jnp.float32) * s, 'ln_g': jnp.ones((H,), dtype=jnp.float32), 'ln_b': jnp.zeros((H,), dtype=jnp.float32)}
    _L1_attn_in = _L1_attn_setup()

    def _L1_ffn_setup():
        import jax, jax.numpy as jnp
        import numpy as np
        B, S, D = (4, 128, 256)
        E, K, H = (64, 8, 64)
        ES, HS = (2, 512)
        key = jax.random.key(seed)
        ks = jax.random.split(key, 8)
        scale = 0.02
        rn = lambda k, shape, s: jax.random.normal(k, shape, jnp.float32) * s
        return {'x': rn(ks[0], (B, S, D), 1.0), 'router_w': rn(ks[1], (D, E), scale), 'router_b': jnp.zeros((E,), jnp.float32), 'w1': rn(ks[2], (E, D, H), scale), 'b1': jnp.zeros((E, H), jnp.float32), 'w2': rn(ks[3], (E, H, D), scale), 'b2': jnp.zeros((E, D), jnp.float32), 'sw1': rn(ks[4], (ES, D, HS), scale), 'sb1': jnp.zeros((ES, HS), jnp.float32), 'sw2': rn(ks[5], (ES, HS, D), scale), 'sb2': jnp.zeros((ES, D), jnp.float32)}
    _L1_ffn_in = _L1_ffn_setup()
    _d = {'L0_attn_x': _L0_attn_in['x'], 'L0_attn_Wq': _L0_attn_in['Wq'], 'L0_attn_bq': _L0_attn_in['bq'], 'L0_attn_Wk': _L0_attn_in['Wk'], 'L0_attn_bk': _L0_attn_in['bk'], 'L0_attn_Wv': _L0_attn_in['Wv'], 'L0_attn_bv': _L0_attn_in['bv'], 'L0_attn_Wo': _L0_attn_in['Wo'], 'L0_attn_bo': _L0_attn_in['bo'], 'L0_ffn_gate_w': _L0_ffn_in['gate_w'], 'L0_ffn_w1': _L0_ffn_in['w1'], 'L0_ffn_b1': _L0_ffn_in['b1'], 'L0_ffn_w2': _L0_ffn_in['w2'], 'L0_ffn_b2': _L0_ffn_in['b2'], 'L0_ffn_sw1': _L0_ffn_in['sw1'], 'L0_ffn_sb1': _L0_ffn_in['sb1'], 'L0_ffn_sw2': _L0_ffn_in['sw2'], 'L0_ffn_sb2': _L0_ffn_in['sb2'], 'L1_attn_w_qkv': _L1_attn_in['w_qkv'], 'L1_attn_b_qkv': _L1_attn_in['b_qkv'], 'L1_attn_w_g1': _L1_attn_in['w_g1'], 'L1_attn_b_g1': _L1_attn_in['b_g1'], 'L1_attn_w_g2': _L1_attn_in['w_g2'], 'L1_attn_b_g2': _L1_attn_in['b_g2'], 'L1_attn_w_out': _L1_attn_in['w_out'], 'L1_attn_b_out': _L1_attn_in['b_out'], 'L1_attn_ln_g': _L1_attn_in['ln_g'], 'L1_attn_ln_b': _L1_attn_in['ln_b'], 'L1_ffn_router_w': _L1_ffn_in['router_w'], 'L1_ffn_router_b': _L1_ffn_in['router_b'], 'L1_ffn_w1': _L1_ffn_in['w1'], 'L1_ffn_b1': _L1_ffn_in['b1'], 'L1_ffn_w2': _L1_ffn_in['w2'], 'L1_ffn_b2': _L1_ffn_in['b2'], 'L1_ffn_sw1': _L1_ffn_in['sw1'], 'L1_ffn_sb1': _L1_ffn_in['sb1'], 'L1_ffn_sw2': _L1_ffn_in['sw2'], 'L1_ffn_sb2': _L1_ffn_in['sb2']}
    _x0 = _d['L0_attn_x']
    _d['L0_attn_x'] = jax.random.normal(jax.random.fold_in(jax.random.key(seed), 1), (1, 4096, 256), dtype=_x0.dtype)
    del _x0
    return _d

def reference(L0_attn_x, L0_attn_Wq, L0_attn_bq, L0_attn_Wk, L0_attn_bk, L0_attn_Wv, L0_attn_bv, L0_attn_Wo, L0_attn_bo, L0_ffn_gate_w, L0_ffn_w1, L0_ffn_b1, L0_ffn_w2, L0_ffn_b2, L0_ffn_sw1, L0_ffn_sb1, L0_ffn_sw2, L0_ffn_sb2, L1_attn_w_qkv, L1_attn_b_qkv, L1_attn_w_g1, L1_attn_b_g1, L1_attn_w_g2, L1_attn_b_g2, L1_attn_w_out, L1_attn_b_out, L1_attn_ln_g, L1_attn_ln_b, L1_ffn_router_w, L1_ffn_router_b, L1_ffn_w1, L1_ffn_b1, L1_ffn_w2, L1_ffn_b2, L1_ffn_sw1, L1_ffn_sb1, L1_ffn_sw2, L1_ffn_sb2):

    def _L0_attn_ref(x, Wq, bq, Wk, bk, Wv, bv, Wo, bo):
        import jax, jax.numpy as jnp
        import numpy as np
        DIM = 256
        HEADS = 16
        HEAD_DIM = DIM // HEADS
        B, N = (2, 512)
        SCALE = 1.0 / np.float32(np.sqrt(DIM))

        def _split_heads(t):
            b, n, _ = t.shape
            return jnp.moveaxis(t.reshape(b, n, HEADS, HEAD_DIM), 2, 0)
        q = _split_heads(x @ Wq.T + bq)
        k = _split_heads(x @ Wk.T + bk)
        v = _split_heads(x @ Wv.T + bv)
        scores = jnp.einsum('hbnd,hbmd->hbnm', k, q) * SCALE
        attn = jax.nn.softmax(scores, axis=-1)
        out = jnp.einsum('hbnm,hbmd->hbnd', attn, v)
        out = jnp.moveaxis(out, 0, 2).reshape(x.shape[0], x.shape[1], DIM)
        return out @ Wo.T + bo

    def _L0_ffn_ref(x, gate_w, w1, b1, w2, b2, sw1, sb1, sw2, sb2):
        import jax, jax.numpy as jnp
        import numpy as np
        D_MODEL = 256
        HIDDEN = 1024
        N_ROUTING = 2
        B, S, D = x.shape
        xf = x.reshape(-1, D)
        gate_scores = xf @ gate_w.T
        gate_probs = jax.nn.softmax(gate_scores, axis=-1)
        top1 = jnp.argmax(gate_probs, axis=-1)
        one_hot = jax.nn.one_hot(top1, N_ROUTING, dtype=xf.dtype)
        masked = xf[None, :, :] * one_hot.T[:, :, None]
        h = jax.nn.relu(jnp.einsum('end,edh->enh', masked, w1) + b1[:, None, :])
        expert_out = jnp.einsum('enh,ehd->end', h, w2) + b2[:, None, :]
        routing_output = expert_out.sum(axis=0)
        shared = jax.nn.relu(xf @ sw1 + sb1) @ sw2 + sb2
        return (routing_output + shared).reshape(B, S, D)

    def _L1_attn_ref(x, w_qkv, b_qkv, w_g1, b_g1, w_g2, b_g2, w_out, b_out, ln_g, ln_b):
        import jax, jax.numpy as jnp
        import numpy as np
        B, N, H = (4, 1024, 256)
        NUM_HEADS = 16
        HEAD_DIM = H // NUM_HEADS
        EPS = 1e-05

        def _layernorm(x, g, b):
            mu = jnp.mean(x, axis=-1, keepdims=True)
            var = jnp.mean(jnp.square(x - mu), axis=-1, keepdims=True)
            return (x - mu) * jax.lax.rsqrt(var + EPS) * g + b
        b, n, hdim = x.shape
        qkv = jnp.einsum('bnh,oh->bno', x, w_qkv) + b_qkv
        q, k, v = jnp.split(qkv, 3, axis=-1)

        def split_heads(t):
            return t.reshape(b, n, NUM_HEADS, HEAD_DIM).transpose(0, 2, 1, 3)
        q, k, v = (split_heads(q), split_heads(k), split_heads(v))
        q = jax.nn.silu(q)
        k = jax.nn.softmax(k, axis=-2)
        if n <= HEAD_DIM:
            attn = jnp.einsum('bhnd,bhmd->bhnm', q, k)
            out = jnp.einsum('bhnm,bhmd->bhnd', attn, v)
        else:
            kv = jnp.einsum('bhnd,bhne->bhde', k, v)
            out = jnp.einsum('bhnd,bhde->bhne', q, kv)
        out = out.transpose(0, 2, 1, 3).reshape(b, n, hdim)
        out = _layernorm(out, ln_g, ln_b)
        gate_hidden = jnp.einsum('bnh,dh->bnd', x, w_g1) + b_g1
        gate = jax.nn.sigmoid(jnp.einsum('bnd,hd->bnh', gate_hidden, w_g2) + b_g2)
        out = out * gate
        out = jnp.einsum('bnh,oh->bno', out, w_out) + b_out
        return out

    def _L1_ffn_ref(x, router_w, router_b, w1, b1, w2, b2, sw1, sb1, sw2, sb2):
        import jax, jax.numpy as jnp
        import numpy as np
        B, S, D = (4, 128, 256)
        E, K, H = (64, 8, 64)
        ES, HS = (2, 512)
        b_, s_, d_ = x.shape
        xf = x.reshape(-1, d_)
        probs = jax.nn.softmax(xf @ router_w + router_b, axis=-1)
        tw, ti = jax.lax.top_k(probs, K)
        tw = tw / jnp.sum(tw, axis=-1, keepdims=True)

        def body(acc, p):
            W1, B1, W2, B2, e = p
            h = jax.nn.silu(xf @ W1 + B1) @ W2 + B2
            cw = jnp.sum(jnp.where(ti == e, tw, 0.0), axis=-1)
            return (acc + cw[:, None] * h, None)
        routed, _ = jax.lax.scan(body, jnp.zeros_like(xf), (w1, b1, w2, b2, jnp.arange(w1.shape[0])))

        def shared_mlp(W1, B1, W2, B2):
            return jax.nn.silu(xf @ W1 + B1) @ W2 + B2
        shared = jnp.sum(jax.vmap(shared_mlp)(sw1, sb1, sw2, sb2), axis=0)
        return (routed + shared).reshape(b_, s_, d_)
    x = L0_attn_x
    x = x + _L0_attn_ref(_layernorm(x, axis=-1), L0_attn_Wq, L0_attn_bq, L0_attn_Wk, L0_attn_bk, L0_attn_Wv, L0_attn_bv, L0_attn_Wo, L0_attn_bo)
    x = x + _L0_ffn_ref(_layernorm(x, axis=-1), L0_ffn_gate_w, L0_ffn_w1, L0_ffn_b1, L0_ffn_w2, L0_ffn_b2, L0_ffn_sw1, L0_ffn_sb1, L0_ffn_sw2, L0_ffn_sb2)
    x = x + _L1_attn_ref(_layernorm(x, axis=-1), L1_attn_w_qkv, L1_attn_b_qkv, L1_attn_w_g1, L1_attn_b_g1, L1_attn_w_g2, L1_attn_b_g2, L1_attn_w_out, L1_attn_b_out, L1_attn_ln_g, L1_attn_ln_b)
    x = x + _L1_ffn_ref(_layernorm(x, axis=-1), L1_ffn_router_w, L1_ffn_router_b, L1_ffn_w1, L1_ffn_b1, L1_ffn_w2, L1_ffn_b2, L1_ffn_sw1, L1_ffn_sb1, L1_ffn_sw2, L1_ffn_sb2)
    return x

_drawn_inputs = setup_inputs


def setup_inputs(seed=0):
    import zlib

    import numpy as np

    out = dict(_drawn_inputs(seed))
    spreads = {'L1_attn_ln_g': (1.0, 0.6),
     'L1_attn_ln_b': (0.0, 0.542),
     'L1_ffn_router_b': (0.0, 0.353),
     'L1_ffn_b1': (0.0, 0.8),
     'L1_ffn_b2': (0.0, 0.719),
     'L1_ffn_sb1': (0.0, 0.8),
     'L1_ffn_sb2': (0.0, 0.1)}
    factors = {'L0_attn_Wq': 8.0,
     'L0_attn_bq': 64.0,
     'L0_attn_Wk': 8.0,
     'L0_attn_bk': 8.0,
     'L0_attn_Wv': 8.0,
     'L0_attn_bv': 4.067,
     'L0_attn_Wo': 5.192,
     'L0_ffn_b1': 12.35,
     'L0_ffn_sb1': 16.877,
     'L1_attn_w_g1': 8.0,
     'L1_attn_b_g1': 64.0,
     'L1_attn_w_g2': 8.0,
     'L1_attn_b_g2': 63.64,
     'L1_attn_b_out': 3.034,
     'L1_ffn_w1': 6.338,
     'L1_ffn_w2': 5.992,
     'L0_attn_bo': 5.725,
     'L0_ffn_b2': 4.42,
     'L0_ffn_sb2': 5.208}
    for name, (base, spread) in spreads.items():
        noise = np.random.default_rng([zlib.crc32(name.encode()), seed]).standard_normal(out[name].shape)
        drawn = base * np.exp(spread * noise) if base else spread * noise
        out[name] = jnp.asarray(drawn.astype(out[name].dtype))
    for name, factor in factors.items():
        out[name] = (out[name] * factor).astype(out[name].dtype)
    return out
```

```python
from contextlib import ExitStack

import concourse.bass as bass
from concourse import mybir

F32 = mybir.dt.float32
F32R = mybir.dt.float32r
BF16 = mybir.dt.bfloat16
ALU = mybir.AluOpType
ACT = mybir.ActivationFunctionType
AX = mybir.AxisListType

P = 128
D = 256
KC = D // P
T = 4096
TB = 512
NB = T // TB
TT = TB // P
HEADS = 16
HD = D // HEADS
EPS = 1e-5


def ds(i, n):
    return bass.ds(i * n, n)


def alone(eng, passed):
    eng.sem_inc(passed, 1)


def feature_major(ap):
    return ap.rearrange("(k p) n -> p k n", p=P)


def column(ap):
    return ap.rearrange("(c p) -> p c", p=P)


def product3(nc, out, w, x, first, last):
    nc.tensor.matmul(out, w[0], x[0], start=first, stop=False)
    nc.tensor.matmul(out, w[0], x[1], start=False, stop=False)
    return nc.tensor.matmul(out, w[1], x[0], start=False, stop=last)


def project3(nc, out, w, x, cols, first=True, last=True):
    for k in range(KC):
        mm = product3(nc, out, [v[:, k, cols] for v in w], [v[:, k, :] for v in x],
                      first and k == 0, last and k == KC - 1)
    return mm


class PhaseSemaphores:

    def __init__(self, nc, phase):
        self.nc, self.phase, self.held, self.from_zero = nc, phase, [], []

    def __call__(self, name, from_zero=False):
        self.held.append(self.nc.alloc_semaphore(f"{self.phase}_{name}"))
        if from_zero:
            self.from_zero.append(len(self.held) - 1)
        return self.held[-1]

    def start(self):
        for n, s in enumerate(self.held):
            if n not in self.from_zero:
                self.nc.gpsimd.sem_inc(s, FIRST)
        self.nc.all_engine_barrier()

    def __enter__(self):
        return self

    def __exit__(self, *_):
        self.nc.clear_and_free_semaphores(self.held)
        self.nc.all_engine_barrier()


FIRST = 1


def count(events):
    return events + FIRST


class LayerNorm:

    def __init__(self, name, nc, sb, sem, ones, x, x_ready, mean_ps, var_ps, slots=1):
        self.nc, self.ones, self.x, self.x_ready = nc, ones, x, x_ready
        self.mean_ps, self.var_ps = mean_ps, var_ps
        self.xc = sb(f"{name}_xc", [P, KC, TB], F32)
        self.sq = sb(f"{name}_sq", [P, KC, TB], F32)
        self.std = sb(f"{name}_std", [P, TB], F32)
        self.xn = self.sq
        self.cut = [[sb(f"{name}_{p}{s}", [P, KC, TB], F32R) for p in ("hi", "lo")] for s in range(slots)]
        self.mean_ready, self.centred, self.squared, self.var_ready, self.std_ready, self.rstd_ready, \
            self.normed, self.hi_ready, self.lo_ready = (
                sem(f"{name}_{s}") for s in ("mean", "centred", "squared", "var", "std", "rstd",
                                             "normed", "hi", "lo"))

    def tensor_mean(self, pe, i, slot=0):
        pe.wait_ge(self.x_ready, count(i + 1))
        self.tensor_mean_of_ready(slot)

    def tensor_mean_of_ready(self, slot=0):
        for k in range(KC):
            mm = self.nc.tensor.matmul(self.mean_ps, self.ones[:, :], self.x[slot][:, k, :],
                                       start=(k == 0), stop=(k == KC - 1))
        mm.then_inc(self.mean_ready, 1)

    def tensor_var(self, pe, i):
        pe.wait_ge(self.squared, count(i + 1))
        for k in range(KC):
            mm = self.nc.tensor.matmul(self.var_ps, self.ones[:, :], self.sq[:, k, :],
                                       start=(k == 0), stop=(k == KC - 1))
        mm.then_inc(self.var_ready, 1)

    def vector_centre(self, dve, i, slot=0):
        dve.wait_ge(self.mean_ready, count(i + 1))
        mean = self.mean_ps.unsqueeze(1).to_broadcast([P, KC, TB])
        self.nc.vector.tensor_tensor(self.xc[:, :, :], self.x[slot][:, :, :], mean,
                                     ALU.subtract).then_inc(self.centred, 1)

    def vector_reciprocal(self, dve, i):
        dve.wait_ge(self.std_ready, count(i + 1))
        self.nc.vector.reciprocal(self.std[:, :], self.std[:, :]).then_inc(self.rstd_ready, 1)

    def vector_scale(self, dve, i):
        dve.wait_ge(self.rstd_ready, count(i + 1))
        rstd = self.std[:, :].unsqueeze(1).to_broadcast([P, KC, TB])
        self.nc.vector.tensor_tensor(self.xn[:, :, :], self.xc[:, :, :], rstd,
                                     ALU.mult).then_inc(self.normed, 1)

    def vector_lo(self, dve, i, slot=0):
        dve.wait_ge(self.hi_ready, count(i + 1))
        hi, lo = self.cut[slot]
        self.nc.vector.tensor_tensor(lo[:, :, :], self.xn[:, :, :], hi[:, :, :].bitcast(F32),
                                     ALU.subtract).then_inc(self.lo_ready, 1)

    def scalar_square(self, act, i):
        act.wait_ge(self.centred, count(i + 1))
        self.nc.scalar.activation(self.sq[:, :, :], self.xc[:, :, :], ACT.Square).then_inc(self.squared, 1)

    def scalar_std(self, act, i, eps):
        act.wait_ge(self.var_ready, count(i + 1))
        self.nc.scalar.activation(self.std[:, :], self.var_ps, ACT.Sqrt,
                                  bias=eps[:, 0:1]).then_inc(self.std_ready, 1)

    def scalar_hi(self, act, i, slot=0):
        act.wait_ge(self.normed, count(i + 1))
        self.nc.scalar.copy(self.cut[slot][0][:, :, :], self.xn[:, :, :]).then_inc(self.hi_ready, 1)


def overlapped(eng, body):
    with eng.Fori(0, NB // 2 - 1) as half:
        for slot in range(2):
            body(half, half * 2 + slot, slot, 2)
    for slot in range(2):
        body(NB // 2 - 1, NB - 2 + slot, slot, 1 - slot)



NATURAL = [("L0_attn_Wq", 2), ("L0_attn_Wk", 2), ("L0_attn_Wv", 2), ("L0_attn_Wo", 2),
           ("L1_attn_w_qkv", 6), ("L1_attn_w_out", 2)]
CHUNKS = sum(n for _, n in NATURAL)


def chunk_of(name):
    at = 0
    for n, c in NATURAL:
        if n == name:
            return at * P
        at += c


def setup_phase(nc, d, K):
    with ExitStack() as ctx:
        sb = lambda n, s, t: ctx.enter_context(nc.sbuf_tensor(n, s, t))
        sem = ctx.enter_context(PhaseSemaphores(nc, "setup"))
        natural = sb("natural", [P, CHUNKS, D], F32)
        g1_nat = sb("g1_nat", [HD, D], F32)
        g2_nat = sb("g2_nat", [P, KC, HD], F32)
        ps = ctx.enter_context(nc.psum_tensor("setup_ps", [P, 4, TB], F32))
        loaded, zeroed, consts = sem("w_loaded"), sem("zeroed"), sem("consts")
        turned, hi_done, lo_done = sem("turned"), sem("w_hi_done"), sem("w_lo_done")
        ident_b = sem("ident_bf16")
        wt_hi, wt_lo, ident = K["wt_hi"], K["wt_lo"], K["ident"]
        GROUPS = CHUNKS // 2
        LOADS = len(NATURAL) + 2

        with nc.Block() as block:
            @block.sync
            def _(sp):
                at = 0
                for name, c in NATURAL:
                    sp.dma_start(natural[:, at:at + c, :],
                                 d[name].rearrange("(c p) n -> p c n", p=P)).then_inc(loaded, 16)
                    at += c
                sp.dma_start(g1_nat[:, :], d["L1_attn_w_g1"]).then_inc(loaded, 16)
                sp.dma_start(g2_nat[:, :, :],
                             d["L1_attn_w_g2"].rearrange("(k p) n -> p k n", p=P)).then_inc(loaded, 16)

            @block.gpsimd
            def _(pool):
                nc.gpsimd.memset(ident[:, :], 0.0).then_inc(zeroed, 1)
                nc.gpsimd.memset(K["ones"][:, :], 1.0 / D).then_inc(consts, 1)
                nc.gpsimd.memset(K["eps"][:, :], EPS).then_inc(consts, 1)
                pool.wait_ge(zeroed, 1)
                nc.gpsimd.affine_select(out=ident[:, :], in_=ident[:, :], compare_op=ALU.not_equal,
                                        fill=1.0, base=0, pattern=[[-1, P]],
                                        channel_multiplier=1).then_inc(consts, 1)

            @block.tensor
            def _(pe):
                pe.wait_ge(consts, 3)
                pe.wait_ge(loaded, 16 * LOADS)
                for g in range(GROUPS):
                    if g >= 4:
                        pe.wait_ge(lo_done, g - 3)
                    for c in range(2):
                        for k in range(KC):
                            mm = nc.tensor.transpose(
                                ps[:, g % 4, k * D + c * P:k * D + (c + 1) * P],
                                natural[:, 2 * g + c, k * P:(k + 1) * P], ident[:, :])
                    mm.then_inc(turned, 1)
                pe.wait_ge(lo_done, GROUPS)
                for k in range(KC):
                    nc.tensor.transpose(ps[:, 0, k * HD:(k + 1) * HD], g1_nat[:, k * P:(k + 1) * P],
                                        ident[0:HD, 0:HD])
                for k in range(KC):
                    mm = nc.tensor.transpose(ps[0:HD, 1, k * P:(k + 1) * P], g2_nat[:, k, :],
                                             ident[:, :])
                mm.then_inc(turned, 1)

            @block.scalar
            def _(act):
                act.wait_ge(consts, 3)
                nc.scalar.copy(K["ident_b"][:, :], ident[:, :]).then_inc(ident_b, 1)
                for g in range(GROUPS):
                    act.wait_ge(turned, g + 1)
                    nc.scalar.copy(wt_hi[:, :, g * D:(g + 1) * D],
                                   ps[:, g % 4, :].rearrange("p (k n) -> p k n", k=KC)).then_inc(hi_done, 1)
                act.wait_ge(turned, GROUPS + 1)
                nc.scalar.copy(K["g1_hi"][:, :, :],
                               ps[:, 0, 0:KC * HD].rearrange("p (k n) -> p k n", k=KC)).then_inc(hi_done, 1)
                nc.scalar.copy(K["g2_hi"][:, :], ps[0:HD, 1, 0:D]).then_inc(hi_done, 1)

            @block.vector
            def _(dve):
                for g in range(GROUPS):
                    dve.wait_ge(hi_done, g + 1)
                    nc.vector.tensor_tensor(
                        wt_lo[:, :, g * D:(g + 1) * D], ps[:, g % 4, :].rearrange("p (k n) -> p k n", k=KC),
                        wt_hi[:, :, g * D:(g + 1) * D].bitcast(F32), ALU.subtract).then_inc(lo_done, 1)
                dve.wait_ge(hi_done, GROUPS + 2)
                nc.vector.tensor_tensor(
                    K["g1_lo"][:, :, :], ps[:, 0, 0:KC * HD].rearrange("p (k n) -> p k n", k=KC),
                    K["g1_hi"][:, :, :].bitcast(F32), ALU.subtract)
                nc.vector.tensor_tensor(K["g2_lo"][:, :], ps[0:HD, 1, 0:D],
                                        K["g2_hi"][:, :].bitcast(F32), ALU.subtract)



PARTS = 3


def qkv0_phase(nc, d, K, V_all):
    with ExitStack() as ctx:
        sb = lambda n, s, t: ctx.enter_context(nc.sbuf_tensor(n, s, t))
        sem = ctx.enter_context(PhaseSemaphores(nc, "qkv0"))
        ps = lambda n, s: ctx.enter_context(nc.psum_tensor(n, s, F32))
        x_tok = sb("x_tok", [P, TT, D], F32)
        xT = sb("xT", [P, KC, TB], F32)
        full = sb("full", [P, 2, TB], F32)
        rest = sb("rest", [P, 2, TB], F32)
        parts = sb("parts", [P, 4, PARTS, TB], BF16)
        qk_bias = sb("qk_bias", [P, 4], F32)
        v_bias = sb("v_bias", [P, D], F32)
        turn_ps, ln_ps = ps("turn_ps", [P, KC, TB]), ps("ln_ps", [P, 2, TB])
        qk_ps, v_ps = ps("qk_ps", [P, 2, TB]), ps("v_ps", [P, 2, TB])
        passed = sem("passed")
        x_loaded, bias_loaded, turned, xT_ready = sem("x_loaded"), sem("bias_loaded"), sem("turned0"), sem("xT_ready")
        xT_stored, qk_done, full_ready, high_ready = sem("xT_stored"), sem("qk_done"), sem("full_ready"), sem("high_ready")
        rest_ready, mid_ready, low_ready, qk_stored = sem("rest_ready"), sem("mid_ready"), sem("low_ready"), sem("qk_stored")
        v_done, v_ready = sem("v_done"), sem("v_ready")
        ln = LayerNorm("ln0", nc, sb, sem, K["ones"], [xT], xT_ready, ln_ps[:, 0, :], ln_ps[:, 1, :])
        WQK = [(K["wt_hi"], K["wt_lo"])]
        wq0 = chunk_of("L0_attn_Wq")
        wv0 = chunk_of("L0_attn_Wv")
        x_dram = d["L0_attn_x"].rearrange("a (t p) n -> p (a t) n", p=P)

        sem.start()
        with nc.Block() as block:
            @block.sync
            def _(sp):
                sp.dma_start(qk_bias[:, 0:2], column(d["L0_attn_bq"]), allow_slow_non_contiguous=True).then_inc(bias_loaded, 16)
                sp.dma_start(qk_bias[:, 2:4], column(d["L0_attn_bk"]), allow_slow_non_contiguous=True).then_inc(bias_loaded, 16)
                sp.dma_start(v_bias[:, :], d["L0_attn_bv"].partition_broadcast(P)).then_inc(bias_loaded, 16)
                with sp.Fori(0, NB) as i:
                    sp.wait_ge(turned, count(i))
                    sp.dma_start(x_tok[:, :, :], x_dram[:, ds(i, TT), :]).then_inc(x_loaded, 16)
                    sp.wait_ge(xT_ready, count(i + 1))
                    sp.dma_start(feature_major(d["X0T"])[:, :, ds(i, TB)], xT[:, :, :]).then_inc(xT_stored, 16)
                    for c in range(4):
                        sp.wait_ge(low_ready, count(i * 4 + c + 1))
                        alone(sp, passed)
                        dst = d["QS"] if c < 2 else d["KS"]
                        sp.dma_start(
                            dst.rearrange("j (k p) n -> p k j n", p=P)[:, c % 2, :, ds(i, TB)],
                            parts[:, c, :, :]).then_inc(qk_stored, 16)
                sp.wait_ge(xT_stored, count(16 * NB))
                sp.wait_ge(qk_stored, count(16 * 4 * NB))

            @block.tensor
            def _(pe):
                with pe.Fori(0, NB) as i:
                    pe.wait_ge(x_loaded, count(16 * (i + 1)))
                    pe.wait_ge(xT_ready, count(i))
                    for k in range(KC):
                        for t in range(TT):
                            mm = nc.tensor.transpose(turn_ps[:, k, t * P:(t + 1) * P],
                                                     x_tok[:, t, k * P:(k + 1) * P], K["ident"][:, :])
                    mm.then_inc(turned, 1)
                    ln.tensor_mean(pe, i)
                    ln.tensor_var(pe, i)
                    pe.wait_ge(ln.lo_ready, count(i + 1))
                    for c in range(4):
                        if c < 2:
                            pe.wait_ge(rest_ready, count(4 * i + c))
                        else:
                            pe.wait_ge(rest_ready, count(4 * i + c - 1))
                        if c == 0:
                            pass
                        project3(nc, qk_ps[:, c % 2, :], WQK[0], ln.cut[0],
                                 slice(wq0 + c * P, wq0 + (c + 1) * P)).then_inc(qk_done, 1)
                    for t in range(TT):
                        if t % 2 == 0:
                            pe.wait_ge(v_ready, count(2 * i + (t // 2)))
                        for k in range(KC):
                            x = [v[:, k, t * P:(t + 1) * P] for v in ln.cut[0]]
                            w = [v[:, k, wv0:wv0 + D] for v in (K["wt_hi"], K["wt_lo"])]
                            mm = product3(nc, v_ps[:, t // 2, t % 2 * D:(t % 2 + 1) * D], x, w,
                                          k == 0, k == KC - 1)
                        if t % 2 == 1:
                            mm.then_inc(v_done, 1)

            @block.scalar
            def _(act):
                act.wait_ge(bias_loaded, count(48))
                with act.Fori(0, NB) as i:
                    act.wait_ge(turned, count(i + 1))
                    act.wait_ge(ln.centred, count(i))
                    act.wait_ge(xT_stored, count(16 * i))
                    nc.scalar.copy(xT[:, :, :], turn_ps[:, :, :]).then_inc(xT_ready, 1)
                    ln.scalar_square(act, i)
                    ln.scalar_std(act, i, K["eps"])
                    ln.scalar_hi(act, i)
                    for c in range(4):
                        act.wait_ge(qk_done, count(4 * i + c + 1))
                        if c < 2:
                            act.wait_ge(rest_ready, count(4 * i))
                            act.wait_ge(qk_stored, count(64 * i))
                        else:
                            act.wait_ge(rest_ready, count(4 * i + c - 1))
                        bias = qk_bias[:, c:c + 1]
                        nc.scalar.activation(full[:, c % 2, :], qk_ps[:, c % 2, :], ACT.Identity,
                                             bias=bias).then_inc(full_ready, 1)
                        nc.scalar.activation(parts[:, c, 0, :], qk_ps[:, c % 2, :], ACT.Identity,
                                             bias=bias).then_inc(high_ready, 1)
                        act.wait_ge(rest_ready, count(4 * i + c + 1))
                        nc.scalar.copy(parts[:, c, 1, :], rest[:, c % 2, :]).then_inc(mid_ready, 1)

            @block.vector
            def _(dve):
                dve.wait_ge(bias_loaded, count(48))
                with dve.Fori(0, NB) as i:
                    ln.vector_centre(dve, i)
                    ln.vector_reciprocal(dve, i)
                    ln.vector_scale(dve, i)
                    ln.vector_lo(dve, i)
                    for c in range(4):
                        dve.wait_ge(high_ready, count(4 * i + c + 1))
                        nc.vector.tensor_tensor(rest[:, c % 2, :], full[:, c % 2, :], parts[:, c, 0, :],
                                                ALU.subtract).then_inc(rest_ready, 1)
                        dve.wait_ge(mid_ready, count(4 * i + c + 1))
                        nc.vector.tensor_tensor(parts[:, c, 2, :], rest[:, c % 2, :], parts[:, c, 1, :],
                                                ALU.subtract).then_inc(low_ready, 1)
                    for t in range(TT // 2):
                        dve.wait_ge(v_done, count(2 * i + t + 1))
                        nc.vector.tensor_tensor(
                            V_all[:, bass.ds(i * TT + 2 * t, 2), :],
                            v_ps[:, t, :].rearrange("p (a n) -> p a n", a=2),
                            v_bias[:, :].unsqueeze(1).to_broadcast([P, 2, D]), ALU.add).then_inc(v_ready, 1)



MC = T // P
QUADS = MC // 4
STACK = 6 * HD
ROWS = STACK + PARTS
K_PARTS = (0, 0, 0, 1, 1, 2)
Q_PARTS = (0, 1, 2, 0, 1, 0)
SCALE = 1.0 / D ** 0.5
A_BANKS = 3
TURN_SLOT = 24


def a_slot(u):
    return u - 12 if u >= 12 else u + TURN_SLOT - 4 + (u >= 4)


def attention_phase(nc, d, K, V_all):
    with ExitStack() as ctx:
        sb = lambda n, s, t: ctx.enter_context(nc.sbuf_tensor(n, s, t))
        sem = ctx.enter_context(PhaseSemaphores(nc, "att"))
        ps = lambda n, s: ctx.enter_context(nc.psum_tensor(n, s, F32))
        QST = sb("QST", [P, 2, T], BF16)
        KA = sb("KA", [P, 2, TB], BF16)
        KB = sb("KB", [P, 2, TB], BF16)
        VH = sb("VH", [P, 2, MC, 2 * HD], F32)
        PR = sb("PR", [P, 4, 2, TB], F32)
        PM = sb("PM", [P, 2, TT, NB], F32)
        neg = sb("neg", [P, 2, TT], F32)
        neg_rest = sb("neg_rest", [P, TT], F32)
        NM = sb("NM", [P, TT, 4], BF16)
        OS = sb("OS", [P, 2, TB], F32)
        OG = sb("OG", [2 * HD, 3, TB], F32)
        O2 = sb("O2", [2 * HD, 3, TB], F32)
        SB = ps("SB", [P, 2, 2, TB])
        A = ps("A", [P, A_BANKS, TB])
        PV = ps("PV", [P, TB])
        TN = A[:, TURN_SLOT % A_BANKS, :]

        q_loaded = [sem(f"q_loaded{i}") for i in range(2)]
        ka_loaded = [sem(f"ka_loaded{i}") for i in range(2)]
        kb_loaded = [sem(f"kb_loaded{i}") for i in range(2)]
        passed = sem("passed")
        rows_set, ones_set, vh_ready = sem("rows_set"), sem("ones_set"), sem("vh_ready")
        b_done = sem("b_done")
        a_done = sem("a_done")
        b_free = sem("b_free")
        a_free = sem("a_free")
        p_free = sem("p_free")
        os_free = sem("os_free")
        AHEAD = 2
        neg_ready, neg_high, neg_left, neg_parts = (
            sem("neg_ready"), sem("neg_high"), sem("neg_left"), sem("neg_parts"))
        shift_turned, shift_ready = sem("shift_turned"), sem("shift_ready")
        pv_read, groups_moved, half_sums, o_stored = (
            sem("pv_read"), sem("groups_moved", from_zero=True), sem("half_sums"),
            sem("o_stored", from_zero=True))
        STEPS = HEADS * NB
        UNITS = TT * NB
        LOAD = 16 * len(K_PARTS)

        def in_steps(eng, body):
            with eng.Fori(0, HEADS // 2) as pair:
                for hp in range(2):
                    with eng.Fori(0, NB // 2 - 1) as two:
                        for par in range(2):
                            body(pair * NB + two + hp * (NB // 2), pair, hp, None, par)
                    for nb in (NB - 2, NB - 1):
                        body(pair * NB + (hp * NB + nb) // 2, pair, hp, nb, nb % 2)

        sem.start()
        with nc.Block() as block:
            @block.sync
            def _(sp):
                def load_stack(dst, name, parts, head, cols, signal):
                    for r, j in enumerate(parts):
                        sp.dma_start(dst[r * HD:(r + 1) * HD, :],
                                     d[name][j, bass.ds(head * HD, HD), cols]).then_inc(signal, 16)

                def load_k(dst, par, head, nb, signal):
                    load_stack(dst[:, par, :], "KS", K_PARTS, head, slice(nb * TB, (nb + 1) * TB),
                               signal[par])

                def head_loads(h, hp, following):
                    for nb in range(NB):
                        t = h * NB + nb
                        sp.wait_ge(b_done, count(t * (2 * QUADS)))
                        load_k(KB, (nb + 1) % 2, h if nb + 1 < NB else following, (nb + 1) % NB, kb_loaded)
                        sp.wait_ge(a_done, count((t + 1) * UNITS))
                        load_k(KA, nb % 2, h if nb + 2 < NB else following, (nb + 2) % NB, ka_loaded)
                        if nb == 0:
                            load_stack(QST[:, 1 - hp, :], "QS", Q_PARTS, following, slice(0, T),
                                       q_loaded[1 - hp])

                load_k(KA, 0, 0, 0, ka_loaded)
                load_stack(QST[:, 0, :], "QS", Q_PARTS, 0, slice(0, T), q_loaded[0])
                load_k(KA, 1, 0, 1, ka_loaded)
                load_k(KB, 0, 0, 0, kb_loaded)
                with sp.Fori(0, HEADS // 2 - 1) as pair:
                    for hp in range(2):
                        head_loads(pair * 2 + hp, hp, pair * 2 + (hp + 1))
                head_loads(HEADS - 2, 0, HEADS - 1)
                head_loads(HEADS - 1, 1, 0)

            @block.tensor
            def _(pe):
                def unit_a(block, u, par, slot):
                    i, j = divmod(u, NB)
                    before = a_slot(u) - TURN_SLOT
                    if before == A_BANKS:
                        pe.wait_ge(shift_ready, count(block))
                    elif 0 < before < A_BANKS:
                        pe.wait_ge(a_free, count(block * UNITS + (u + 2)))
                    else:
                        pe.wait_ge(a_free, count(block * UNITS + (u + 1)))
                    nc.tensor.matmul(A[:, a_slot(u) % A_BANKS, :], KA[0:STACK, par, i * P:(i + 1) * P],
                                     QST[0:STACK, slot, j * TB:(j + 1) * TB],
                                     start=True, stop=True).then_inc(a_done, 1)

                def chunk_b(step, m, par, slot):
                    pair, e = divmod(m, 2)
                    if e == 0:
                        pe.wait_ge(b_free, count(step * (2 * QUADS) + (pair + 1)))
                    mm = nc.tensor.matmul(SB[:, pair % 2, e, :], QST[0:ROWS, slot, m * P:(m + 1) * P],
                                          KB[0:ROWS, par, :], start=True, stop=True)
                    if e == 1:
                        mm.then_inc(b_done, 1)

                def values(step, q, slot):
                    if q == 0:
                        pe.wait_ge(pv_read, count(step))
                    pe.wait_ge(b_free, count(step * (2 * QUADS) + (AHEAD + 2 * q + 2)))
                    for r in range(4):
                        m = 4 * q + r
                        mm = nc.tensor.matmul(PV[32 * r:32 * r + 32, :], VH[:, slot, m, :],
                                              PR[:, m // 2 % 4, r % 2, :],
                                              start=(q == 0), stop=(q == QUADS - 1))
                    mm.then_inc(p_free, 1)

                def turn_shift(block):
                    pe.wait_ge(neg_parts, count(block + 1))
                    pe.wait_ge(a_free, count((block + 1) * UNITS + (2 + A_BANKS)))
                    for i in range(TT):
                        mm = nc.tensor.matmul(TN[STACK:ROWS, i * P:(i + 1) * P], NM[:, i, 0:PARTS],
                                              K["ident_b"][:, :], start=True, stop=True)
                    mm.then_inc(shift_turned, 1)

                def step(half, pair, hp, nb, par):
                    t = half * 2 + par
                    for q in range(1, QUADS + 1):
                        a_block, a_par = (t + 1, 1 - par) if q < 6 else (t + 2, par)
                        a_next = nb == NB - 1 or (nb == NB - 2 and q >= 6)
                        a_slot = 1 - hp if a_next else hp
                        if q == 6:
                            pe.wait_ge(ka_loaded[par], count((half + 2) * LOAD))
                            if nb == NB - 2:
                                pe.wait_ge(q_loaded[1 - hp], count((pair + (hp + 1)) * LOAD))
                        b_next = q == QUADS
                        if b_next:
                            pe.wait_ge(kb_loaded[1 - par], count((half + (par + 1)) * LOAD))
                            pe.wait_ge(shift_ready, count(t + 2))
                        for r in range(4):
                            chunk_b(t + 1 if b_next else t, 4 * (q % QUADS) + r,
                                    1 - par if b_next else par, 1 - hp if b_next and nb == NB - 1 else hp)
                            unit_a(a_block, 4 * ((q + 2) % QUADS) + r, a_par, a_slot)
                        if q == 1:
                            pe.wait_ge(vh_ready, count(pair * 2 + (hp + 1)))
                        if q == 6:
                            turn_shift(t + 1)
                        values(t, q - 1, hp)

                pe.wait_ge(rows_set, count(1))
                pe.wait_ge(q_loaded[0], count(LOAD))
                pe.wait_ge(ka_loaded[0], count(LOAD))
                for u in range(UNITS):
                    unit_a(0, u, 0, 0)
                pe.wait_ge(ka_loaded[1], count(LOAD))
                for u in range(4):
                    unit_a(1, u, 1, 0)
                turn_shift(0)
                for u in range(4, 8):
                    unit_a(1, u, 1, 0)
                pe.wait_ge(kb_loaded[0], count(LOAD))
                pe.wait_ge(shift_ready, count(1))
                for r in range(4):
                    chunk_b(0, r, 0, 0)
                    unit_a(1, 8 + r, 1, 0)
                in_steps(pe, step)

            @block.scalar
            def _(act):
                def exp_pair(step, pair):
                    if pair % 2 == 0:
                        act.wait_ge(p_free, count(step * QUADS + (pair // 2 + 1)))
                    act.wait_ge(b_done, count(step * (2 * QUADS) + (pair + 1)))
                    nc.scalar.activation(PR[:, pair % 4, :, :], SB[:, pair % 2, :, :], ACT.Exp,
                                         scale=SCALE).then_inc(b_free, 1)

                def place_shift(block, par):
                    act.wait_ge(shift_turned, count(block + 1))
                    nc.scalar.copy(KB[STACK:ROWS, par, :], TN[STACK:ROWS, :]).then_inc(shift_ready, 1)

                def step(half, pair, hp, nb, par):
                    t = half * 2 + par
                    for q in range(1, QUADS):
                        if q == QUADS - 1:
                            place_shift(t + 1, 1 - par)
                        exp_pair(t, 2 * q)
                        exp_pair(t, 2 * q + 1)
                    exp_pair(t + 1, 0)
                    exp_pair(t + 1, 1)
                    act.wait_ge(p_free, count((t + 1) * QUADS + AHEAD))
                    act.wait_ge(os_free, count(t + 1))
                    nc.scalar.copy(OS[:, par, :], PV[:, :]).then_inc(pv_read, 1)

                act.sem_inc(b_free, AHEAD)
                place_shift(0, 0)
                exp_pair(0, 0)
                exp_pair(0, 1)
                in_steps(act, step)

            @block.vector
            def _(dve):
                def unit_max(block, u, par):
                    dve.wait_ge(a_done, count(block * UNITS + (u + 1)))
                    i, j = divmod(u, NB)
                    nc.vector.tensor_reduce(PM[:, par, i, j:j + 1], A[:, a_slot(u) % A_BANKS, :], AX.X,
                                            ALU.max).then_inc(a_free, 1)

                def block_max(block, par):
                    for u in range(UNITS):
                        unit_max(block, u, par)
                    dve.wait_ge(a_free, count((block + 1) * UNITS + A_BANKS))
                    nc.vector.tensor_reduce(neg[:, par, :], PM[:, par, :, :], AX.X, ALU.max,
                                            negate=True).then_inc(neg_ready, 1)

                nc.vector.memset(QST[STACK:ROWS, :, :], 1.0).then_inc(rows_set, 1)
                dve.sem_inc(a_free, A_BANKS)
                with dve.Fori(0, STEPS // 2) as two:
                    for par in range(2):
                        block_max(two * 2 + par, par)
                block_max(STEPS, 0)
                for u in range(12):
                    unit_max(STEPS + 1, u, 1)

            @block.gpsimd
            def _(pool):
                def values_of(head, slot):
                    nc.gpsimd.tensor_copy(VH[:, slot, :, 0:HD],
                                          V_all[:, :, bass.ds(head * HD, HD)]).then_inc(vh_ready, 1)

                def shift_parts(block, par):
                    pool.wait_ge(neg_ready, count(block + 1))
                    pool.wait_ge(shift_turned, count(block))
                    alone(pool, passed)
                    nc.gpsimd.tensor_copy(NM[:, :, 0], neg[:, par, :]).then_inc(neg_high, 1)
                    pool.wait_ge(neg_high, count(block * 2 + 1))
                    nc.gpsimd.tensor_tensor(neg_rest[:, :], neg[:, par, :], NM[:, :, 0],
                                            ALU.subtract).then_inc(neg_left, 1)
                    pool.wait_ge(neg_left, count(block + 1))
                    alone(pool, passed)
                    nc.gpsimd.tensor_copy(NM[:, :, 1], neg_rest[:, :]).then_inc(neg_high, 1)
                    pool.wait_ge(neg_high, count(block * 2 + 2))
                    nc.gpsimd.tensor_tensor(NM[:, :, 2], neg_rest[:, :], NM[:, :, 1],
                                            ALU.subtract).then_inc(neg_parts, 1)

                def step(t, h, hp, nb, par, block_of_head, next_head):
                    shift_parts(t + 1, 1 - par)
                    if next_head is not None:
                        pool.wait_ge(p_free, count(h * (NB * QUADS) + AHEAD))
                        alone(pool, passed)
                        values_of(next_head, 1 - hp)
                    pool.wait_ge(pv_read, count(t + 1))
                    pool.wait_ge(os_free, count(t + AHEAD))
                    alone(pool, passed)
                    for g in range(3):
                        pool.dma_start(OG[:, g, :], OS[32 * (g + 1):32 * (g + 2), par, :]
                                       ).then_inc(groups_moved, 16)
                    pool.wait_ge(groups_moved, (t + 1) * 48)
                    nc.gpsimd.tensor_tensor(O2[:, 0, :], OS[0:2 * HD, par, :], OG[:, 0, :],
                                            ALU.add).then_inc(half_sums, 1)
                    nc.gpsimd.tensor_tensor(O2[:, 1, :], OG[:, 1, :], OG[:, 2, :],
                                            ALU.add).then_inc(half_sums, 1)
                    pool.wait_ge(half_sums, count((t + 1) * 2))
                    nc.gpsimd.tensor_tensor(O2[:, 2, :], O2[:, 0, :], O2[:, 1, :],
                                            ALU.add).then_inc(os_free, 1)
                    pool.wait_ge(os_free, count(t + 1 + AHEAD))
                    alone(pool, passed)
                    cols = bass.ds(block_of_head * TB, TB)
                    for j, name in enumerate(("NUM", "DEN")):
                        pool.dma_start(d[name][bass.ds(h * HD, HD), cols],
                                       O2[j * HD:(j + 1) * HD, 2, :]).then_inc(o_stored, 16)
                    pool.wait_ge(o_stored, (t + 1) * 32)

                pool.sem_inc(p_free, AHEAD)
                pool.sem_inc(os_free, AHEAD)
                nc.gpsimd.memset(VH[:, :, :, HD:2 * HD], 1.0).then_inc(ones_set, 1)
                pool.wait_ge(ones_set, count(1))
                values_of(0, 0)
                shift_parts(0, 0)
                with pool.Fori(0, HEADS // 2 - 1) as pair:
                    for hp in range(2):
                        for nb in range(NB):
                            step(pair * (2 * NB) + (hp * NB + nb), pair * 2 + hp, hp, None, nb % 2, nb,
                                 pair * 2 + (hp + 1) if nb == 0 else None)
                for hp in range(2):
                    h = HEADS - 2 + hp
                    for nb in range(NB):
                        step(h * NB + nb, h, hp, None, nb % 2, nb, h + 1 if nb == 0 and hp == 0 else None)



def cut_weights(nc, name, items, width):
    with ExitStack() as ctx:
        raw = ctx.enter_context(nc.sbuf_tensor(f"{name}_raw", [P, 2, width], F32))
        sem = ctx.enter_context(PhaseSemaphores(nc, name))
        loaded = [sem(f"loaded{i}") for i in range(2)]
        hi_done, lo_done = (sem(f"{n}_done") for n in ("hi", "lo"))

        def staged(n, like):
            a, b = like.shape[1], like.shape[2]
            return raw[0:like.shape[0], n % 2, 0:a * b].rearrange("p (a b) -> p a b", a=a)

        with nc.Block() as block:
            @block.sync
            def _(sp):
                for n, (src, hi, lo) in enumerate(items):
                    if n >= 2:
                        sp.wait_ge(lo_done, n - 1)
                    sp.dma_start(staged(n, hi), src).then_inc(loaded[n % 2], 16)

            @block.scalar
            def _(act):
                for n, (src, hi, lo) in enumerate(items):
                    act.wait_ge(loaded[n % 2], 16 * (n // 2 + 1))
                    nc.scalar.copy(hi, staged(n, hi)).then_inc(hi_done, 1)

            @block.vector
            def _(dve):
                for n, (src, hi, lo) in enumerate(items):
                    dve.wait_ge(hi_done, n + 1)
                    nc.vector.tensor_tensor(lo, staged(n, hi), hi.bitcast(F32),
                                            ALU.subtract).then_inc(lo_done, 1)



HID = 1024
HC = HID // P
EXPERTS0 = 3
RING = 3
LAG = 2


def ffn0_phase(nc, d, K):
    with ExitStack() as wctx:
        wsb = lambda n, s, t: wctx.enter_context(nc.sbuf_tensor(n, s, t))
        w1 = [wsb(f"f0_w1_{p}", [P, EXPERTS0, KC, HID], F32R) for p in ("hi", "lo")]
        w2 = [wsb(f"f0_w2_{p}", [P, EXPERTS0, HC, D], F32R) for p in ("hi", "lo")]
        sources = [(d["L0_ffn_sw1"], d["L0_ffn_sw2"])] + [(d["L0_ffn_w1"][e], d["L0_ffn_w2"][e]) for e in range(2)]
        items = []
        for e, (a, b) in enumerate(sources):
            items.append((a.rearrange("(k p) h -> p k h", p=P), w1[0][:, e, :, :], w1[1][:, e, :, :]))
            items.append((b.rearrange("(c p) n -> p c n", p=P), w2[0][:, e, :, :], w2[1][:, e, :, :]))
        cut_weights(nc, "f0", items, KC * HID)
        ffn0_blocks(nc, d, K, w1, w2)


def ffn0_blocks(nc, d, K, w1, w2):
    with ExitStack() as ctx:
        sb = lambda n, s, t: ctx.enter_context(nc.sbuf_tensor(n, s, t))
        sem = ctx.enter_context(PhaseSemaphores(nc, "ffn0"))
        ps = lambda n, s: ctx.enter_context(nc.psum_tensor(n, s, F32))
        num, den = sb("num", [P, KC, TB], F32), sb("den", [P, KC, TB], F32)
        x = [sb(f"f0_x{s}", [P, KC, TB], F32) for s in range(2)]
        gate_out = [sb(f"gate_out{s}", [P, TB], F32) for s in range(2)]
        chosen = sb("chosen", [P, 2, TB], F32)
        h_full = sb("h_full", [P, RING, TB], F32)
        h = [sb(f"h_{p}", [P, RING, TB], F32R) for p in ("hi", "lo")]
        bo, b1, b2 = sb("bo", [P, KC], F32), sb("b1", [P, EXPERTS0 * HC], F32), sb("b2", [P, EXPERTS0, KC], F32)
        b2_sum = sb("b2_sum", [P, KC], F32)
        gate_cols = sb("gate_cols", [P, 2, KC], F32)
        gate_diff = sb("gate_diff", [P, KC, 2], F32)
        gate = [sb(f"gate_{p}", [P, KC, P], F32R) for p in ("hi", "lo")]
        front_ps, h_ps, y_ps = ps("front_ps", [P, KC, TB]), ps("h_ps", [P, RING, TB]), ps("y_ps", [P, KC, TB])
        (consts, diffed, num_loaded, rden, o_full, o_hi, o_lo, proj_done, x1_ready, gate_done,
         gate_ready, h_done, chosen_ready, full_ready, hi_ready, lo_ready, h_free, summed, x2_ready, x2_stored) = (
            sem(n) for n in ("consts", "diffed", "num_loaded", "rden", "o_full", "o_hi", "o_lo",
                             "proj_done", "x1_ready", "gate_done", "gate_ready", "h_done", "chosen",
                             "full_ready", "hi_ready", "lo_ready", "h_free", "summed", "x2_ready", "x2_stored"))
        x_loaded = [sem(f"x_loaded{s}") for s in range(2)]
        passed = sem("passed")
        ln = LayerNorm("ln1", nc, sb, sem, K["ones"], x, x1_ready, front_ps[:, 0, :], front_ps[:, 1, :], 2)
        wo = chunk_of("L0_attn_Wo")
        C = EXPERTS0 * HC
        ROUTED = C - HC
        CONST_LOADS = 16 * 9

        sem.start()
        with nc.Block() as block:
            @block.sync
            def _(sp):
                def col(dst, src):
                    sp.dma_start(dst, column(src), allow_slow_non_contiguous=True).then_inc(consts, 16)

                def load_sums(j):
                    sp.dma_start(num[:, :, :], feature_major(d["NUM"])[:, :, ds(j, TB)]).then_inc(num_loaded, 16)
                    sp.dma_start(den[:, :, :], feature_major(d["DEN"])[:, :, ds(j, TB)]).then_inc(num_loaded, 16)

                def load_x(j, slot):
                    sp.dma_start(x[slot][:, :, :], feature_major(d["X0T"])[:, :, ds(j, TB)]
                                 ).then_inc(x_loaded[slot], 16)

                def blocks(half, i, slot, following):
                    if following:
                        sp.wait_ge(x2_stored, count(i * 16))
                        alone(sp, passed)
                        load_x(i + 1, 1 - slot)
                    if following == 2:
                        sp.wait_ge(o_lo, count(i + 2))
                        load_sums(i + 2)
                    sp.wait_ge(x2_ready, count(i + 1))
                    sp.dma_start(feature_major(d["X2T"])[:, :, ds(i, TB)], x[slot][:, :, :]).then_inc(x2_stored, 16)

                load_sums(0)
                load_x(0, 0)
                col(bo[:, :], d["L0_attn_bo"])
                col(b1[:, 0:HC], d["L0_ffn_sb1"])
                col(b2[:, 0, :], d["L0_ffn_sb2"])
                for e in range(2):
                    col(b1[:, (e + 1) * HC:(e + 2) * HC], d["L0_ffn_b1"][e])
                    col(b2[:, e + 1, :], d["L0_ffn_b2"][e])
                    col(gate_cols[:, e, :], d["L0_ffn_gate_w"][e])
                sp.wait_ge(o_lo, count(1))
                load_sums(1)
                overlapped(sp, blocks)
                sp.wait_ge(x2_stored, count(16 * NB))

            @block.tensor
            def _(pe):
                def front(j, slot, part):
                    if part == "projection":
                        pe.wait_ge(gate_ready, count(j))
                        pe.wait_ge(o_lo, count(j + 1))
                        for n in range(KC):
                            mm = project3(nc, front_ps[:, n, :], (K["wt_hi"], K["wt_lo"]), ln.cut[slot],
                                          slice(wo + n * P, wo + (n + 1) * P))
                        mm.then_inc(proj_done, 1)
                    elif part == "mean":
                        ln.tensor_mean(pe, j, slot)
                    elif part == "variance":
                        ln.tensor_var(pe, j)
                    elif part == "gate":
                        pe.wait_ge(ln.lo_ready, count(j + 1))
                        project3(nc, front_ps[:, 0, :], gate, ln.cut[slot], slice(0, P)).then_inc(gate_done, 1)

                def hidden(i, slot, c):
                    if c < RING:
                        pe.wait_ge(chosen_ready, count(i * ROUTED))
                    elif c - RING < HC:
                        pe.wait_ge(hi_ready, count(i * C + (c - RING + 1)))
                    else:
                        pe.wait_ge(chosen_ready, count(i * ROUTED + (c - RING - HC + 1)))
                    project3(nc, h_ps[:, c % RING, :], [w[:, c // HC, :, :] for w in w1], ln.cut[slot],
                             slice(c % HC * P, (c % HC + 1) * P)).then_inc(h_done, 1)

                def output(i, c):
                    e, k = divmod(c, HC)
                    pe.wait_ge(lo_ready, count(i * C + (c + 1)))
                    if c == 0:
                        pe.wait_ge(x2_ready, count(i))
                    for n in range(KC):
                        mm = product3(nc, y_ps[:, n, :], [w[:, e, k, n * P:(n + 1) * P] for w in w2],
                                      [v[:, c % RING, :] for v in h], c == 0, c == C - 1)
                    mm.then_inc(h_free, 1)

                def blocks(half, i, slot, following):
                    for c in range(C + LAG):
                        if c < C:
                            hidden(i, slot, c)
                        if c >= LAG:
                            output(i, c - LAG)
                        if following:
                            front(i + 1, 1 - slot, {6: "projection", 9: "mean", 13: "variance", 20: "gate"}.get(c))

                pe.wait_ge(diffed, count(4))
                for part in ("projection", "mean", "variance", "gate"):
                    front(0, 0, part)
                overlapped(pe, blocks)

            @block.scalar
            def _(act):
                def front(j, slot, part):
                    if part == "o_hi":
                        act.wait_ge(o_full, count(j + 1))
                        nc.scalar.copy(ln.cut[slot][0][:, :, :], num[:, :, :]).then_inc(o_hi, 1)
                    elif part == "square":
                        ln.scalar_square(act, j)
                    elif part == "std":
                        ln.scalar_std(act, j, K["eps"])
                    elif part == "hi":
                        ln.scalar_hi(act, j, slot)

                def blocks(half, i, slot, following):
                    for c in range(C):
                        if following:
                            front(i + 1, 1 - slot, {3: "o_hi", 11: "square", 14: "std", 17: "hi"}.get(c))
                        act.wait_ge(h_free, count(i * C + (c + 1)))
                        if c < HC:
                            act.wait_ge(h_done, count(i * C + (c + 1)))
                            src = h_ps[:, c % RING, :]
                        else:
                            act.wait_ge(chosen_ready, count(i * ROUTED + (c - HC + 1)))
                            src = chosen[:, c % 2, :]
                        nc.scalar.activation(h_full[:, c % RING, :], src, ACT.Relu,
                                             bias=b1[:, c:c + 1]).then_inc(full_ready, 1)
                        nc.scalar.activation(h[0][:, c % RING, :], src, ACT.Relu,
                                             bias=b1[:, c:c + 1]).then_inc(hi_ready, 1)

                act.sem_inc(h_free, RING)
                act.wait_ge(consts, count(CONST_LOADS))
                act.wait_ge(diffed, count(2))
                nc.scalar.copy(gate[0][:, :, :], gate_diff[:, :, 0:1].to_broadcast([P, KC, P])
                               ).then_inc(diffed, 1)
                for part in ("o_hi", "square", "std", "hi"):
                    front(0, 0, part)
                overlapped(act, blocks)

            @block.vector
            def _(dve):
                def front(j, half, slot, part):
                    if part == "den0":
                        dve.wait_ge(num_loaded, count((j + 1) * 32))
                        nc.vector.reciprocal(den[:, 0, :], den[:, 0, :]).then_inc(rden, 1)
                    elif part == "den1":
                        nc.vector.reciprocal(den[:, 1, :], den[:, 1, :]).then_inc(rden, 1)
                    elif part == "quotient":
                        dve.wait_ge(rden, count((j + 1) * KC))
                        nc.vector.tensor_tensor(num[:, :, :], num[:, :, :], den[:, :, :],
                                                ALU.mult).then_inc(o_full, 1)
                    elif part == "o_lo":
                        dve.wait_ge(o_hi, count(j + 1))
                        o = ln.cut[slot]
                        nc.vector.tensor_tensor(o[1][:, :, :], num[:, :, :], o[0][:, :, :].bitcast(F32),
                                                ALU.subtract).then_inc(o_lo, 1)
                    elif part == "x1":
                        dve.wait_ge(proj_done, count(j + 1))
                        dve.wait_ge(x_loaded[slot], count((half + 1) * 16))
                        for n in range(KC):
                            ins = nc.vector.scalar_tensor_tensor(
                                out=x[slot][:, n, :], in0=front_ps[:, n, :], scalar=bo[:, n:n + 1],
                                in1=x[slot][:, n, :], op0=ALU.add, op1=ALU.add)
                        ins.then_inc(x1_ready, 1)
                    elif part == "centre":
                        ln.vector_centre(dve, j, slot)
                    elif part == "reciprocal":
                        ln.vector_reciprocal(dve, j)
                    elif part == "scale":
                        ln.vector_scale(dve, j)
                    elif part == "lo":
                        ln.vector_lo(dve, j, slot)
                    elif part == "gate":
                        dve.wait_ge(gate_done, count(j + 1))
                        nc.vector.tensor_copy(gate_out[slot][:, :], front_ps[:, 0, :]).then_inc(gate_ready, 1)

                def choose(i, slot, c):
                    if c == HC:
                        dve.wait_ge(gate_ready, count(i + 1))
                    dve.wait_ge(h_done, count(i * C + (c + 1)))
                    if c < HC + 2:
                        dve.wait_ge(hi_ready, count(i * C))
                    else:
                        dve.wait_ge(hi_ready, count(i * C + (c - 1)))
                    nc.vector.scalar_tensor_tensor(
                        out=chosen[:, c % 2, :], in0=gate_out[slot][:, :], scalar=0.0, in1=h_ps[:, c % RING, :],
                        op0=(ALU.is_le, ALU.is_gt)[c // HC - 1], op1=ALU.mult).then_inc(chosen_ready, 1)

                def blocks(half, i, slot, following):
                    for c in range(C):
                        if c + 1 == HC:
                            choose(i, slot, c + 1)
                        elif HC <= c < C - 1:
                            choose(i, slot, c + 1)
                        dve.wait_ge(hi_ready, count(i * C + (c + 1)))
                        nc.vector.tensor_tensor(h[1][:, c % RING, :], h_full[:, c % RING, :],
                                                h[0][:, c % RING, :].bitcast(F32),
                                                ALU.subtract).then_inc(lo_ready, 1)
                        if following:
                            front(i + 1, half + slot, 1 - slot, {
                                0: "den0", 1: "den1", 2: "quotient", 4: "o_lo", 7: "x1", 10: "centre",
                                15: "reciprocal", 16: "scale", 18: "lo", 21: "gate"}.get(c))
                    dve.wait_ge(h_free, count((i + 1) * C + RING))
                    for n in range(KC):
                        ins = nc.vector.scalar_tensor_tensor(
                            out=x[slot][:, n, :], in0=y_ps[:, n, :], scalar=b2_sum[:, n:n + 1],
                            in1=x[slot][:, n, :], op0=ALU.add, op1=ALU.add)
                    ins.then_inc(x2_ready, 1)

                dve.wait_ge(consts, count(CONST_LOADS))
                for k in range(KC):
                    nc.vector.tensor_tensor(gate_diff[:, k, 0:1], gate_cols[:, 1, k:k + 1],
                                            gate_cols[:, 0, k:k + 1], ALU.subtract).then_inc(diffed, 1)
                nc.vector.tensor_tensor(b2_sum[:, :], b2[:, 0, :], b2[:, 1, :], ALU.add).then_inc(summed, 1)
                dve.wait_ge(summed, count(1))
                nc.vector.tensor_tensor(b2_sum[:, :], b2_sum[:, :], b2[:, 2, :], ALU.add)
                dve.wait_ge(diffed, count(3))
                nc.vector.tensor_tensor(gate[1][:, :, :], gate_diff[:, :, 0:1].to_broadcast([P, KC, P]),
                                        gate[0][:, :, :].bitcast(F32), ALU.subtract).then_inc(diffed, 1)
                for part in ("den0", "den1", "quotient", "o_lo", "x1", "centre", "reciprocal", "scale",
                             "lo", "gate"):
                    front(0, 0, 0, part)
                overlapped(dve, blocks)



def qkv1_phase(nc, d, K, R):
    with ExitStack() as ctx:
        sb = lambda n, s, t: ctx.enter_context(nc.sbuf_tensor(n, s, t))
        sem = ctx.enter_context(PhaseSemaphores(nc, "qkv1"))
        ps = lambda n, s: ctx.enter_context(nc.psum_tensor(n, s, F32))
        x2 = sb("x2_in", [P, KC, TB], F32)
        gh_full = sb("gh_full", [HD, TB], F32)
        gh = [sb(f"gh_{p}", [HD, TB], F32R) for p in ("hi", "lo")]
        qk_bias, g1_bias, g2_bias = sb("p1_qk_bias", [P, 4], F32), sb("g1_bias", [HD, 1], F32), sb("g2_bias", [P, KC], F32)
        v_bias = sb("p1_v_bias", [P, D], F32)
        ln_ps, qk_ps, v_ps, g_ps = (ps(n, [P, 2, TB]) for n in ("p1_ln_ps", "p1_qk_ps", "p1_v_ps", "p1_g_ps"))
        (consts, x_loaded, qk_done, qk_ready, gh_done, gh_full_ready, gh_hi_ready, gh_lo_ready, g_done,
         g_ready, v_done, v_ready) = (sem(n) for n in (
             "consts", "x_loaded", "qk_done", "qk_ready", "gh_done", "gh_full_ready", "gh_hi_ready",
             "gh_lo_ready", "g_done", "g_ready", "v_done", "v_ready"))
        x_ready = sem("x_ready")
        ln = LayerNorm("ln2", nc, sb, sem, K["ones"], [x2], x_ready, ln_ps[:, 0, :], ln_ps[:, 1, :])
        w0 = chunk_of("L1_attn_w_qkv")

        sem.start()
        with nc.Block() as block:
            @block.sync
            def _(sp):
                def col(dst, src):
                    sp.dma_start(dst, src, allow_slow_non_contiguous=True).then_inc(consts, 16)
                col(qk_bias[:, :], column(d["L1_attn_b_qkv"][0:2 * D]))
                col(g1_bias[:, :], d["L1_attn_b_g1"].rearrange("(p c) -> p c", c=1))
                col(g2_bias[:, :], column(d["L1_attn_b_g2"]))
                sp.dma_start(v_bias[:, :], d["L1_attn_b_qkv"][2 * D:3 * D].partition_broadcast(P)).then_inc(consts, 16)
                with sp.Fori(0, NB) as i:
                    sp.wait_ge(ln.centred, count(i))
                    sp.dma_start(x2[:, :, :], feature_major(d["X2T"])[:, :, ds(i, TB)]).then_inc(x_ready, 16)

            @block.tensor
            def _(pe):
                with pe.Fori(0, NB) as i:
                    pe.wait_ge(x_ready, count(16 * (i + 1)))
                    ln.tensor_mean_of_ready()
                    ln.tensor_var(pe, i)
                    pe.wait_ge(ln.lo_ready, count(i + 1))
                    pe.wait_ge(gh_lo_ready, count(i))
                    pe.wait_ge(g_ready, count(2 * i))
                    project3(nc, g_ps[0:HD, 0, :], (K["g1_hi"], K["g1_lo"]), ln.cut[0],
                             slice(0, HD)).then_inc(gh_done, 1)
                    for c in range(4):
                        pe.wait_ge(qk_ready, count(4 * i + max(c - 1, 0)))
                        project3(nc, qk_ps[:, c % 2, :], (K["wt_hi"], K["wt_lo"]), ln.cut[0],
                                 slice(w0 + c * P, w0 + (c + 1) * P)).then_inc(qk_done, 1)
                    pe.wait_ge(gh_lo_ready, count(i + 1))
                    for c in range(KC):
                        product3(nc, g_ps[:, c, :], [w[:, c * P:(c + 1) * P] for w in (K["g2_hi"], K["g2_lo"])],
                                 [v[:, :] for v in gh], True, True).then_inc(g_done, 1)
                    for t in range(TT):
                        if t % 2 == 0:
                            pe.wait_ge(v_ready, count(2 * i + t // 2))
                        for k in range(KC):
                            x = [v[:, k, t * P:(t + 1) * P] for v in ln.cut[0]]
                            w = [v[:, k, w0 + 2 * D:w0 + 3 * D] for v in (K["wt_hi"], K["wt_lo"])]
                            mm = product3(nc, v_ps[:, t // 2, t % 2 * D:(t % 2 + 1) * D], x, w,
                                          k == 0, k == KC - 1)
                        if t % 2 == 1:
                            mm.then_inc(v_done, 1)

            @block.scalar
            def _(act):
                act.wait_ge(consts, count(64))
                with act.Fori(0, NB) as i:
                    ln.scalar_square(act, i)
                    ln.scalar_std(act, i, K["eps"])
                    ln.scalar_hi(act, i)
                    act.wait_ge(gh_done, count(i + 1))
                    act.wait_ge(g_done, count(2 * i))
                    nc.scalar.activation(gh_full[:, :], g_ps[0:HD, 0, :], ACT.Identity,
                                         bias=g1_bias[:, 0:1]).then_inc(gh_full_ready, 1)
                    nc.scalar.activation(gh[0][:, :], g_ps[0:HD, 0, :], ACT.Identity,
                                         bias=g1_bias[:, 0:1]).then_inc(gh_hi_ready, 1)
                    for c in range(4):
                        act.wait_ge(qk_done, count(4 * i + c + 1))
                        dst = R["Q1"] if c < 2 else R["K1"]
                        nc.scalar.activation(dst[:, c % 2, ds(i, TB)], qk_ps[:, c % 2, :],
                                             ACT.Silu if c < 2 else ACT.Identity,
                                             bias=qk_bias[:, c:c + 1]).then_inc(qk_ready, 1)
                    for c in range(KC):
                        act.wait_ge(g_done, count(2 * i + c + 1))
                        nc.scalar.activation(R["G1"][:, c, ds(i, TB)], g_ps[:, c, :], ACT.Sigmoid,
                                             bias=g2_bias[:, c:c + 1]).then_inc(g_ready, 1)

            @block.vector
            def _(dve):
                dve.wait_ge(consts, count(64))
                with dve.Fori(0, NB) as i:
                    ln.vector_centre(dve, i)
                    ln.vector_reciprocal(dve, i)
                    ln.vector_scale(dve, i)
                    ln.vector_lo(dve, i)
                    dve.wait_ge(gh_hi_ready, count(i + 1))
                    nc.vector.tensor_tensor(gh[1][:, :], gh_full[:, :], gh[0][:, :].bitcast(F32),
                                            ALU.subtract).then_inc(gh_lo_ready, 1)
                    for t in range(TT // 2):
                        dve.wait_ge(v_done, count(2 * i + t + 1))
                        nc.vector.tensor_tensor(
                            R["V1"][:, bass.ds(i * TT + 2 * t, 2), :],
                            v_ps[:, t, :].rearrange("p (a n) -> p a n", a=2),
                            v_bias[:, :].unsqueeze(1).to_broadcast([P, 2, D]), ALU.add).then_inc(v_ready, 1)



def kv1_phase(nc, d, K, R):
    with ExitStack() as ctx:
        sb = lambda n, s, t: ctx.enter_context(nc.sbuf_tensor(n, s, t))
        sem = ctx.enter_context(PhaseSemaphores(nc, "kv1"))
        ps = lambda n, s: ctx.enter_context(nc.psum_tensor(n, s, F32))
        k_tok = sb("k_tok", [P, MC, D], F32)
        neg_max, total, r_total = (sb(n, [P, KC], F32) for n in ("k_neg_max", "k_total", "k_rtotal"))
        mask = sb("head_mask", [P, P], F32)
        kv_full = sb("kv_full", [P, KC, P], F32)
        turn_ps, kv_ps = ps("k_turn_ps", [P, 2, TB]), ps("kv_ps", [P, KC, TB])
        copied_even = sem("copied_even")
        mask_set, max_ready, exp_ready, turned, copied_odd, kv_done, r_ready, full_ready, hi_ready = (
            sem(n) for n in ("mask", "max", "exp", "turned", "copied_odd", "done", "r", "full", "hi"))
        PAIRS = MC // 2

        with nc.Block() as block:
            @block.gpsimd
            def _(pool):
                view = mask[:, :].rearrange("p (b j) -> p b j", j=HD)
                nc.gpsimd.memset(mask[:, :], 1.0).then_inc(mask_set, 1)
                pool.wait_ge(mask_set, 1)
                nc.gpsimd.affine_select(out=view, in_=view, compare_op=ALU.is_ge, fill=0.0, base=0,
                                        pattern=[[-HD, P // HD], [0, HD]],
                                        channel_multiplier=1).then_inc(mask_set, 1)
                pool.wait_ge(mask_set, 2)
                nc.gpsimd.affine_select(out=view, in_=view, compare_op=ALU.is_ge, fill=0.0, base=HD - 1,
                                        pattern=[[HD, P // HD], [0, HD]],
                                        channel_multiplier=-1).then_inc(mask_set, 1)

            @block.vector
            def _(dve):
                for k in range(KC):
                    nc.vector.tensor_reduce(neg_max[:, k:k + 1], R["K1"][:, k, :], AX.X, ALU.max,
                                            negate=True).then_inc(max_ready, 1)
                for m in range(1, PAIRS, 2):
                    dve.wait_ge(turned, m + 1)
                    nc.vector.tensor_copy(k_tok[:, 2 * m:2 * m + 2, :],
                                          turn_ps[:, 1, :].rearrange("p (a n) -> p a n", a=2)
                                          ).then_inc(copied_odd, 1)
                dve.wait_ge(exp_ready, KC)
                nc.vector.reciprocal(r_total[:, :], total[:, :]).then_inc(r_ready, 1)
                dve.wait_ge(r_ready, 1)
                dve.wait_ge(kv_done, 1)
                dve.wait_ge(mask_set, 3)
                for k in range(KC):
                    nc.vector.scalar_tensor_tensor(
                        out=kv_full[:, k, :], in0=kv_ps[:, k, 0:P], scalar=r_total[:, k:k + 1],
                        in1=mask[:, :], op0=ALU.mult, op1=ALU.mult).then_inc(full_ready, 1)
                dve.wait_ge(hi_ready, 1)
                nc.vector.tensor_tensor(R["kv"][1][:, :, :], kv_full[:, :, :], R["kv"][0][:, :, :].bitcast(F32),
                                        ALU.subtract)

            @block.scalar
            def _(act):
                for k in range(KC):
                    act.wait_ge(max_ready, k + 1)
                    nc.scalar.activation(R["K1"][:, k, :], R["K1"][:, k, :], ACT.Exp,
                                         bias=neg_max[:, k:k + 1],
                                         accum_out=total[:, k:k + 1]).then_inc(exp_ready, 1)
                for m in range(0, PAIRS, 2):
                    act.wait_ge(turned, m + 1)
                    nc.scalar.copy(k_tok[:, 2 * m:2 * m + 2, :],
                                   turn_ps[:, 0, :].rearrange("p (a n) -> p a n", a=2)
                                   ).then_inc(copied_even, 1)
                act.wait_ge(full_ready, KC)
                nc.scalar.copy(R["kv"][0][:, :, :], kv_full[:, :, :]).then_inc(hi_ready, 1)

            @block.tensor
            def _(pe):
                pe.wait_ge(exp_ready, KC)
                for m in range(PAIRS):
                    if m >= 2:
                        pe.wait_ge((copied_even, copied_odd)[m % 2], m // 2)
                    for a in range(2):
                        for k in range(KC):
                            tok = (2 * m + a) * P
                            mm = nc.tensor.transpose(turn_ps[:, m % 2, a * D + k * P:a * D + (k + 1) * P],
                                                     R["K1"][:, k, tok:tok + P], K["ident"][:, :])
                    mm.then_inc(turned, 1)
                for s in (copied_even, copied_odd):
                    pe.wait_ge(s, PAIRS // 2)
                for k in range(KC):
                    for t in range(MC):
                        mm = nc.tensor.matmul(kv_ps[:, k, 0:P], k_tok[:, t, k * P:(k + 1) * P],
                                              R["V1"][:, t, k * P:(k + 1) * P],
                                              start=(t == 0), stop=(t == MC - 1))
                mm.then_inc(kv_done, 1)



def out1_phase(nc, d, K, R):
    with ExitStack() as ctx:
        sb = lambda n, s, t: ctx.enter_context(nc.sbuf_tensor(n, s, t))
        sem = ctx.enter_context(PhaseSemaphores(nc, "out1"))
        ps = lambda n, s: ctx.enter_context(nc.psum_tensor(n, s, F32))
        q = [sb(f"q1_{p}", [P, KC, TB], F32R) for p in ("hi", "lo")]
        o = sb("o1", [P, KC, TB], F32)
        x2, x3 = sb("x2_res", [P, KC, TB], F32), sb("x3", [P, KC, TB], F32)
        gain, offset, bias = (sb(n, [P, KC], F32) for n in ("ln_gain", "ln_offset", "b_out"))
        att_ps, ln_ps, out_ps = ps("att_ps", [P, KC, TB]), ps("o1_ln_ps", [P, 2, TB]), ps("out_ps", [P, KC, TB])
        (consts, x_loaded, q_hi, q_lo, att_done, o_ready, affine, gated, out_done, x3_ready, x3_stored) = (
            sem(n) for n in ("consts", "x_loaded", "q_hi", "q_lo", "att_done", "o_ready", "affine",
                             "gated", "out_done", "x3_ready", "x3_stored"))
        ln = LayerNorm("ln3", nc, sb, sem, K["ones"], [o], o_ready, ln_ps[:, 0, :], ln_ps[:, 1, :])
        wout = chunk_of("L1_attn_w_out")

        sem.start()
        with nc.Block() as block:
            @block.sync
            def _(sp):
                for dst, name in ((gain, "L1_attn_ln_g"), (offset, "L1_attn_ln_b"), (bias, "L1_attn_b_out")):
                    sp.dma_start(dst[:, :], column(d[name]), allow_slow_non_contiguous=True).then_inc(consts, 16)
                with sp.Fori(0, NB) as i:
                    sp.wait_ge(x3_ready, count(i))
                    sp.dma_start(x2[:, :, :], feature_major(d["X2T"])[:, :, ds(i, TB)]).then_inc(x_loaded, 16)
                    sp.wait_ge(x3_ready, count(i + 1))
                    sp.dma_start(feature_major(d["X3T"])[:, :, ds(i, TB)], x3[:, :, :]).then_inc(x3_stored, 16)
                sp.wait_ge(x3_stored, count(16 * NB))

            @block.tensor
            def _(pe):
                with pe.Fori(0, NB) as i:
                    pe.wait_ge(q_lo, count(i + 1))
                    pe.wait_ge(o_ready, count(i))
                    for k in range(KC):
                        mm = product3(nc, att_ps[:, k, :], [w[:, k, :] for w in R["kv"]],
                                      [v[:, k, :] for v in q], True, True)
                    mm.then_inc(att_done, 1)
                    ln.tensor_mean(pe, i)
                    ln.tensor_var(pe, i)
                    pe.wait_ge(ln.lo_ready, count(i + 1))
                    pe.wait_ge(x3_ready, count(i))
                    for n in range(KC):
                        mm = project3(nc, out_ps[:, n, :], (K["wt_hi"], K["wt_lo"]), ln.cut[0],
                                      slice(wout + n * P, wout + (n + 1) * P))
                    mm.then_inc(out_done, 1)

            @block.scalar
            def _(act):
                act.wait_ge(consts, count(48))
                with act.Fori(0, NB) as i:
                    act.wait_ge(att_done, count(i))
                    nc.scalar.copy(q[0][:, :, :], R["Q1"][:, :, ds(i, TB)]).then_inc(q_hi, 1)
                    act.wait_ge(att_done, count(i + 1))
                    nc.scalar.copy(o[:, :, :], att_ps[:, :, :]).then_inc(o_ready, 1)
                    ln.scalar_square(act, i)
                    ln.scalar_std(act, i, K["eps"])
                    act.wait_ge(ln.normed, count(i + 1))
                    for k in range(KC):
                        nc.scalar.activation(ln.xc[:, k, :], ln.xn[:, k, :], ACT.Identity,
                                             bias=offset[:, k:k + 1], scale=gain[:, k:k + 1]).then_inc(affine, 1)
                    act.wait_ge(gated, count(i + 1))
                    nc.scalar.copy(ln.cut[0][0][:, :, :], ln.xn[:, :, :]).then_inc(ln.hi_ready, 1)

            @block.vector
            def _(dve):
                dve.wait_ge(consts, count(48))
                with dve.Fori(0, NB) as i:
                    dve.wait_ge(q_hi, count(i + 1))
                    nc.vector.tensor_tensor(q[1][:, :, :], R["Q1"][:, :, ds(i, TB)],
                                            q[0][:, :, :].bitcast(F32), ALU.subtract).then_inc(q_lo, 1)
                    ln.vector_centre(dve, i)
                    ln.vector_reciprocal(dve, i)
                    ln.vector_scale(dve, i)
                    dve.wait_ge(affine, count(KC * (i + 1)))
                    nc.vector.tensor_tensor(ln.xn[:, :, :], ln.xc[:, :, :], R["G1"][:, :, ds(i, TB)],
                                            ALU.mult).then_inc(gated, 1)
                    ln.vector_lo(dve, i)
                    dve.wait_ge(out_done, count(i + 1))
                    dve.wait_ge(x_loaded, count(16 * (i + 1)))
                    dve.wait_ge(x3_stored, count(16 * i))
                    for n in range(KC):
                        ins = nc.vector.scalar_tensor_tensor(
                            out=x3[:, n, :], in0=out_ps[:, n, :], scalar=bias[:, n:n + 1],
                            in1=x2[:, n, :], op0=ALU.add, op1=ALU.add)
                    ins.then_inc(x3_ready, 1)



E = 64
TOP = 8
EH = 64
PAIRS = E * EH // P
SH = 1024
SC = SH // P


def moe_phase(nc, d, K):
    with ExitStack() as wctx:
        wsb = lambda n, s, t: wctx.enter_context(nc.sbuf_tensor(n, s, t))
        w1 = [wsb(f"moe_w1_{p}", [P, KC, E * EH], F32R) for p in ("hi", "lo")]
        w2 = [wsb(f"moe_w2_{p}", [P, PAIRS, D], F32R) for p in ("hi", "lo")]
        s1 = [wsb(f"moe_s1_{p}", [P, KC, SH], F32R) for p in ("hi", "lo")]
        s2 = [wsb(f"moe_s2_{p}", [P, SC, D], F32R) for p in ("hi", "lo")]
        rw = [wsb(f"moe_rw_{p}", [P, KC, E], F32R) for p in ("hi", "lo")]
        items = []
        for k in range(KC):
            src = d["L1_ffn_router_w"].rearrange("(k p) (o e) -> p k o e", p=P, o=1)[:, k]
            items.append((src, *[v[:, k:k + 1, :] for v in rw]))
        G = 16
        for g in range(E // G):
            for k in range(KC):
                src = d["L1_ffn_w1"][g * G:(g + 1) * G, k * P:(k + 1) * P, :].rearrange("e p h -> p e h")
                items.append((src, *[v[:, k, g * G * EH:(g + 1) * G * EH].rearrange("p (e h) -> p e h", e=G)
                                     for v in w1]))
            for a in range(G // 8):
                lo_e = g * G + a * 8
                src = d["L1_ffn_w2"].rearrange("e h n -> (e h) n")[lo_e * EH:(lo_e + 8) * EH].rearrange(
                    "(a p) n -> p a n", p=P)
                items.append((src, *[v[:, lo_e // 2:lo_e // 2 + 4, :] for v in w2]))
        for s in range(2):
            half = SH // 2
            for k in range(KC):
                src = d["L1_ffn_sw1"][s, k * P:(k + 1) * P, :].rearrange("p (o h) -> p o h", o=1)
                items.append((src, *[v[:, k:k + 1, s * half:(s + 1) * half] for v in s1]))
            src = d["L1_ffn_sw2"][s].rearrange("(c p) n -> p c n", p=P)
            items.append((src, *[v[:, s * SC // 2:(s + 1) * SC // 2, :] for v in s2]))
        cut_weights(nc, "moe", items, G * EH)
        moe_blocks(nc, d, K, w1, w2, s1, s2, rw)


HEAD = 3


def moe_blocks(nc, d, K, w1, w2, s1, s2, rw):
    with ExitStack() as ctx:
        sb = lambda n, s, t: ctx.enter_context(nc.sbuf_tensor(n, s, t))
        sem = ctx.enter_context(PhaseSemaphores(nc, "moe"))
        ps = lambda n, s: ctx.enter_context(nc.psum_tensor(n, s, F32))
        x = sb("m_x", [P, KC, TB], F32)
        h_full = sb("m_h_full", [P, 2, TB], F32)
        h = [sb(f"m_h_{p}", [P, 2, TB], F32R) for p in ("hi", "lo")]
        logits, dropped = sb("logits", [P, TT, E], F32), sb("dropped", [P, TT, E], F32)
        best, row_max, row_sum = sb("best", [P, TT, TOP], F32), sb("row_max", [P, TT], F32), sb("row_sum", [P, TT], F32)
        cw = sb("cw", [P, TB], F32R)
        pick = sb("pick", [P, E], F32)
        pick_pair = sb("pick_pair", [P, 2, 2, EH], F32R)
        r_bias = sb("r_bias", [P, E], F32)
        b1, s_b1, s_b2 = sb("m_b1", [P, PAIRS], F32), sb("m_sb1", [P, SC], F32), sb("m_sb2", [P, 2, KC], F32)
        b2_sum = sb("m_b2_sum", [P, KC], F32)
        b2_raw = sb("m_b2_raw", [P, D], F32)
        b2 = [sb(f"m_b2_{p}", [P, D], F32R) for p in ("hi", "lo")]
        turn_ps, h_ps, c_ps, y_ps = (ps(n, [P, 2, TB]) for n in ("m_turn", "m_h", "m_c", "m_y"))
        (consts, pick_set, b_cut, x_loaded, x_reloaded, logit_done, logit_ready, max_ready,
         cent_ready, exp_ready, best_ready, drop_ready, kept_ready, sum_ready, r_ready, cw_ready, cw_turned,
         cw_hi, cw_lo, h_done, spread, full_ready, hi_ready, lo_ready, y_used, x4_ready, out_turned,
         out_ready, out_stored, kept_weights, picked, dve_passed, pe_passed, passed) = (
            sem(n) for n in (
                "consts", "pick", "b_cut", "x_loaded", "x_reloaded", "logit_done",
                "logit_ready", "max", "cent", "exp", "best", "drop", "kept", "sum", "r", "cw", "cw_turned",
                "cw_hi", "cw_lo", "h_done", "spread", "full", "hi", "lo", "y_used", "x4", "out_turned",
                "out_ready", "out_stored", "kept_weights", "picked", "dve_passed", "pe_passed",
                "pool_passed"))
        sp_passed = sem("sp_passed")
        ln = LayerNorm("ln4", nc, sb, sem, K["ones"], [x], x_loaded, turn_ps[:, 0, :], turn_ps[:, 1, :])
        out_tok = ln.xc[:, :, :].rearrange("p k n -> p (k n)").rearrange("p (t f) -> p t f", t=TT)
        out_dram = d["out"].rearrange("a (t p) n -> p (a t) n", p=P)
        x3_dram = feature_major(d["X3T"])
        C = SC + PAIRS

        def heads_and_tails(eng, head, tail):
            head(0, False)
            with eng.Fori(0, NB - 1) as i:
                tail(i, True)
                head(i + 1, True)
            tail(NB - 1, False)

        sem.start()
        with nc.Block() as block:
            @block.sync
            def _(sp):
                def col(dst, src):
                    sp.dma_start(dst, src, allow_slow_non_contiguous=True).then_inc(consts, 16)

                sp.dma_start(x[:, :, :], x3_dram[:, :, 0:TB]).then_inc(x_loaded, 16)
                sp.dma_start(r_bias[:, :], d["L1_ffn_router_b"].partition_broadcast(P)).then_inc(consts, 16)
                col(b1[:, :], column(d["L1_ffn_b1"].rearrange("e h -> (e h)")))
                col(s_b1[:, :], column(d["L1_ffn_sb1"].rearrange("e h -> (e h)")))
                for s in range(2):
                    col(s_b2[:, s, :], column(d["L1_ffn_sb2"][s]))
                    sp.dma_start(b2_raw[s * E:(s + 1) * E, :], d["L1_ffn_b2"]).then_inc(consts, 16)
                sp.wait_ge(ln.centred, count(1))
                with sp.Fori(0, NB - 1) as i:
                    sp.dma_start(x[:, :, :], x3_dram[:, :, ds(i + 1, TB)]).then_inc(x_loaded, 16)
                    sp.wait_ge(ln.centred, count(i + 2))
                    alone(sp, sp_passed)
                    sp.dma_start(x[:, :, :], x3_dram[:, :, ds(i, TB)]).then_inc(x_reloaded, 16)
                    sp.wait_ge(out_ready, count((i + 1) * 2))
                    sp.dma_start(out_dram[:, ds(i, TT), :], out_tok).then_inc(out_stored, 16)
                sp.dma_start(x[:, :, :], x3_dram[:, :, (NB - 1) * TB:]).then_inc(x_reloaded, 16)
                sp.wait_ge(out_ready, count(2 * NB))
                sp.dma_start(out_dram[:, (NB - 1) * TT:, :], out_tok).then_inc(out_stored, 16)
                sp.wait_ge(out_stored, count(16 * NB))

            @block.gpsimd
            def _(pool):
                nc.gpsimd.memset(pick[:, :], 0.0).then_inc(pick_set, 1)
                for n, base in enumerate((0, -E)):
                    pool.wait_ge(pick_set, count(n + 1))
                    nc.gpsimd.affine_select(out=pick[:, :], in_=pick[:, :], compare_op=ALU.not_equal,
                                            fill=1.0, base=base, pattern=[[-1, E]],
                                            channel_multiplier=1).then_inc(pick_set, 1)
                pool.wait_ge(pick_set, count(3))
                with pool.Fori(0, NB) as i:
                    for p in range(PAIRS):
                        pool.wait_ge(spread, count(i * PAIRS + max(p - 1, 0)))
                        alone(pool, passed)
                        nc.gpsimd.tensor_copy(pick_pair[:, p % 2, :, :],
                                              pick[:, 2 * p:2 * p + 2].unsqueeze(2).to_broadcast([P, 2, EH])
                                              ).then_inc(picked, 1)
                        pool.wait_ge(picked, count(i * PAIRS + (p + 1)))

            @block.tensor
            def _(pe):
                def hidden(i, c):
                    pe.wait_ge(full_ready, count(i * C + max(c - 1, 0)))
                    if c < SC:
                        w, cols = s1, slice(c * P, (c + 1) * P)
                    else:
                        w, cols = w1, slice((c - SC) * P, (c - SC + 1) * P)
                    project3(nc, h_ps[:, c % 2, :], w, ln.cut[0], cols).then_inc(h_done, 1)
                    if c >= SC:
                        p = c - SC
                        if p == 0:
                            pe.wait_ge(cw_lo, count(i + 1))
                            pe.wait_ge(out_ready, count(i * 2))
                        pe.wait_ge(kept_ready, count(i * PAIRS + max(p - 1, 0)))
                        pe.wait_ge(picked, count(i * PAIRS + (p + 1)))
                        nc.tensor.matmul(c_ps[:, c % 2, :],
                                         pick_pair[:, p % 2, :, :].rearrange("q a b -> q (a b)"),
                                         cw[:, :], start=True, stop=True).then_inc(spread, 1)

                def output(i, c):
                    w, k = (s2, c) if c < SC else (w2, c - SC)
                    pe.wait_ge(lo_ready, count(i * C + (c + 1)))
                    if c == 0:
                        pe.wait_ge(x4_ready, count(i))
                    for n in range(KC):
                        mm = product3(nc, y_ps[:, n, :], [v[:, k, n * P:(n + 1) * P] for v in w],
                                      [v[:, c % 2, :] for v in h], c == 0, c == C - 1)
                    mm.then_inc(y_used, 1)

                def second_bias():
                    for n in range(KC):
                        for p in range(2):
                            nc.tensor.matmul(y_ps[:, n, :], b2[p][:, n * P:(n + 1) * P], cw[:, :],
                                             start=False, stop=False)

                def turn_output(i):
                    pe.wait_ge(x4_ready, count(i + 1))
                    alone(pe, pe_passed)
                    for k in range(KC):
                        for t in range(TT):
                            mm = nc.tensor.transpose(
                                c_ps[:, t // 2, t % 2 * D + k * P:t % 2 * D + (k + 1) * P],
                                x[:, k, t * P:(t + 1) * P], K["ident"][:, :])
                    mm.then_inc(out_turned, 1)

                def head(i, finish):
                    pe.wait_ge(ln.lo_ready, count(i + 1))
                    for t in range(TT):
                        for k in range(KC):
                            mm = product3(nc, turn_ps[:, 0, t * E:(t + 1) * E],
                                          [v[:, k, t * P:(t + 1) * P] for v in ln.cut[0]],
                                          [v[:, k, :] for v in rw], k == 0, k == KC - 1)
                    mm.then_inc(logit_done, 1)
                    hidden(i, 0)
                    for c in range(1, HEAD):
                        hidden(i, c)
                        output(i, c - 1)
                        if c == 1 and finish:
                            turn_output(i - 1)

                def tail(i, following):
                    for c in range(HEAD, C):
                        hidden(i, c)
                        output(i, c - 1)
                        if c == SC - 2:
                            pe.wait_ge(cw_ready, count(i + 1))
                            alone(pe, pe_passed)
                            for t in range(TT):
                                mm = nc.tensor.transpose(turn_ps[0:E, 1, t * P:(t + 1) * P], dropped[:, t, :],
                                                         K["ident"][:, :])
                            mm.then_inc(cw_turned, 1)
                        if following and c == 12:
                            pe.wait_ge(x_loaded, count((i + 2) * 16))
                            ln.tensor_mean_of_ready()
                        if following and c == 16:
                            ln.tensor_var(pe, i + 1)
                    second_bias()
                    output(i, C - 1)

                pe.wait_ge(b_cut, count(3))
                pe.wait_ge(x_loaded, count(16))
                ln.tensor_mean_of_ready()
                ln.tensor_var(pe, 0)
                heads_and_tails(pe, head, tail)
                turn_output(NB - 1)

            @block.scalar
            def _(act):
                def chunk(i, c):
                    act.wait_ge(h_done, count(i * C + (c + 1)))
                    act.wait_ge(y_used, count(i * C + max(c - 1, 0)))
                    bias = s_b1[:, c:c + 1] if c < SC else b1[:, c - SC:c - SC + 1]
                    nc.scalar.activation(h_full[:, c % 2, :], h_ps[:, c % 2, :], ACT.Silu,
                                         bias=bias).then_inc(full_ready, 1)
                    if c < SC:
                        act.wait_ge(full_ready, count(i * C + (c + 1)))
                    else:
                        act.wait_ge(kept_ready, count(i * PAIRS + (c - SC + 1)))
                    nc.scalar.copy(h[0][:, c % 2, :], h_full[:, c % 2, :]).then_inc(hi_ready, 1)

                def copy_output(i):
                    act.wait_ge(out_turned, count(i + 1))
                    for t in range(2):
                        nc.scalar.copy(out_tok[:, 2 * t:2 * t + 2, :],
                                       c_ps[:, t, :].rearrange("p (a n) -> p a n", a=2)).then_inc(out_ready, 1)

                def head(i, finish):
                    for c in range(HEAD):
                        chunk(i, c)
                    if finish:
                        copy_output(i - 1)

                def tail(i, following):
                    act.wait_ge(cent_ready, count(i + 1))
                    nc.scalar.activation(logits[:, :, :], logits[:, :, :], ACT.Exp).then_inc(exp_ready, 1)
                    for c in range(HEAD, C):
                        if following and c == 14:
                            ln.scalar_square(act, i + 1)
                        if following and c == 18:
                            ln.scalar_std(act, i + 1, K["eps"])
                        chunk(i, c)
                    if following:
                        ln.scalar_hi(act, i + 1)

                act.wait_ge(consts, count(16 * 7))
                nc.scalar.copy(b2[0][:, :], b2_raw[:, :]).then_inc(b_cut, 1)
                ln.scalar_square(act, 0)
                ln.scalar_std(act, 0, K["eps"])
                ln.scalar_hi(act, 0)
                heads_and_tails(act, head, tail)
                copy_output(NB - 1)

            @block.vector
            def _(dve):
                def router(i, step):
                    if step == "centre":
                        dve.wait_ge(logit_done, count(i + 1))
                        nc.vector.tensor_tensor(
                            logits[:, :, :], turn_ps[:, 0, 0:TT * E].rearrange("p (t e) -> p t e", t=TT),
                            r_bias[:, :].unsqueeze(1).to_broadcast([P, TT, E]), ALU.add).then_inc(logit_ready, 1)
                        dve.wait_ge(logit_ready, count(i + 1))
                        nc.vector.tensor_reduce(row_max[:, :], logits[:, :, :], AX.X,
                                                ALU.max).then_inc(max_ready, 1)
                        dve.wait_ge(max_ready, count(i + 1))
                        nc.vector.tensor_tensor(logits[:, :, :], logits[:, :, :],
                                                row_max[:, :].unsqueeze(2).to_broadcast([P, TT, E]),
                                                ALU.subtract).then_inc(cent_ready, 1)
                    elif step == "best":
                        dve.wait_ge(exp_ready, count(i + 1))
                        alone(dve, dve_passed)
                        for t in range(TT):
                            nc.vector.max(best[:, t, :], logits[:, t, :]).then_inc(best_ready, 1)
                    elif step == "drop":
                        dve.wait_ge(best_ready, count((i + 1) * TT))
                        dve.wait_ge(cw_turned, count(i))
                        alone(dve, dve_passed)
                        for t in range(TT):
                            nc.vector.match_replace(dropped[:, t, :], best[:, t, :], logits[:, t, :],
                                                    0.0).then_inc(drop_ready, 1)
                        nc.vector.tensor_reduce(row_sum[:, :], best[:, :, :], AX.X, ALU.add).then_inc(sum_ready, 1)
                        dve.wait_ge(sum_ready, count(i + 1))
                        nc.vector.reciprocal(row_sum[:, :], row_sum[:, :]).then_inc(r_ready, 1)
                    elif step == "weights":
                        dve.wait_ge(drop_ready, count((i + 1) * TT))
                        nc.vector.tensor_tensor(logits[:, :, :], logits[:, :, :], dropped[:, :, :],
                                                ALU.subtract).then_inc(kept_weights, 1)
                        dve.wait_ge(r_ready, count(i + 1))
                        dve.wait_ge(kept_weights, count(i + 1))
                        nc.vector.tensor_tensor(dropped[:, :, :], logits[:, :, :],
                                                row_sum[:, :].unsqueeze(2).to_broadcast([P, TT, E]),
                                                ALU.mult).then_inc(cw_ready, 1)
                    elif step == "cut":
                        dve.wait_ge(cw_turned, count(i + 1))
                        dve.wait_ge(y_used, count(i * C))
                        nc.vector.tensor_copy(cw[0:E, :], turn_ps[0:E, 1, :]).then_inc(cw_hi, 1)
                        dve.wait_ge(cw_hi, count(i + 1))
                        nc.vector.tensor_tensor(cw[E:2 * E, :], turn_ps[0:E, 1, :], cw[0:E, :].bitcast(F32),
                                                ALU.subtract).then_inc(cw_lo, 1)

                def chunk(i, c):
                    if c >= SC:
                        dve.wait_ge(full_ready, count(i * C + (c + 1)))
                        dve.wait_ge(spread, count(i * PAIRS + (c - SC + 1)))
                        nc.vector.tensor_tensor(h_full[:, c % 2, :], h_full[:, c % 2, :], c_ps[:, c % 2, :],
                                                ALU.mult).then_inc(kept_ready, 1)
                    dve.wait_ge(hi_ready, count(i * C + (c + 1)))
                    nc.vector.tensor_tensor(h[1][:, c % 2, :], h_full[:, c % 2, :],
                                            h[0][:, c % 2, :].bitcast(F32),
                                            ALU.subtract).then_inc(lo_ready, 1)

                def head(i, finish):
                    chunk(i, 0)
                    router(i, "centre")
                    for c in range(1, HEAD):
                        chunk(i, c)

                def tail(i, following):
                    for c in range(HEAD, C):
                        chunk(i, c)
                        router(i, {HEAD: "best", HEAD + 1: "drop", HEAD + 2: "weights", SC - 2: "cut"}.get(c))
                        if following and c == 13:
                            dve.wait_ge(out_stored, count(i * 16))
                            ln.vector_centre(dve, i + 1)
                        if following and c == 19:
                            ln.vector_reciprocal(dve, i + 1)
                        if following and c == 21:
                            ln.vector_scale(dve, i + 1)
                    if following:
                        ln.vector_lo(dve, i + 1)
                    dve.wait_ge(y_used, count((i + 1) * C))
                    dve.wait_ge(x_reloaded, count((i + 1) * 16))
                    for n in range(KC):
                        ins = nc.vector.scalar_tensor_tensor(
                            out=x[:, n, :], in0=y_ps[:, n, :], scalar=b2_sum[:, n:n + 1],
                            in1=x[:, n, :], op0=ALU.add, op1=ALU.add)
                    ins.then_inc(x4_ready, 1)

                dve.wait_ge(consts, count(16 * 7))
                nc.vector.tensor_tensor(b2_sum[:, :], s_b2[:, 0, :], s_b2[:, 1, :], ALU.add).then_inc(b_cut, 1)
                dve.wait_ge(b_cut, count(2))
                nc.vector.tensor_tensor(b2[1][:, :], b2_raw[:, :], b2[0][:, :].bitcast(F32),
                                        ALU.subtract).then_inc(b_cut, 1)
                ln.vector_centre(dve, 0)
                ln.vector_reciprocal(dve, 0)
                ln.vector_scale(dve, 0)
                ln.vector_lo(dve, 0)
                heads_and_tails(dve, head, tail)



def scratch(nc):
    t = lambda n, s, dt: nc.dram_tensor(n, s, dt).ap()
    return {"X0T": t("X0T", (D, T), F32), "QS": t("QS", (PARTS, D, T), BF16),
            "KS": t("KS", (PARTS, D, T), BF16), "NUM": t("NUM", (D, T), F32), "DEN": t("DEN", (D, T), F32),
            "X2T": t("X2T", (D, T), F32), "X3T": t("X3T", (D, T), F32)}


def program(nc, d):
    d = {**d, **scratch(nc)}
    with ExitStack() as ctx:
        sb = lambda n, s, t: ctx.enter_context(nc.sbuf_tensor(n, s, t))
        K = {"ident": sb("ident", [P, P], F32), "ident_b": sb("ident_b", [P, P], BF16),
             "ones": sb("ones", [P, P], F32), "eps": sb("eps", [P, 1], F32)}
        with ExitStack() as weights:
            wsb = lambda n, s: weights.enter_context(nc.sbuf_tensor(n, s, F32R))
            K |= {f"wt_{p}": wsb(f"wt_{p}", [P, KC, CHUNKS * P]) for p in ("hi", "lo")}
            K |= {f"g1_{p}": wsb(f"g1_{p}", [P, KC, HD]) for p in ("hi", "lo")}
            K |= {f"g2_{p}": wsb(f"g2_{p}", [HD, D]) for p in ("hi", "lo")}
            setup_phase(nc, d, K)
            with ExitStack() as att:
                V_all = att.enter_context(nc.sbuf_tensor("V_all", [P, MC, D], F32))
                qkv0_phase(nc, d, K, V_all)
                attention_phase(nc, d, K, V_all)
            ffn0_phase(nc, d, K)
            with ExitStack() as layer1:
                rsb = lambda n, s, t: layer1.enter_context(nc.sbuf_tensor(n, s, t))
                R = {n: rsb(n, [P, KC, T], F32) for n in ("Q1", "K1", "G1")}
                R["V1"] = rsb("V1", [P, MC, D], F32)
                R["kv"] = [rsb(f"kv_{p}", [P, KC, P], F32R) for p in ("hi", "lo")]
                qkv1_phase(nc, d, K, R)
                kv1_phase(nc, d, K, R)
                out1_phase(nc, d, K, R)
        moe_phase(nc, d, K)



def kernel(**inputs):
    import numpy as np
    from concourse import bacc
    from concourse.bass_utils import run_bass_kernel_spmd

    nc = bacc.Bacc("TRN2", target_bir_lowering=False, num_devices=1)
    arrays, d = {}, {}
    for name, value in inputs.items():
        a = np.ascontiguousarray(value)
        arrays[f"in_{name}"] = a
        d[name] = nc.dram_tensor(f"in_{name}", a.shape, mybir.dt.from_np(a.dtype), kind="ExternalInput").ap()
    d["out"] = nc.dram_tensor("out_0", (1, T, D), F32, kind="ExternalOutput").ap()
    program(nc, d)
    r = run_bass_kernel_spmd(nc, [arrays], core_ids=[0])
    return r.results[0]["out_0"]
```

```python
from contextlib import ExitStack

import concourse.bass as bass
from concourse import mybir

F32 = mybir.dt.float32
F32R = mybir.dt.float32r
BF16 = mybir.dt.bfloat16
ALU = mybir.AluOpType
ACT = mybir.ActivationFunctionType
AX = mybir.AxisListType

P = 128
D = 256
KC = D // P
T = 4096
TB = 512
NB = T // TB
TT = TB // P
HEADS = 16
HD = D // HEADS
EPS = 1e-5


def ds(i, n):
    return bass.ds(i * n, n)


def alone(eng, passed):
    eng.sem_inc(passed, 1)


def feature_major(ap):
    return ap.rearrange("(k p) n -> p k n", p=P)


def column(ap):
    return ap.rearrange("(c p) -> p c", p=P)


def product3(nc, out, w, x, first, last):
    nc.tensor.matmul(out, w[0], x[0], start=first, stop=False)
    nc.tensor.matmul(out, w[0], x[1], start=False, stop=False)
    return nc.tensor.matmul(out, w[1], x[0], start=False, stop=last)


def project3(nc, out, w, x, cols, first=True, last=True):
    for k in range(KC):
        mm = product3(nc, out, [v[:, k, cols] for v in w], [v[:, k, :] for v in x],
                      first and k == 0, last and k == KC - 1)
    return mm


class PhaseSemaphores:

    def __init__(self, nc, phase):
        self.nc, self.phase, self.held, self.from_zero = nc, phase, [], []

    def __call__(self, name, from_zero=False):
        self.held.append(self.nc.alloc_semaphore(f"{self.phase}_{name}"))
        if from_zero:
            self.from_zero.append(len(self.held) - 1)
        return self.held[-1]

    def start(self):
        for n, s in enumerate(self.held):
            if n not in self.from_zero:
                self.nc.gpsimd.sem_inc(s, FIRST)
        self.nc.all_engine_barrier()

    def __enter__(self):
        return self

    def __exit__(self, *_):
        self.nc.clear_and_free_semaphores(self.held)
        self.nc.all_engine_barrier()


FIRST = 1


def count(events):
    return events + FIRST


class LayerNorm:

    def __init__(self, name, nc, sb, sem, ones, x, x_ready, mean_ps, var_ps, slots=1):
        self.nc, self.ones, self.x, self.x_ready = nc, ones, x, x_ready
        self.mean_ps, self.var_ps = mean_ps, var_ps
        self.xc = sb(f"{name}_xc", [P, KC, TB], F32)
        self.sq = sb(f"{name}_sq", [P, KC, TB], F32)
        self.std = self.sq[:, 0, :]
        self.xn = self.xc
        self.cut = [[sb(f"{name}_{p}{s}", [P, KC, TB], F32R) for p in ("hi", "lo")] for s in range(slots)]
        self.mean_ready, self.centred, self.squared, self.var_ready, self.std_ready, self.rstd_ready, \
            self.normed, self.hi_ready, self.lo_ready = (
                sem(f"{name}_{s}") for s in ("mean", "centred", "squared", "var", "std", "rstd",
                                             "normed", "hi", "lo"))

    def tensor_mean(self, pe, i, slot=0):
        pe.wait_ge(self.x_ready, count(i + 1))
        self.tensor_mean_of_ready(slot)

    def tensor_mean_of_ready(self, slot=0):
        for k in range(KC):
            mm = self.nc.tensor.matmul(self.mean_ps, self.ones[:, :], self.x[slot][:, k, :],
                                       start=(k == 0), stop=(k == KC - 1))
        mm.then_inc(self.mean_ready, 1)

    def tensor_var(self, pe, i):
        pe.wait_ge(self.squared, count(i + 1))
        for k in range(KC):
            mm = self.nc.tensor.matmul(self.var_ps, self.ones[:, :], self.sq[:, k, :],
                                       start=(k == 0), stop=(k == KC - 1))
        mm.then_inc(self.var_ready, 1)

    def vector_centre(self, dve, i, slot=0):
        dve.wait_ge(self.lo_ready, count(i))
        dve.wait_ge(self.mean_ready, count(i + 1))
        mean = self.mean_ps.unsqueeze(1).to_broadcast([P, KC, TB])
        self.nc.vector.tensor_tensor(self.xc[:, :, :], self.x[slot][:, :, :], mean,
                                     ALU.subtract).then_inc(self.centred, 1)

    def vector_reciprocal(self, dve, i, half):
        dve.wait_ge(self.std_ready, count(i + 1))
        std = self.std[:, half * (TB // 2):(half + 1) * (TB // 2)]
        self.nc.vector.reciprocal(std, std).then_inc(self.rstd_ready, 1)

    def vector_scale(self, dve, i):
        dve.wait_ge(self.rstd_ready, count(i * 2 + 2))
        rstd = self.std.unsqueeze(1).to_broadcast([P, KC, TB])
        self.nc.vector.tensor_tensor(self.xn[:, :, :], self.xc[:, :, :], rstd,
                                     ALU.mult).then_inc(self.normed, 1)

    def vector_lo(self, dve, i, slot=0):
        dve.wait_ge(self.hi_ready, count(i + 1))
        hi, lo = self.cut[slot]
        self.nc.vector.tensor_tensor(lo[:, :, :], self.xn[:, :, :], hi[:, :, :].bitcast(F32),
                                     ALU.subtract).then_inc(self.lo_ready, 1)

    def scalar_square(self, act, i):
        act.wait_ge(self.centred, count(i + 1))
        self.nc.scalar.activation(self.sq[:, :, :], self.xc[:, :, :], ACT.Square).then_inc(self.squared, 1)

    def scalar_std(self, act, i, eps):
        act.wait_ge(self.var_ready, count(i + 1))
        self.nc.scalar.activation(self.std, self.var_ps, ACT.Sqrt,
                                  bias=eps[:, 0:1]).then_inc(self.std_ready, 1)

    def scalar_hi(self, act, i, slot=0):
        act.wait_ge(self.normed, count(i + 1))
        self.nc.scalar.copy(self.cut[slot][0][:, :, :], self.xn[:, :, :]).then_inc(self.hi_ready, 1)


def overlapped(eng, body):
    with eng.Fori(0, NB // 2 - 1) as half:
        for slot in range(2):
            body(half, half * 2 + slot, slot, 2)
    for slot in range(2):
        body(NB // 2 - 1, NB - 2 + slot, slot, 1 - slot)



NATURAL = [("L0_attn_Wq", 2), ("L0_attn_Wk", 2), ("L0_attn_Wv", 2), ("L0_attn_Wo", 2),
           ("L1_attn_w_qkv", 6), ("L1_attn_w_out", 2)]
CHUNKS = sum(n for _, n in NATURAL)


def chunk_of(name):
    at = 0
    for n, c in NATURAL:
        if n == name:
            return at * P
        at += c


def setup_phase(nc, d, K):
    with ExitStack() as ctx:
        sb = lambda n, s, t: ctx.enter_context(nc.sbuf_tensor(n, s, t))
        sem = ctx.enter_context(PhaseSemaphores(nc, "setup"))
        natural = sb("natural", [P, CHUNKS, D], F32)
        g1_nat = sb("g1_nat", [HD, D], F32)
        g2_nat = sb("g2_nat", [P, KC, HD], F32)
        ps = ctx.enter_context(nc.psum_tensor("setup_ps", [P, 4, TB], F32))
        loaded, zeroed, consts = sem("w_loaded"), sem("zeroed"), sem("consts")
        turned, hi_done, lo_done = sem("turned"), sem("w_hi_done"), sem("w_lo_done")
        ident_b = sem("ident_bf16")
        wt_hi, wt_lo, ident = K["wt_hi"], K["wt_lo"], K["ident"]
        GROUPS = CHUNKS // 2
        LOADS = len(NATURAL) + 2

        with nc.Block() as block:
            @block.sync
            def _(sp):
                at = 0
                for name, c in NATURAL:
                    sp.dma_start(natural[:, at:at + c, :],
                                 d[name].rearrange("(c p) n -> p c n", p=P)).then_inc(loaded, 16)
                    at += c
                sp.dma_start(g1_nat[:, :], d["L1_attn_w_g1"]).then_inc(loaded, 16)
                sp.dma_start(g2_nat[:, :, :],
                             d["L1_attn_w_g2"].rearrange("(k p) n -> p k n", p=P)).then_inc(loaded, 16)

            @block.gpsimd
            def _(pool):
                nc.gpsimd.memset(ident[:, :], 0.0).then_inc(zeroed, 1)
                nc.gpsimd.memset(K["ones"][:, :], 1.0 / D).then_inc(consts, 1)
                nc.gpsimd.memset(K["eps"][:, :], EPS).then_inc(consts, 1)
                pool.wait_ge(zeroed, 1)
                nc.gpsimd.affine_select(out=ident[:, :], in_=ident[:, :], compare_op=ALU.not_equal,
                                        fill=1.0, base=0, pattern=[[-1, P]],
                                        channel_multiplier=1).then_inc(consts, 1)

            @block.tensor
            def _(pe):
                pe.wait_ge(consts, 3)
                pe.wait_ge(loaded, 16 * LOADS)
                for g in range(GROUPS):
                    if g >= 4:
                        pe.wait_ge(lo_done, g - 3)
                    for c in range(2):
                        for k in range(KC):
                            mm = nc.tensor.transpose(
                                ps[:, g % 4, k * D + c * P:k * D + (c + 1) * P],
                                natural[:, 2 * g + c, k * P:(k + 1) * P], ident[:, :])
                    mm.then_inc(turned, 1)
                pe.wait_ge(lo_done, GROUPS)
                for k in range(KC):
                    nc.tensor.transpose(ps[:, 0, k * HD:(k + 1) * HD], g1_nat[:, k * P:(k + 1) * P],
                                        ident[0:HD, 0:HD])
                for k in range(KC):
                    mm = nc.tensor.transpose(ps[0:HD, 1, k * P:(k + 1) * P], g2_nat[:, k, :],
                                             ident[:, :])
                mm.then_inc(turned, 1)

            @block.scalar
            def _(act):
                act.wait_ge(consts, 3)
                nc.scalar.copy(K["ident_b"][:, :], ident[:, :]).then_inc(ident_b, 1)
                for g in range(GROUPS):
                    act.wait_ge(turned, g + 1)
                    nc.scalar.copy(wt_hi[:, :, g * D:(g + 1) * D],
                                   ps[:, g % 4, :].rearrange("p (k n) -> p k n", k=KC)).then_inc(hi_done, 1)
                act.wait_ge(turned, GROUPS + 1)
                nc.scalar.copy(K["g1_hi"][:, :, :],
                               ps[:, 0, 0:KC * HD].rearrange("p (k n) -> p k n", k=KC)).then_inc(hi_done, 1)
                nc.scalar.copy(K["g2_hi"][:, :], ps[0:HD, 1, 0:D]).then_inc(hi_done, 1)

            @block.vector
            def _(dve):
                for g in range(GROUPS):
                    dve.wait_ge(hi_done, g + 1)
                    nc.vector.tensor_tensor(
                        wt_lo[:, :, g * D:(g + 1) * D], ps[:, g % 4, :].rearrange("p (k n) -> p k n", k=KC),
                        wt_hi[:, :, g * D:(g + 1) * D].bitcast(F32), ALU.subtract).then_inc(lo_done, 1)
                dve.wait_ge(hi_done, GROUPS + 2)
                nc.vector.tensor_tensor(
                    K["g1_lo"][:, :, :], ps[:, 0, 0:KC * HD].rearrange("p (k n) -> p k n", k=KC),
                    K["g1_hi"][:, :, :].bitcast(F32), ALU.subtract)
                nc.vector.tensor_tensor(K["g2_lo"][:, :], ps[0:HD, 1, 0:D],
                                        K["g2_hi"][:, :].bitcast(F32), ALU.subtract)



PARTS = 3


def qkv0_phase(nc, d, K, V_all):
    with ExitStack() as ctx:
        sb = lambda n, s, t: ctx.enter_context(nc.sbuf_tensor(n, s, t))
        sem = ctx.enter_context(PhaseSemaphores(nc, "qkv0"))
        ps = lambda n, s: ctx.enter_context(nc.psum_tensor(n, s, F32))
        x_tok = [sb(f"x_tok{s}", [P, TT, D], F32) for s in range(2)]
        xT = sb("xT", [P, KC, TB], F32)
        rest = sb("rest", [P, 2, TB], F32)
        parts = [sb(f"parts{s}", [P, 4, PARTS, TB], BF16) for s in range(2)]
        qk_bias = sb("qk_bias", [P, 4], F32)
        v_bias = sb("v_bias", [P, D], F32)
        turn_ps, ln_ps = ps("turn_ps", [P, KC, TB]), ps("ln_ps", [P, 2, TB])
        qk_ps, v_ps = ps("qk_ps", [P, 2, TB]), ps("v_ps", [P, 2, TB])
        (passed, bias_loaded, turned, xT_ready, xT_stored, qk_done, high_ready, rest_ready,
         mid_ready, low_ready, v_done, v_ready) = (sem(n) for n in (
             "passed", "bias_loaded", "turned0", "xT_ready", "xT_stored", "qk_done",
             "high_ready", "rest_ready", "mid_ready", "low_ready", "v_done", "v_ready"))
        x_loaded = [sem(f"x_loaded{s}") for s in range(2)]
        qk_stored = [sem(f"qk_stored{s}") for s in range(2)]
        ln = LayerNorm("ln0", nc, sb, sem, K["ones"], [xT], xT_ready, ln_ps[:, 0, :], ln_ps[:, 1, :], 2)
        wq = chunk_of("L0_attn_Wq")
        wv = chunk_of("L0_attn_Wv")
        x_dram = d["L0_attn_x"].rearrange("a (t p) n -> p (a t) n", p=P)

        sem.start()
        with nc.Block() as block:
            @block.sync
            def _(sp):
                def load_x(j, slot):
                    sp.dma_start(x_tok[slot][:, :, :], x_dram[:, ds(j, TT), :]).then_inc(x_loaded[slot], 16)

                def store_xT(j):
                    sp.wait_ge(xT_ready, count(j + 1))
                    sp.dma_start(feature_major(d["X0T"])[:, :, ds(j, TB)], xT[:, :, :]).then_inc(xT_stored, 16)

                def blocks(half, i, slot, following):
                    if following == 2:
                        sp.wait_ge(turned, count(i + 1))
                        load_x(i + 2, slot)
                    if following:
                        store_xT(i + 1)
                    for c in range(4):
                        sp.wait_ge(low_ready, count(i * 4 + (c + 1)))
                        alone(sp, passed)
                        dst = d["QS"] if c < 2 else d["KS"]
                        sp.dma_start(
                            dst.rearrange("j (k p) n -> p k j n", p=P)[:, c % 2, :, ds(i, TB)],
                            parts[slot][:, c, :, :]).then_inc(qk_stored[slot], 16)

                load_x(0, 0)
                load_x(1, 1)
                sp.dma_start(qk_bias[:, 0:2], column(d["L0_attn_bq"]), allow_slow_non_contiguous=True).then_inc(bias_loaded, 16)
                sp.dma_start(qk_bias[:, 2:4], column(d["L0_attn_bk"]), allow_slow_non_contiguous=True).then_inc(bias_loaded, 16)
                sp.dma_start(v_bias[:, :], d["L0_attn_bv"].partition_broadcast(P)).then_inc(bias_loaded, 16)
                store_xT(0)
                overlapped(sp, blocks)
                sp.wait_ge(xT_stored, count(16 * NB))
                for s in range(2):
                    sp.wait_ge(qk_stored[s], count(16 * 4 * NB // 2))

            @block.tensor
            def _(pe):
                def turn(j, half, slot):
                    pe.wait_ge(x_loaded[slot], count(half * 16 + 16))
                    pe.wait_ge(xT_ready, count(j))
                    for k in range(KC):
                        for t in range(TT):
                            mm = nc.tensor.transpose(turn_ps[:, k, t * P:(t + 1) * P],
                                                     x_tok[slot][:, t, k * P:(k + 1) * P], K["ident"][:, :])
                    mm.then_inc(turned, 1)

                def queries_keys(i, slot, c):
                    pe.wait_ge(rest_ready, count(i * 4 + max(c - 1, 0)))
                    project3(nc, qk_ps[:, c % 2, :], (K["wt_hi"], K["wt_lo"]), ln.cut[slot],
                             slice(wq + c * P, wq + (c + 1) * P)).then_inc(qk_done, 1)

                def values(i, slot, pair):
                    pe.wait_ge(v_ready, count(i * 2))
                    for t in (2 * pair, 2 * pair + 1):
                        for k in range(KC):
                            x = [v[:, k, t * P:(t + 1) * P] for v in ln.cut[slot]]
                            w = [v[:, k, wv:wv + D] for v in (K["wt_hi"], K["wt_lo"])]
                            mm = product3(nc, v_ps[:, pair, t % 2 * D:(t % 2 + 1) * D], x, w,
                                          k == 0, k == KC - 1)
                    mm.then_inc(v_done, 1)

                def blocks(half, i, slot, following):
                    pe.wait_ge(ln.lo_ready, count(i + 1))
                    queries_keys(i, slot, 0)
                    if following:
                        ln.tensor_mean(pe, i + 1)
                    queries_keys(i, slot, 1)
                    queries_keys(i, slot, 2)
                    if following:
                        ln.tensor_var(pe, i + 1)
                    queries_keys(i, slot, 3)
                    for pair in range(TT // 2):
                        values(i, slot, pair)
                    if following == 2:
                        turn(i + 2, half + 1, slot)

                turn(0, 0, 0)
                ln.tensor_mean(pe, 0)
                ln.tensor_var(pe, 0)
                turn(1, 0, 1)
                overlapped(pe, blocks)

            @block.scalar
            def _(act):
                def copy_xT(j):
                    act.wait_ge(turned, count(j + 1))
                    act.wait_ge(ln.centred, count(j))
                    act.wait_ge(xT_stored, count(j * 16))
                    nc.scalar.copy(xT[:, :, :], turn_ps[:, :, :]).then_inc(xT_ready, 1)

                def high(half, i, slot, c):
                    act.wait_ge(qk_done, count(i * 4 + (c + 1)))
                    act.wait_ge(qk_stored[slot], count(half * 64))
                    nc.scalar.activation(parts[slot][:, c, 0, :], qk_ps[:, c % 2, :], ACT.Identity,
                                         bias=qk_bias[:, c:c + 1]).then_inc(high_ready, 1)

                def mid(i, slot, c):
                    act.wait_ge(rest_ready, count(i * 4 + (c + 1)))
                    nc.scalar.copy(parts[slot][:, c, 1, :], rest[:, c % 2, :]).then_inc(mid_ready, 1)

                def blocks(half, i, slot, following):
                    high(half, i, slot, 0)
                    high(half, i, slot, 1)
                    if following:
                        ln.scalar_square(act, i + 1)
                    mid(i, slot, 0)
                    high(half, i, slot, 2)
                    mid(i, slot, 1)
                    if following:
                        ln.scalar_std(act, i + 1, K["eps"])
                    high(half, i, slot, 3)
                    mid(i, slot, 2)
                    if following:
                        ln.scalar_hi(act, i + 1, 1 - slot)
                    mid(i, slot, 3)
                    if following == 2:
                        copy_xT(i + 2)

                copy_xT(0)
                ln.scalar_square(act, 0)
                ln.scalar_std(act, 0, K["eps"])
                ln.scalar_hi(act, 0, 0)
                copy_xT(1)
                act.wait_ge(bias_loaded, count(48))
                overlapped(act, blocks)

            @block.vector
            def _(dve):
                def left(i, slot, c):
                    dve.wait_ge(high_ready, count(i * 4 + (c + 1)))
                    dve.wait_ge(low_ready, count(i * 4 + max(c - 1, 0)))
                    nc.vector.scalar_tensor_tensor(
                        out=rest[:, c % 2, :], in0=qk_ps[:, c % 2, :], scalar=qk_bias[:, c:c + 1],
                        in1=parts[slot][:, c, 0, :], op0=ALU.add, op1=ALU.subtract).then_inc(rest_ready, 1)

                def low(i, slot, c):
                    dve.wait_ge(mid_ready, count(i * 4 + (c + 1)))
                    nc.vector.tensor_tensor(parts[slot][:, c, 2, :], rest[:, c % 2, :], parts[slot][:, c, 1, :],
                                            ALU.subtract).then_inc(low_ready, 1)

                def values(i, pair):
                    dve.wait_ge(v_done, count(i * 2 + (pair + 1)))
                    nc.vector.tensor_tensor(
                        V_all[:, bass.ds(i * TT + 2 * pair, 2), :],
                        v_ps[:, pair, :].rearrange("p (a n) -> p a n", a=2),
                        v_bias[:, :].unsqueeze(1).to_broadcast([P, 2, D]), ALU.add).then_inc(v_ready, 1)

                def blocks(half, i, slot, following):
                    left(i, slot, 0)
                    if following:
                        ln.vector_centre(dve, i + 1)
                    left(i, slot, 1)
                    low(i, slot, 0)
                    left(i, slot, 2)
                    low(i, slot, 1)
                    if following:
                        for part in range(2):
                            ln.vector_reciprocal(dve, i + 1, part)
                        ln.vector_scale(dve, i + 1)
                    left(i, slot, 3)
                    low(i, slot, 2)
                    if following:
                        ln.vector_lo(dve, i + 1, 1 - slot)
                    low(i, slot, 3)
                    values(i, 0)
                    values(i, 1)

                ln.vector_centre(dve, 0)
                for part in range(2):
                    ln.vector_reciprocal(dve, 0, part)
                ln.vector_scale(dve, 0)
                ln.vector_lo(dve, 0, 0)
                dve.wait_ge(bias_loaded, count(48))
                overlapped(dve, blocks)



MC = T // P
QUADS = MC // 4
STACK = 6 * HD
ROWS = STACK + PARTS
K_PARTS = (0, 0, 0, 1, 1, 2)
Q_PARTS = (0, 1, 2, 0, 1, 0)
SCALE = 1.0 / D ** 0.5
A_BANKS = 3
TURN_SLOT = 24


def a_slot(u):
    return u - 12 if u >= 12 else u + TURN_SLOT - 4 + (u >= 4)


def attention_phase(nc, d, K, V_all):
    with ExitStack() as ctx:
        sb = lambda n, s, t: ctx.enter_context(nc.sbuf_tensor(n, s, t))
        sem = ctx.enter_context(PhaseSemaphores(nc, "att"))
        ps = lambda n, s: ctx.enter_context(nc.psum_tensor(n, s, F32))
        QST = sb("QST", [P, 2, T], BF16)
        KA = sb("KA", [P, 2, TB], BF16)
        KB = sb("KB", [P, 2, TB], BF16)
        VH = sb("VH", [P, 2, MC, 2 * HD], F32)
        PR = sb("PR", [P, 4, 2, TB], F32)
        PM = sb("PM", [P, 2, TT, NB], F32)
        neg = sb("neg", [P, 2, TT], F32)
        neg_rest = sb("neg_rest", [P, TT], F32)
        NM = sb("NM", [P, TT, 4], BF16)
        OS = sb("OS", [P, 2, TB], F32)
        OG = sb("OG", [2 * HD, 3, TB], F32)
        O2 = sb("O2", [2 * HD, 3, TB], F32)
        SB = ps("SB", [P, 2, 2, TB])
        A = ps("A", [P, A_BANKS, TB])
        PV = ps("PV", [P, TB])
        TN = A[:, TURN_SLOT % A_BANKS, :]

        q_loaded = [sem(f"q_loaded{i}") for i in range(2)]
        ka_loaded = [sem(f"ka_loaded{i}") for i in range(2)]
        kb_loaded = [sem(f"kb_loaded{i}") for i in range(2)]
        passed = sem("passed")
        rows_set, ones_set, vh_ready = sem("rows_set"), sem("ones_set"), sem("vh_ready")
        b_done = sem("b_done")
        a_done = sem("a_done")
        b_free = sem("b_free")
        a_free = sem("a_free")
        p_free = sem("p_free")
        os_free = sem("os_free")
        AHEAD = 2
        neg_ready, neg_high, neg_left, neg_parts = (
            sem("neg_ready"), sem("neg_high"), sem("neg_left"), sem("neg_parts"))
        shift_turned, shift_ready = sem("shift_turned"), sem("shift_ready")
        pv_read, groups_moved, half_sums, o_stored = (
            sem("pv_read"), sem("groups_moved", from_zero=True), sem("half_sums"),
            sem("o_stored", from_zero=True))
        STEPS = HEADS * NB
        UNITS = TT * NB
        LOAD = 16 * len(K_PARTS)

        def in_steps(eng, body):
            with eng.Fori(0, HEADS // 2) as pair:
                for hp in range(2):
                    with eng.Fori(0, NB // 2 - 1) as two:
                        for par in range(2):
                            body(pair * NB + two + hp * (NB // 2), pair, hp, None, par)
                    for nb in (NB - 2, NB - 1):
                        body(pair * NB + (hp * NB + nb) // 2, pair, hp, nb, nb % 2)

        sem.start()
        with nc.Block() as block:
            @block.sync
            def _(sp):
                def load_stack(dst, name, parts, head, cols, signal):
                    for r, j in enumerate(parts):
                        sp.dma_start(dst[r * HD:(r + 1) * HD, :],
                                     d[name][j, bass.ds(head * HD, HD), cols]).then_inc(signal, 16)

                def load_k(dst, par, head, nb, signal):
                    load_stack(dst[:, par, :], "KS", K_PARTS, head, slice(nb * TB, (nb + 1) * TB),
                               signal[par])

                def head_loads(h, hp, following):
                    for nb in range(NB):
                        t = h * NB + nb
                        sp.wait_ge(b_done, count(t * (2 * QUADS)))
                        load_k(KB, (nb + 1) % 2, h if nb + 1 < NB else following, (nb + 1) % NB, kb_loaded)
                        sp.wait_ge(a_done, count((t + 1) * UNITS))
                        load_k(KA, nb % 2, h if nb + 2 < NB else following, (nb + 2) % NB, ka_loaded)
                        if nb == 0:
                            load_stack(QST[:, 1 - hp, :], "QS", Q_PARTS, following, slice(0, T),
                                       q_loaded[1 - hp])

                load_k(KA, 0, 0, 0, ka_loaded)
                load_stack(QST[:, 0, :], "QS", Q_PARTS, 0, slice(0, T), q_loaded[0])
                load_k(KA, 1, 0, 1, ka_loaded)
                load_k(KB, 0, 0, 0, kb_loaded)
                with sp.Fori(0, HEADS // 2 - 1) as pair:
                    for hp in range(2):
                        head_loads(pair * 2 + hp, hp, pair * 2 + (hp + 1))
                head_loads(HEADS - 2, 0, HEADS - 1)
                head_loads(HEADS - 1, 1, 0)

            @block.tensor
            def _(pe):
                def unit_a(block, u, par, slot):
                    i, j = divmod(u, NB)
                    before = a_slot(u) - TURN_SLOT
                    if before == A_BANKS:
                        pe.wait_ge(shift_ready, count(block))
                    elif 0 < before < A_BANKS:
                        pe.wait_ge(a_free, count(block * UNITS + (u + 2)))
                    else:
                        pe.wait_ge(a_free, count(block * UNITS + (u + 1)))
                    nc.tensor.matmul(A[:, a_slot(u) % A_BANKS, :], KA[0:STACK, par, i * P:(i + 1) * P],
                                     QST[0:STACK, slot, j * TB:(j + 1) * TB],
                                     start=True, stop=True).then_inc(a_done, 1)

                def chunk_b(step, m, par, slot):
                    pair, e = divmod(m, 2)
                    if e == 0:
                        pe.wait_ge(b_free, count(step * (2 * QUADS) + (pair + 1)))
                    mm = nc.tensor.matmul(SB[:, pair % 2, e, :], QST[0:ROWS, slot, m * P:(m + 1) * P],
                                          KB[0:ROWS, par, :], start=True, stop=True)
                    if e == 1:
                        mm.then_inc(b_done, 1)

                def values(step, q, slot):
                    if q == 0:
                        pe.wait_ge(pv_read, count(step))
                    pe.wait_ge(b_free, count(step * (2 * QUADS) + (AHEAD + 2 * q + 2)))
                    for r in range(4):
                        m = 4 * q + r
                        mm = nc.tensor.matmul(PV[32 * r:32 * r + 32, :], VH[:, slot, m, :],
                                              PR[:, m // 2 % 4, r % 2, :],
                                              start=(q == 0), stop=(q == QUADS - 1))
                    mm.then_inc(p_free, 1)

                def turn_shift(block):
                    pe.wait_ge(neg_parts, count(block + 1))
                    pe.wait_ge(a_free, count((block + 1) * UNITS + (2 + A_BANKS)))
                    for i in range(TT):
                        mm = nc.tensor.matmul(TN[STACK:ROWS, i * P:(i + 1) * P], NM[:, i, 0:PARTS],
                                              K["ident_b"][:, :], start=True, stop=True)
                    mm.then_inc(shift_turned, 1)

                def step(half, pair, hp, nb, par):
                    t = half * 2 + par
                    for q in range(1, QUADS + 1):
                        a_block, a_par = (t + 1, 1 - par) if q < 6 else (t + 2, par)
                        a_next = nb == NB - 1 or (nb == NB - 2 and q >= 6)
                        a_slot = 1 - hp if a_next else hp
                        if q == 6:
                            pe.wait_ge(ka_loaded[par], count((half + 2) * LOAD))
                            if nb == NB - 2:
                                pe.wait_ge(q_loaded[1 - hp], count((pair + (hp + 1)) * LOAD))
                        b_next = q == QUADS
                        if b_next:
                            pe.wait_ge(kb_loaded[1 - par], count((half + (par + 1)) * LOAD))
                            pe.wait_ge(shift_ready, count(t + 2))
                        for r in range(4):
                            chunk_b(t + 1 if b_next else t, 4 * (q % QUADS) + r,
                                    1 - par if b_next else par, 1 - hp if b_next and nb == NB - 1 else hp)
                            unit_a(a_block, 4 * ((q + 2) % QUADS) + r, a_par, a_slot)
                        if q == 1:
                            pe.wait_ge(vh_ready, count(pair * 2 + (hp + 1)))
                        if q == 6:
                            turn_shift(t + 1)
                        values(t, q - 1, hp)

                pe.wait_ge(rows_set, count(1))
                pe.wait_ge(q_loaded[0], count(LOAD))
                pe.wait_ge(ka_loaded[0], count(LOAD))
                for u in range(UNITS):
                    unit_a(0, u, 0, 0)
                pe.wait_ge(ka_loaded[1], count(LOAD))
                for u in range(4):
                    unit_a(1, u, 1, 0)
                turn_shift(0)
                for u in range(4, 8):
                    unit_a(1, u, 1, 0)
                pe.wait_ge(kb_loaded[0], count(LOAD))
                pe.wait_ge(shift_ready, count(1))
                for r in range(4):
                    chunk_b(0, r, 0, 0)
                    unit_a(1, 8 + r, 1, 0)
                in_steps(pe, step)

            @block.scalar
            def _(act):
                def exp_pair(step, pair):
                    if pair % 2 == 0:
                        act.wait_ge(p_free, count(step * QUADS + (pair // 2 + 1)))
                    act.wait_ge(b_done, count(step * (2 * QUADS) + (pair + 1)))
                    nc.scalar.activation(PR[:, pair % 4, :, :], SB[:, pair % 2, :, :], ACT.Exp,
                                         scale=SCALE).then_inc(b_free, 1)

                def place_shift(block, par):
                    act.wait_ge(shift_turned, count(block + 1))
                    nc.scalar.copy(KB[STACK:ROWS, par, :], TN[STACK:ROWS, :]).then_inc(shift_ready, 1)

                def step(half, pair, hp, nb, par):
                    t = half * 2 + par
                    for q in range(1, QUADS):
                        if q == QUADS - 1:
                            place_shift(t + 1, 1 - par)
                        exp_pair(t, 2 * q)
                        exp_pair(t, 2 * q + 1)
                    exp_pair(t + 1, 0)
                    exp_pair(t + 1, 1)
                    act.wait_ge(p_free, count((t + 1) * QUADS + AHEAD))
                    act.wait_ge(os_free, count(t + 1))
                    nc.scalar.copy(OS[:, par, :], PV[:, :]).then_inc(pv_read, 1)

                act.sem_inc(b_free, AHEAD)
                place_shift(0, 0)
                exp_pair(0, 0)
                exp_pair(0, 1)
                in_steps(act, step)

            @block.vector
            def _(dve):
                def unit_max(block, u, par):
                    dve.wait_ge(a_done, count(block * UNITS + (u + 1)))
                    i, j = divmod(u, NB)
                    nc.vector.tensor_reduce(PM[:, par, i, j:j + 1], A[:, a_slot(u) % A_BANKS, :], AX.X,
                                            ALU.max).then_inc(a_free, 1)

                def block_max(block, par):
                    for u in range(UNITS):
                        unit_max(block, u, par)
                    dve.wait_ge(a_free, count((block + 1) * UNITS + A_BANKS))
                    nc.vector.tensor_reduce(neg[:, par, :], PM[:, par, :, :], AX.X, ALU.max,
                                            negate=True).then_inc(neg_ready, 1)

                nc.vector.memset(QST[STACK:ROWS, :, :], 1.0).then_inc(rows_set, 1)
                dve.sem_inc(a_free, A_BANKS)
                with dve.Fori(0, STEPS // 2) as two:
                    for par in range(2):
                        block_max(two * 2 + par, par)
                block_max(STEPS, 0)
                for u in range(12):
                    unit_max(STEPS + 1, u, 1)

            @block.gpsimd
            def _(pool):
                def values_of(head, slot):
                    nc.gpsimd.tensor_copy(VH[:, slot, :, 0:HD],
                                          V_all[:, :, bass.ds(head * HD, HD)]).then_inc(vh_ready, 1)

                def shift_parts(block, par):
                    pool.wait_ge(neg_ready, count(block + 1))
                    pool.wait_ge(shift_turned, count(block))
                    alone(pool, passed)
                    nc.gpsimd.tensor_copy(NM[:, :, 0], neg[:, par, :]).then_inc(neg_high, 1)
                    pool.wait_ge(neg_high, count(block * 2 + 1))
                    nc.gpsimd.tensor_tensor(neg_rest[:, :], neg[:, par, :], NM[:, :, 0],
                                            ALU.subtract).then_inc(neg_left, 1)
                    pool.wait_ge(neg_left, count(block + 1))
                    alone(pool, passed)
                    nc.gpsimd.tensor_copy(NM[:, :, 1], neg_rest[:, :]).then_inc(neg_high, 1)
                    pool.wait_ge(neg_high, count(block * 2 + 2))
                    nc.gpsimd.tensor_tensor(NM[:, :, 2], neg_rest[:, :], NM[:, :, 1],
                                            ALU.subtract).then_inc(neg_parts, 1)

                def step(t, h, hp, par, nb, next_head):
                    shift_parts(t + 1, 1 - par)
                    if next_head is not None:
                        pool.wait_ge(p_free, count(h * (NB * QUADS) + AHEAD))
                        alone(pool, passed)
                        values_of(next_head, 1 - hp)
                    pool.wait_ge(pv_read, count(t + 1))
                    pool.wait_ge(os_free, count(t + AHEAD))
                    alone(pool, passed)
                    for g in range(3):
                        pool.dma_start(OG[:, g, :], OS[32 * (g + 1):32 * (g + 2), par, :]
                                       ).then_inc(groups_moved, 16)
                    pool.wait_ge(groups_moved, (t + 1) * 48)
                    nc.gpsimd.tensor_tensor(O2[:, 0, :], OS[0:2 * HD, par, :], OG[:, 0, :],
                                            ALU.add).then_inc(half_sums, 1)
                    nc.gpsimd.tensor_tensor(O2[:, 1, :], OG[:, 1, :], OG[:, 2, :],
                                            ALU.add).then_inc(half_sums, 1)
                    pool.wait_ge(half_sums, count((t + 1) * 2))
                    nc.gpsimd.tensor_tensor(O2[:, 2, :], O2[:, 0, :], O2[:, 1, :],
                                            ALU.add).then_inc(os_free, 1)
                    pool.wait_ge(os_free, count(t + 1 + AHEAD))
                    alone(pool, passed)
                    cols = bass.ds(nb * TB, TB)
                    for j, name in enumerate(("NUM", "DEN")):
                        pool.dma_start(d[name][bass.ds(h * HD, HD), cols],
                                       O2[j * HD:(j + 1) * HD, 2, :]).then_inc(o_stored, 16)
                    pool.wait_ge(o_stored, (t + 1) * 32)

                pool.sem_inc(p_free, AHEAD)
                pool.sem_inc(os_free, AHEAD)
                nc.gpsimd.memset(VH[:, :, :, HD:2 * HD], 1.0).then_inc(ones_set, 1)
                pool.wait_ge(ones_set, count(1))
                values_of(0, 0)
                shift_parts(0, 0)
                with pool.Fori(0, HEADS // 2 - 1) as pair:
                    for hp in range(2):
                        for nb in range(NB):
                            step(pair * (2 * NB) + (hp * NB + nb), pair * 2 + hp, hp, nb % 2, nb,
                                 pair * 2 + (hp + 1) if nb == 0 else None)
                for hp in range(2):
                    h = HEADS - 2 + hp
                    for nb in range(NB):
                        step(h * NB + nb, h, hp, nb % 2, nb, h + 1 if nb == 0 and hp == 0 else None)



class WeightCut:

    def __init__(self, nc, sem, items, places):
        self.nc, self.items, self.places = nc, items, places
        self.loaded = [sem(f"weights_loaded{p}") for p in range(len(places))]
        self.hi_done, self.lo_done = sem("weights_hi"), sem("weights_lo")

    def staged(self, n):
        part, a, b = self.items[n][1].shape
        return self.places[n % len(self.places)][0:part, 0:a * b].rearrange("p (a b) -> p a b", a=a)

    def load(self, sp):
        ring = len(self.places)
        for n, (src, _, _) in enumerate(self.items):
            if n >= ring:
                sp.wait_ge(self.lo_done, count(n - ring + 1))
            sp.dma_start(self.staged(n), src).then_inc(self.loaded[n % ring], 16)

    def hi(self, act, n):
        act.wait_ge(self.loaded[n % len(self.places)], count(n // len(self.places) * 16 + 16))
        self.nc.scalar.copy(self.items[n][1], self.staged(n)).then_inc(self.hi_done, 1)

    def lo(self, dve, n):
        dve.wait_ge(self.hi_done, count(n + 1))
        self.nc.vector.tensor_tensor(self.items[n][2], self.staged(n), self.items[n][1].bitcast(F32),
                                     ALU.subtract).then_inc(self.lo_done, 1)

    def ready(self, eng):
        eng.wait_ge(self.lo_done, count(len(self.items)))



HID = 1024
HC = HID // P
EXPERTS0 = 3
RING = 3
LAG = 2


def ffn0_phase(nc, d, K):
    with ExitStack() as wctx:
        wsb = lambda n, s, t: wctx.enter_context(nc.sbuf_tensor(n, s, t))
        w1 = [wsb(f"f0_w1_{p}", [P, EXPERTS0, KC, HID], F32R) for p in ("hi", "lo")]
        w2 = [wsb(f"f0_w2_{p}", [P, EXPERTS0, HC, D], F32R) for p in ("hi", "lo")]
        sources = [(d["L0_ffn_sw1"], d["L0_ffn_sw2"])] + [(d["L0_ffn_w1"][e], d["L0_ffn_w2"][e]) for e in range(2)]
        items = []
        for e, (a, b) in enumerate(sources):
            for k in range(KC):
                items.append((a.rearrange("(k p) h -> p k h", p=P)[:, k:k + 1, :],
                              *[v[:, e, k:k + 1, :] for v in w1]))
            for half in (slice(0, HC // 2), slice(HC // 2, HC)):
                items.append((b.rearrange("(c p) n -> p c n", p=P)[:, half, :], *[v[:, e, half, :] for v in w2]))
        ffn0_blocks(nc, d, K, w1, w2, items)


def ffn0_blocks(nc, d, K, w1, w2, items):
    with ExitStack() as ctx:
        sb = lambda n, s, t: ctx.enter_context(nc.sbuf_tensor(n, s, t))
        sem = ctx.enter_context(PhaseSemaphores(nc, "ffn0"))
        ps = lambda n, s: ctx.enter_context(nc.psum_tensor(n, s, F32))
        num, den = sb("num", [P, KC, TB], F32), sb("den", [P, KC, TB], F32)
        x = [sb(f"f0_x{s}", [P, KC, TB], F32) for s in range(2)]
        gate_out = [sb(f"gate_out{s}", [P, TB], F32) for s in range(2)]
        chosen = sb("chosen", [P, 2, TB], F32)
        h_full = sb("h_full", [P, RING, TB], F32)
        h = [sb(f"h_{p}", [P, RING, TB], F32R) for p in ("hi", "lo")]
        bo, b1, b2 = sb("bo", [P, KC], F32), sb("b1", [P, EXPERTS0 * HC], F32), sb("b2", [P, EXPERTS0, KC], F32)
        b2_sum = sb("b2_sum", [P, KC], F32)
        gate_cols = sb("gate_cols", [P, 2, KC], F32)
        gate_diff = sb("gate_diff", [P, KC, 2], F32)
        gate = [sb(f"gate_{p}", [P, KC, P], F32R) for p in ("hi", "lo")]
        front_ps, h_ps, y_ps = ps("front_ps", [P, KC, TB]), ps("h_ps", [P, RING, TB]), ps("y_ps", [P, KC, TB])
        (consts, diffed, num_loaded, rden, o_full, o_hi, o_lo, proj_done, x1_ready, gate_done,
         gate_ready, h_done, chosen_ready, full_ready, hi_ready, lo_ready, h_free, summed, x2_ready, x2_stored) = (
            sem(n) for n in ("consts", "diffed", "num_loaded", "rden", "o_full", "o_hi", "o_lo",
                             "proj_done", "x1_ready", "gate_done", "gate_ready", "h_done", "chosen",
                             "full_ready", "hi_ready", "lo_ready", "h_free", "summed", "x2_ready", "x2_stored"))
        x_loaded = [sem(f"x_loaded{s}") for s in range(2)]
        passed = sem("passed")
        places = [v.rearrange("p a n -> p (a n)") for v in (h_full[:, 0:2, :], chosen[:, :, :], x[1][:, :, :])]
        weights = WeightCut(nc, sem, items, places)
        ln = LayerNorm("ln1", nc, sb, sem, K["ones"], x, x1_ready, front_ps[:, 0, :], front_ps[:, 1, :], 2)
        wo = chunk_of("L0_attn_Wo")
        C = EXPERTS0 * HC
        ROUTED = C - HC
        CONST_LOADS = 16 * 9

        sem.start()
        with nc.Block() as block:
            @block.sync
            def _(sp):
                def col(dst, src):
                    sp.dma_start(dst, column(src), allow_slow_non_contiguous=True).then_inc(consts, 16)

                def load_sums(j):
                    sp.dma_start(num[:, :, :], feature_major(d["NUM"])[:, :, ds(j, TB)]).then_inc(num_loaded, 16)
                    sp.dma_start(den[:, :, :], feature_major(d["DEN"])[:, :, ds(j, TB)]).then_inc(num_loaded, 16)

                def load_x(j, slot):
                    sp.dma_start(x[slot][:, :, :], feature_major(d["X0T"])[:, :, ds(j, TB)]
                                 ).then_inc(x_loaded[slot], 16)

                def blocks(half, i, slot, following):
                    if following:
                        sp.wait_ge(x2_stored, count(i * 16))
                        alone(sp, passed)
                        load_x(i + 1, 1 - slot)
                    if following == 2:
                        sp.wait_ge(o_lo, count(i + 2))
                        load_sums(i + 2)
                    sp.wait_ge(x2_ready, count(i + 1))
                    sp.dma_start(feature_major(d["X2T"])[:, :, ds(i, TB)], x[slot][:, :, :]).then_inc(x2_stored, 16)

                load_sums(0)
                load_x(0, 0)
                col(bo[:, :], d["L0_attn_bo"])
                col(b1[:, 0:HC], d["L0_ffn_sb1"])
                col(b2[:, 0, :], d["L0_ffn_sb2"])
                for e in range(2):
                    col(b1[:, (e + 1) * HC:(e + 2) * HC], d["L0_ffn_b1"][e])
                    col(b2[:, e + 1, :], d["L0_ffn_b2"][e])
                    col(gate_cols[:, e, :], d["L0_ffn_gate_w"][e])
                weights.load(sp)
                weights.ready(sp)
                sp.wait_ge(o_lo, count(1))
                load_sums(1)
                overlapped(sp, blocks)
                sp.wait_ge(x2_stored, count(16 * NB))

            @block.tensor
            def _(pe):
                def front(j, slot, part):
                    if part == "projection":
                        pe.wait_ge(gate_ready, count(j))
                        pe.wait_ge(o_lo, count(j + 1))
                        for n in range(KC):
                            mm = project3(nc, front_ps[:, n, :], (K["wt_hi"], K["wt_lo"]), ln.cut[slot],
                                          slice(wo + n * P, wo + (n + 1) * P))
                        mm.then_inc(proj_done, 1)
                    elif part == "mean":
                        ln.tensor_mean(pe, j, slot)
                    elif part == "variance":
                        ln.tensor_var(pe, j)
                    elif part == "gate":
                        pe.wait_ge(ln.lo_ready, count(j + 1))
                        project3(nc, front_ps[:, 0, :], gate, ln.cut[slot], slice(0, P)).then_inc(gate_done, 1)

                def hidden(i, slot, c):
                    if c < RING:
                        pe.wait_ge(chosen_ready, count(i * ROUTED))
                    elif c - RING < HC:
                        pe.wait_ge(hi_ready, count(i * C + (c - RING + 1)))
                    else:
                        pe.wait_ge(chosen_ready, count(i * ROUTED + (c - RING - HC + 1)))
                    project3(nc, h_ps[:, c % RING, :], [w[:, c // HC, :, :] for w in w1], ln.cut[slot],
                             slice(c % HC * P, (c % HC + 1) * P)).then_inc(h_done, 1)

                def output(i, c):
                    e, k = divmod(c, HC)
                    pe.wait_ge(lo_ready, count(i * C + (c + 1)))
                    if c == 0:
                        pe.wait_ge(x2_ready, count(i))
                    for n in range(KC):
                        mm = product3(nc, y_ps[:, n, :], [w[:, e, k, n * P:(n + 1) * P] for w in w2],
                                      [v[:, c % RING, :] for v in h], c == 0, c == C - 1)
                    mm.then_inc(h_free, 1)

                def blocks(half, i, slot, following):
                    for c in range(C + LAG):
                        if c < C:
                            hidden(i, slot, c)
                        if c >= LAG:
                            output(i, c - LAG)
                        if following:
                            front(i + 1, 1 - slot, {9: "projection", 11: "mean", 14: "variance", 22: "gate"}.get(c))

                pe.wait_ge(diffed, count(4))
                for part in ("projection", "mean", "variance", "gate"):
                    front(0, 0, part)
                weights.ready(pe)
                overlapped(pe, blocks)

            @block.scalar
            def _(act):
                def front(j, slot, part):
                    if part == "o_hi":
                        act.wait_ge(o_full, count(j + 1))
                        nc.scalar.copy(ln.cut[slot][0][:, :, :], num[:, :, :]).then_inc(o_hi, 1)
                    elif part == "square":
                        ln.scalar_square(act, j)
                    elif part == "std":
                        ln.scalar_std(act, j, K["eps"])
                    elif part == "hi":
                        ln.scalar_hi(act, j, slot)

                def blocks(half, i, slot, following):
                    for c in range(C):
                        if following:
                            front(i + 1, 1 - slot, {6: "o_hi", 13: "square", 15: "std", 20: "hi"}.get(c))
                        act.wait_ge(h_free, count(i * C + (c + 1)))
                        if c < HC:
                            act.wait_ge(h_done, count(i * C + (c + 1)))
                            src = h_ps[:, c % RING, :]
                        else:
                            act.wait_ge(chosen_ready, count(i * ROUTED + (c - HC + 1)))
                            src = chosen[:, c % 2, :]
                        nc.scalar.activation(h_full[:, c % RING, :], src, ACT.Relu,
                                             bias=b1[:, c:c + 1]).then_inc(full_ready, 1)
                        nc.scalar.activation(h[0][:, c % RING, :], src, ACT.Relu,
                                             bias=b1[:, c:c + 1]).then_inc(hi_ready, 1)

                act.sem_inc(h_free, RING)
                act.wait_ge(consts, count(CONST_LOADS))
                act.wait_ge(diffed, count(2))
                nc.scalar.copy(gate[0][:, :, :], gate_diff[:, :, 0:1].to_broadcast([P, KC, P])
                               ).then_inc(diffed, 1)
                for n in range(len(items)):
                    weights.hi(act, n)
                    front(0, 0, {1: "o_hi", 4: "square", 6: "std", 9: "hi"}.get(n))
                overlapped(act, blocks)

            @block.vector
            def _(dve):
                def front(j, half, slot, part):
                    if part in ("den0", "den1", "den2", "den3"):
                        dve.wait_ge(num_loaded, count((j + 1) * 32))
                        quarter = den[:, :, int(part[-1]) * P:(int(part[-1]) + 1) * P]
                        nc.vector.reciprocal(quarter, quarter).then_inc(rden, 1)
                    elif part == "quotient":
                        dve.wait_ge(rden, count((j + 1) * 4))
                        nc.vector.tensor_tensor(num[:, :, :], num[:, :, :], den[:, :, :],
                                                ALU.mult).then_inc(o_full, 1)
                    elif part == "o_lo":
                        dve.wait_ge(o_hi, count(j + 1))
                        o = ln.cut[slot]
                        nc.vector.tensor_tensor(o[1][:, :, :], num[:, :, :], o[0][:, :, :].bitcast(F32),
                                                ALU.subtract).then_inc(o_lo, 1)
                    elif part == "x1":
                        dve.wait_ge(proj_done, count(j + 1))
                        dve.wait_ge(x_loaded[slot], count((half + 1) * 16))
                        for n in range(KC):
                            ins = nc.vector.scalar_tensor_tensor(
                                out=x[slot][:, n, :], in0=front_ps[:, n, :], scalar=bo[:, n:n + 1],
                                in1=x[slot][:, n, :], op0=ALU.add, op1=ALU.add)
                        ins.then_inc(x1_ready, 1)
                    elif part == "centre":
                        ln.vector_centre(dve, j, slot)
                    elif part in ("reciprocal0", "reciprocal1"):
                        ln.vector_reciprocal(dve, j, int(part[-1]))
                    elif part == "scale":
                        ln.vector_scale(dve, j)
                    elif part == "lo":
                        ln.vector_lo(dve, j, slot)
                    elif part == "gate":
                        dve.wait_ge(gate_done, count(j + 1))
                        nc.vector.tensor_copy(gate_out[slot][:, :], front_ps[:, 0, :]).then_inc(gate_ready, 1)

                def choose(i, slot, c):
                    if c == HC:
                        dve.wait_ge(gate_ready, count(i + 1))
                    dve.wait_ge(h_done, count(i * C + (c + 1)))
                    if c < HC + 2:
                        dve.wait_ge(hi_ready, count(i * C))
                    else:
                        dve.wait_ge(hi_ready, count(i * C + (c - 1)))
                    nc.vector.scalar_tensor_tensor(
                        out=chosen[:, c % 2, :], in0=gate_out[slot][:, :], scalar=0.0, in1=h_ps[:, c % RING, :],
                        op0=(ALU.is_le, ALU.is_gt)[c // HC - 1], op1=ALU.mult).then_inc(chosen_ready, 1)

                def blocks(half, i, slot, following):
                    for c in range(C):
                        if HC <= c + 1 < C:
                            choose(i, slot, c + 1)
                        dve.wait_ge(hi_ready, count(i * C + (c + 1)))
                        nc.vector.tensor_tensor(h[1][:, c % RING, :], h_full[:, c % RING, :],
                                                h[0][:, c % RING, :].bitcast(F32),
                                                ALU.subtract).then_inc(lo_ready, 1)
                        if following:
                            front(i + 1, half + slot, 1 - slot, {
                                1: "den0", 2: "den1", 3: "den2", 4: "den3", 5: "quotient", 7: "o_lo",
                                10: "x1", 12: "centre", 16: "reciprocal0", 18: "reciprocal1", 19: "scale",
                                21: "lo", 23: "gate"}.get(c))
                    dve.wait_ge(h_free, count((i + 1) * C + RING))
                    for n in range(KC):
                        ins = nc.vector.scalar_tensor_tensor(
                            out=x[slot][:, n, :], in0=y_ps[:, n, :], scalar=b2_sum[:, n:n + 1],
                            in1=x[slot][:, n, :], op0=ALU.add, op1=ALU.add)
                    ins.then_inc(x2_ready, 1)

                dve.wait_ge(consts, count(CONST_LOADS))
                for k in range(KC):
                    nc.vector.tensor_tensor(gate_diff[:, k, 0:1], gate_cols[:, 1, k:k + 1],
                                            gate_cols[:, 0, k:k + 1], ALU.subtract).then_inc(diffed, 1)
                nc.vector.tensor_tensor(b2_sum[:, :], b2[:, 0, :], b2[:, 1, :], ALU.add).then_inc(summed, 1)
                dve.wait_ge(summed, count(1))
                nc.vector.tensor_tensor(b2_sum[:, :], b2_sum[:, :], b2[:, 2, :], ALU.add)
                dve.wait_ge(diffed, count(3))
                nc.vector.tensor_tensor(gate[1][:, :, :], gate_diff[:, :, 0:1].to_broadcast([P, KC, P]),
                                        gate[0][:, :, :].bitcast(F32), ALU.subtract).then_inc(diffed, 1)
                for part in ("den0", "den1", "den2", "den3", "quotient"):
                    front(0, 0, 0, part)
                for n in range(len(items)):
                    weights.lo(dve, n)
                    front(0, 0, 0, {1: "o_lo", 2: "x1", 4: "centre", 6: "reciprocal0", 7: "reciprocal1",
                                    8: "scale", 9: "lo", 11: "gate"}.get(n))
                overlapped(dve, blocks)



def qkv1_phase(nc, d, K, R):
    with ExitStack() as ctx:
        sb = lambda n, s, t: ctx.enter_context(nc.sbuf_tensor(n, s, t))
        sem = ctx.enter_context(PhaseSemaphores(nc, "qkv1"))
        ps = lambda n, s: ctx.enter_context(nc.psum_tensor(n, s, F32))
        x2 = sb("x2_in", [P, KC, TB], F32)
        gh_full = sb("gh_full", [HD, TB], F32)
        gh = [sb(f"gh_{p}", [HD, TB], F32R) for p in ("hi", "lo")]
        qk_bias, g1_bias, g2_bias = sb("p1_qk_bias", [P, 4], F32), sb("g1_bias", [HD, 1], F32), sb("g2_bias", [P, KC], F32)
        v_bias = sb("p1_v_bias", [P, D], F32)
        ln_ps, qk_ps, v_ps, g_ps = (ps(n, [P, 2, TB]) for n in ("p1_ln_ps", "p1_qk_ps", "p1_v_ps", "p1_g_ps"))
        (consts, qk_done, qk_ready, gh_done, gh_full_ready, gh_hi_ready, gh_lo_ready, g_done,
         g_ready, v_done, v_ready) = (sem(n) for n in (
             "consts", "qk_done", "qk_ready", "gh_done", "gh_full_ready", "gh_hi_ready",
             "gh_lo_ready", "g_done", "g_ready", "v_done", "v_ready"))
        x_ready = sem("x_ready")
        ln = LayerNorm("ln2", nc, sb, sem, K["ones"], [x2], x_ready, ln_ps[:, 0, :], ln_ps[:, 1, :], 2)
        w0 = chunk_of("L1_attn_w_qkv")

        sem.start()
        with nc.Block() as block:
            @block.sync
            def _(sp):
                sp.dma_start(x2[:, :, :], feature_major(d["X2T"])[:, :, 0:TB]).then_inc(x_ready, 16)

                def col(dst, src):
                    sp.dma_start(dst, src, allow_slow_non_contiguous=True).then_inc(consts, 16)
                col(qk_bias[:, :], column(d["L1_attn_b_qkv"][0:2 * D]))
                col(g1_bias[:, :], d["L1_attn_b_g1"].rearrange("(p c) -> p c", c=1))
                col(g2_bias[:, :], column(d["L1_attn_b_g2"]))
                sp.dma_start(v_bias[:, :], d["L1_attn_b_qkv"][2 * D:3 * D].partition_broadcast(P)).then_inc(consts, 16)
                with sp.Fori(1, NB) as i:
                    sp.wait_ge(ln.centred, count(i))
                    sp.dma_start(x2[:, :, :], feature_major(d["X2T"])[:, :, ds(i, TB)]).then_inc(x_ready, 16)

            @block.tensor
            def _(pe):
                def mean(j):
                    pe.wait_ge(x_ready, count((j + 1) * 16))
                    ln.tensor_mean_of_ready()

                def queries_keys(i, slot, c):
                    pe.wait_ge(qk_ready, count(i * 4 + max(c - 1, 0)))
                    project3(nc, qk_ps[:, c % 2, :], (K["wt_hi"], K["wt_lo"]), ln.cut[slot],
                             slice(w0 + c * P, w0 + (c + 1) * P)).then_inc(qk_done, 1)

                def values(i, slot, pair):
                    pe.wait_ge(v_ready, count(i * 2))
                    for t in (2 * pair, 2 * pair + 1):
                        for k in range(KC):
                            x = [v[:, k, t * P:(t + 1) * P] for v in ln.cut[slot]]
                            w = [v[:, k, w0 + 2 * D:w0 + 3 * D] for v in (K["wt_hi"], K["wt_lo"])]
                            mm = product3(nc, v_ps[:, pair, t % 2 * D:(t % 2 + 1) * D], x, w,
                                          k == 0, k == KC - 1)
                    mm.then_inc(v_done, 1)

                def blocks(half, i, slot, following):
                    pe.wait_ge(ln.lo_ready, count(i + 1))
                    pe.wait_ge(g_ready, count(i * 2))
                    project3(nc, g_ps[0:HD, 0, :], (K["g1_hi"], K["g1_lo"]), ln.cut[slot],
                             slice(0, HD)).then_inc(gh_done, 1)
                    queries_keys(i, slot, 0)
                    queries_keys(i, slot, 1)
                    if following:
                        ln.tensor_var(pe, i + 1)
                    pe.wait_ge(gh_lo_ready, count(i + 1))
                    for c in range(KC):
                        product3(nc, g_ps[:, c, :], [w[:, c * P:(c + 1) * P] for w in (K["g2_hi"], K["g2_lo"])],
                                 [v[:, :] for v in gh], True, True).then_inc(g_done, 1)
                    queries_keys(i, slot, 2)
                    queries_keys(i, slot, 3)
                    for pair in range(TT // 2):
                        values(i, slot, pair)
                    if following == 2:
                        mean(i + 2)

                mean(0)
                ln.tensor_var(pe, 0)
                mean(1)
                overlapped(pe, blocks)

            @block.scalar
            def _(act):
                def queries_keys(i, c):
                    act.wait_ge(qk_done, count(i * 4 + (c + 1)))
                    dst = R["Q1"] if c < 2 else R["K1"]
                    nc.scalar.activation(dst[:, c % 2, ds(i, TB)], qk_ps[:, c % 2, :],
                                         ACT.Silu if c < 2 else ACT.Identity,
                                         bias=qk_bias[:, c:c + 1]).then_inc(qk_ready, 1)

                def blocks(half, i, slot, following):
                    if following:
                        ln.scalar_square(act, i + 1)
                    act.wait_ge(gh_done, count(i + 1))
                    act.wait_ge(g_done, count(i * 2))
                    nc.scalar.activation(gh_full[:, :], g_ps[0:HD, 0, :], ACT.Identity,
                                         bias=g1_bias[:, 0:1]).then_inc(gh_full_ready, 1)
                    nc.scalar.activation(gh[0][:, :], g_ps[0:HD, 0, :], ACT.Identity,
                                         bias=g1_bias[:, 0:1]).then_inc(gh_hi_ready, 1)
                    queries_keys(i, 0)
                    queries_keys(i, 1)
                    if following:
                        ln.scalar_std(act, i + 1, K["eps"])
                    for c in range(KC):
                        act.wait_ge(g_done, count(i * 2 + (c + 1)))
                        nc.scalar.activation(R["G1"][:, c, ds(i, TB)], g_ps[:, c, :], ACT.Sigmoid,
                                             bias=g2_bias[:, c:c + 1]).then_inc(g_ready, 1)
                    queries_keys(i, 2)
                    queries_keys(i, 3)
                    if following:
                        ln.scalar_hi(act, i + 1, 1 - slot)

                ln.scalar_square(act, 0)
                ln.scalar_std(act, 0, K["eps"])
                ln.scalar_hi(act, 0, 0)
                act.wait_ge(consts, count(64))
                overlapped(act, blocks)

            @block.vector
            def _(dve):
                def values(i, pair):
                    dve.wait_ge(v_done, count(i * 2 + (pair + 1)))
                    nc.vector.tensor_tensor(
                        R["V1"][:, bass.ds(i * TT + 2 * pair, 2), :],
                        v_ps[:, pair, :].rearrange("p (a n) -> p a n", a=2),
                        v_bias[:, :].unsqueeze(1).to_broadcast([P, 2, D]), ALU.add).then_inc(v_ready, 1)

                def blocks(half, i, slot, following):
                    if following:
                        ln.vector_centre(dve, i + 1)
                    dve.wait_ge(gh_hi_ready, count(i + 1))
                    nc.vector.tensor_tensor(gh[1][:, :], gh_full[:, :], gh[0][:, :].bitcast(F32),
                                            ALU.subtract).then_inc(gh_lo_ready, 1)
                    if following:
                        for part in range(2):
                            ln.vector_reciprocal(dve, i + 1, part)
                        ln.vector_scale(dve, i + 1)
                    values(i, 0)
                    if following:
                        ln.vector_lo(dve, i + 1, 1 - slot)
                    values(i, 1)

                ln.vector_centre(dve, 0)
                for part in range(2):
                    ln.vector_reciprocal(dve, 0, part)
                ln.vector_scale(dve, 0)
                ln.vector_lo(dve, 0, 0)
                dve.wait_ge(consts, count(64))
                overlapped(dve, blocks)



def kv1_phase(nc, d, K, R):
    with ExitStack() as ctx:
        sb = lambda n, s, t: ctx.enter_context(nc.sbuf_tensor(n, s, t))
        sem = ctx.enter_context(PhaseSemaphores(nc, "kv1"))
        ps = lambda n, s: ctx.enter_context(nc.psum_tensor(n, s, F32))
        k_tok = sb("k_tok", [P, MC, D], F32)
        neg_max, total, r_total = (sb(n, [P, KC], F32) for n in ("k_neg_max", "k_total", "k_rtotal"))
        mask = sb("head_mask", [P, P], F32)
        kv_full = sb("kv_full", [P, KC, P], F32)
        turn_ps, kv_ps = ps("k_turn_ps", [P, 2, TB]), ps("kv_ps", [P, KC, TB])
        copied_even = sem("copied_even")
        mask_set, max_ready, exp_ready, turned, copied_odd, kv_done, r_ready, full_ready, hi_ready = (
            sem(n) for n in ("mask", "max", "exp", "turned", "copied_odd", "done", "r", "full", "hi"))
        PAIRS = MC // 2

        with nc.Block() as block:
            @block.gpsimd
            def _(pool):
                view = mask[:, :].rearrange("p (b j) -> p b j", j=HD)
                nc.gpsimd.memset(mask[:, :], 1.0).then_inc(mask_set, 1)
                pool.wait_ge(mask_set, 1)
                nc.gpsimd.affine_select(out=view, in_=view, compare_op=ALU.is_ge, fill=0.0, base=0,
                                        pattern=[[-HD, P // HD], [0, HD]],
                                        channel_multiplier=1).then_inc(mask_set, 1)
                pool.wait_ge(mask_set, 2)
                nc.gpsimd.affine_select(out=view, in_=view, compare_op=ALU.is_ge, fill=0.0, base=HD - 1,
                                        pattern=[[HD, P // HD], [0, HD]],
                                        channel_multiplier=-1).then_inc(mask_set, 1)

            @block.vector
            def _(dve):
                for k in range(KC):
                    nc.vector.tensor_reduce(neg_max[:, k:k + 1], R["K1"][:, k, :], AX.X, ALU.max,
                                            negate=True).then_inc(max_ready, 1)
                for m in range(1, PAIRS, 2):
                    dve.wait_ge(turned, m + 1)
                    nc.vector.tensor_copy(k_tok[:, 2 * m:2 * m + 2, :],
                                          turn_ps[:, 1, :].rearrange("p (a n) -> p a n", a=2)
                                          ).then_inc(copied_odd, 1)
                dve.wait_ge(exp_ready, KC)
                nc.vector.reciprocal(r_total[:, :], total[:, :]).then_inc(r_ready, 1)
                dve.wait_ge(r_ready, 1)
                dve.wait_ge(kv_done, 1)
                dve.wait_ge(mask_set, 3)
                for k in range(KC):
                    nc.vector.scalar_tensor_tensor(
                        out=kv_full[:, k, :], in0=kv_ps[:, k, 0:P], scalar=r_total[:, k:k + 1],
                        in1=mask[:, :], op0=ALU.mult, op1=ALU.mult).then_inc(full_ready, 1)
                dve.wait_ge(hi_ready, 1)
                nc.vector.tensor_tensor(R["kv"][1][:, :, :], kv_full[:, :, :], R["kv"][0][:, :, :].bitcast(F32),
                                        ALU.subtract)

            @block.scalar
            def _(act):
                for k in range(KC):
                    act.wait_ge(max_ready, k + 1)
                    nc.scalar.activation(R["K1"][:, k, :], R["K1"][:, k, :], ACT.Exp,
                                         bias=neg_max[:, k:k + 1],
                                         accum_out=total[:, k:k + 1]).then_inc(exp_ready, 1)
                for m in range(0, PAIRS, 2):
                    act.wait_ge(turned, m + 1)
                    nc.scalar.copy(k_tok[:, 2 * m:2 * m + 2, :],
                                   turn_ps[:, 0, :].rearrange("p (a n) -> p a n", a=2)
                                   ).then_inc(copied_even, 1)
                act.wait_ge(full_ready, KC)
                nc.scalar.copy(R["kv"][0][:, :, :], kv_full[:, :, :]).then_inc(hi_ready, 1)

            @block.tensor
            def _(pe):
                pe.wait_ge(exp_ready, KC)
                for m in range(PAIRS):
                    if m >= 2:
                        pe.wait_ge((copied_even, copied_odd)[m % 2], m // 2)
                    for a in range(2):
                        for k in range(KC):
                            tok = (2 * m + a) * P
                            mm = nc.tensor.transpose(turn_ps[:, m % 2, a * D + k * P:a * D + (k + 1) * P],
                                                     R["K1"][:, k, tok:tok + P], K["ident"][:, :])
                    mm.then_inc(turned, 1)
                for s in (copied_even, copied_odd):
                    pe.wait_ge(s, PAIRS // 2)
                for k in range(KC):
                    for t in range(MC):
                        mm = nc.tensor.matmul(kv_ps[:, k, 0:P], k_tok[:, t, k * P:(k + 1) * P],
                                              R["V1"][:, t, k * P:(k + 1) * P],
                                              start=(t == 0), stop=(t == MC - 1))
                mm.then_inc(kv_done, 1)



def out1_phase(nc, d, K, R):
    with ExitStack() as ctx:
        sb = lambda n, s, t: ctx.enter_context(nc.sbuf_tensor(n, s, t))
        sem = ctx.enter_context(PhaseSemaphores(nc, "out1"))
        ps = lambda n, s: ctx.enter_context(nc.psum_tensor(n, s, F32))
        SLOTS = range(2)
        of_slots = lambda make, n, *a: [make(f"{n}_slot{s}", *a) for s in SLOTS]
        q = [[sb(f"q1_{p}{s}", [P, KC, TB], F32R) for p in ("hi", "lo")] for s in SLOTS]
        o, x2, x3 = (of_slots(sb, n, [P, KC, TB], F32) for n in ("o1", "x2_res", "x3"))
        gain, offset, bias = (sb(n, [P, KC], F32) for n in ("ln_gain", "ln_offset", "b_out"))
        att_ps, out_ps = of_slots(ps, "att_ps", [P, KC, TB]), of_slots(ps, "out_ps", [P, KC, TB])
        consts = sem("consts")
        (x_loaded, q_hi, q_lo, att_done, o_ready, affine, gated, out_done, x3_ready, x3_stored) = (
            of_slots(sem, n) for n in ("x_loaded", "q_hi", "q_lo", "att_done", "o_ready", "affine",
                                       "gated", "out_done", "x3_ready", "x3_stored"))
        ln = [LayerNorm(f"ln3_slot{s}", nc, sb, sem, K["ones"], [o[s]], o_ready[s],
                        att_ps[s][:, 0, :], att_ps[s][:, 1, :]) for s in SLOTS]
        wout = chunk_of("L1_attn_w_out")

        sem.start()
        with nc.Block() as block:
            @block.sync
            def _(sp):
                for dst, name in ((gain, "L1_attn_ln_g"), (offset, "L1_attn_ln_b"), (bias, "L1_attn_b_out")):
                    sp.dma_start(dst[:, :], column(d[name]), allow_slow_non_contiguous=True).then_inc(consts, 16)
                with sp.Fori(0, NB // 2) as i:
                    for s in SLOTS:
                        sp.wait_ge(x3_ready[s], count(i))
                        sp.dma_start(x2[s][:, :, :], feature_major(d["X2T"])[:, :, ds(i * 2 + s, TB)]
                                     ).then_inc(x_loaded[s], 16)
                    for s in SLOTS:
                        sp.wait_ge(x3_ready[s], count(i + 1))
                        sp.dma_start(feature_major(d["X3T"])[:, :, ds(i * 2 + s, TB)], x3[s][:, :, :]
                                     ).then_inc(x3_stored[s], 16)
                for s in SLOTS:
                    sp.wait_ge(x3_stored[s], count(16 * NB // 2))

            @block.tensor
            def _(pe):
                def attend(i):
                    for s in SLOTS:
                        pe.wait_ge(q_lo[s], count(i + 1))
                        for k in range(KC):
                            mm = product3(nc, att_ps[s][:, k, :], [w[:, k, :] for w in R["kv"]],
                                          [v[:, k, :] for v in q[s]], True, True)
                        mm.then_inc(att_done[s], 1)

                def blocks(i, following):
                    for s in SLOTS:
                        ln[s].tensor_mean(pe, i)
                    for s in SLOTS:
                        ln[s].tensor_var(pe, i)
                    for s in SLOTS:
                        pe.wait_ge(ln[s].lo_ready, count(i + 1))
                        pe.wait_ge(x3_ready[s], count(i))
                        for n in range(KC):
                            mm = project3(nc, out_ps[s][:, n, :], (K["wt_hi"], K["wt_lo"]), ln[s].cut[0],
                                          slice(wout + n * P, wout + (n + 1) * P))
                        mm.then_inc(out_done[s], 1)
                        if following and s == 0:
                            attend(i + 1)

                attend(0)
                with pe.Fori(0, NB // 2 - 1) as i:
                    blocks(i, True)
                blocks(NB // 2 - 1, False)

            @block.scalar
            def _(act):
                def cut_q(i):
                    for s in SLOTS:
                        act.wait_ge(att_done[s], count(i))
                        nc.scalar.copy(q[s][0][:, :, :], R["Q1"][:, :, ds(i * 2 + s, TB)]).then_inc(q_hi[s], 1)

                def copy_o(i):
                    for s in SLOTS:
                        act.wait_ge(att_done[s], count(i + 1))
                        nc.scalar.copy(o[s][:, :, :], att_ps[s][:, :, :]).then_inc(o_ready[s], 1)

                def blocks(i, following):
                    for s in SLOTS:
                        ln[s].scalar_square(act, i)
                    for s in SLOTS:
                        ln[s].scalar_std(act, i, K["eps"])
                    if following:
                        cut_q(i + 1)
                    for s in SLOTS:
                        act.wait_ge(ln[s].normed, count(i + 1))
                        for k in range(KC):
                            nc.scalar.activation(ln[s].xc[:, k, :], ln[s].xn[:, k, :], ACT.Identity,
                                                 bias=offset[:, k:k + 1], scale=gain[:, k:k + 1]
                                                 ).then_inc(affine[s], 1)
                    for s in SLOTS:
                        act.wait_ge(gated[s], count(i + 1))
                        nc.scalar.copy(ln[s].cut[0][0][:, :, :], ln[s].xn[:, :, :]).then_inc(ln[s].hi_ready, 1)
                    if following:
                        copy_o(i + 1)

                cut_q(0)
                copy_o(0)
                act.wait_ge(consts, count(48))
                with act.Fori(0, NB // 2 - 1) as i:
                    blocks(i, True)
                blocks(NB // 2 - 1, False)

            @block.vector
            def _(dve):
                def q_rest(i):
                    for s in SLOTS:
                        dve.wait_ge(q_hi[s], count(i + 1))
                        nc.vector.tensor_tensor(q[s][1][:, :, :], R["Q1"][:, :, ds(i * 2 + s, TB)],
                                                q[s][0][:, :, :].bitcast(F32), ALU.subtract).then_inc(q_lo[s], 1)

                def blocks(i, following):
                    for s in SLOTS:
                        ln[s].vector_centre(dve, i)
                    for s in SLOTS:
                        for part in range(2):
                            ln[s].vector_reciprocal(dve, i, part)
                        ln[s].vector_scale(dve, i)
                    for s in SLOTS:
                        dve.wait_ge(affine[s], count((i + 1) * KC))
                        nc.vector.tensor_tensor(ln[s].xn[:, :, :], ln[s].xc[:, :, :],
                                                R["G1"][:, :, ds(i * 2 + s, TB)], ALU.mult).then_inc(gated[s], 1)
                    for s in SLOTS:
                        ln[s].vector_lo(dve, i)
                    if following:
                        q_rest(i + 1)
                    for s in SLOTS:
                        dve.wait_ge(out_done[s], count(i + 1))
                        dve.wait_ge(x_loaded[s], count((i + 1) * 16))
                        dve.wait_ge(x3_stored[s], count(i * 16))
                        for n in range(KC):
                            ins = nc.vector.scalar_tensor_tensor(
                                out=x3[s][:, n, :], in0=out_ps[s][:, n, :], scalar=bias[:, n:n + 1],
                                in1=x2[s][:, n, :], op0=ALU.add, op1=ALU.add)
                        ins.then_inc(x3_ready[s], 1)

                q_rest(0)
                dve.wait_ge(consts, count(48))
                with dve.Fori(0, NB // 2 - 1) as i:
                    blocks(i, True)
                blocks(NB // 2 - 1, False)



E = 64
TOP = 8
EH = 64
PAIRS = E * EH // P
SH = 1024
SC = SH // P


def moe_phase(nc, d, K):
    with ExitStack() as wctx:
        wsb = lambda n, s, t: wctx.enter_context(nc.sbuf_tensor(n, s, t))
        w1 = [wsb(f"moe_w1_{p}", [P, KC, E * EH], F32R) for p in ("hi", "lo")]
        w2 = [wsb(f"moe_w2_{p}", [P, PAIRS, D], F32R) for p in ("hi", "lo")]
        s1 = [wsb(f"moe_s1_{p}", [P, KC, SH], F32R) for p in ("hi", "lo")]
        s2 = [wsb(f"moe_s2_{p}", [P, SC, D], F32R) for p in ("hi", "lo")]
        rw = [wsb(f"moe_rw_{p}", [P, KC, E], F32R) for p in ("hi", "lo")]
        items = []
        items.append((d["L1_ffn_router_w"].rearrange("(k p) e -> p k e", p=P), *[v[:, :, :] for v in rw]))
        G = 16
        for g in range(E // G):
            for k in range(KC):
                src = d["L1_ffn_w1"][g * G:(g + 1) * G, k * P:(k + 1) * P, :].rearrange("e p h -> p e h")
                items.append((src, *[v[:, k, g * G * EH:(g + 1) * G * EH].rearrange("p (e h) -> p e h", e=G)
                                     for v in w1]))
            for a in range(G // 8):
                lo_e = g * G + a * 8
                src = d["L1_ffn_w2"].rearrange("e h n -> (e h) n")[lo_e * EH:(lo_e + 8) * EH].rearrange(
                    "(a p) n -> p a n", p=P)
                items.append((src, *[v[:, lo_e // 2:lo_e // 2 + 4, :] for v in w2]))
        for s in range(2):
            half = SH // 2
            for k in range(KC):
                src = d["L1_ffn_sw1"][s, k * P:(k + 1) * P, :].rearrange("p (o h) -> p o h", o=1)
                items.append((src, *[v[:, k:k + 1, s * half:(s + 1) * half] for v in s1]))
            src = d["L1_ffn_sw2"][s].rearrange("(c p) n -> p c n", p=P)
            items.append((src, *[v[:, s * SC // 2:(s + 1) * SC // 2, :] for v in s2]))
        moe_blocks(nc, d, K, w1, w2, s1, s2, rw, items)


HEAD = 3


def moe_blocks(nc, d, K, w1, w2, s1, s2, rw, items):
    with ExitStack() as ctx:
        sb = lambda n, s, t: ctx.enter_context(nc.sbuf_tensor(n, s, t))
        sem = ctx.enter_context(PhaseSemaphores(nc, "moe"))
        ps = lambda n, s: ctx.enter_context(nc.psum_tensor(n, s, F32))
        x = sb("m_x", [P, KC, TB], F32)
        h_full = sb("m_h_full", [P, RING, TB], F32)
        h = [sb(f"m_h_{p}", [P, RING, TB], F32R) for p in ("hi", "lo")]
        best, row_max, row_sum = sb("best", [P, TT, TOP], F32), sb("row_max", [P, TT], F32), sb("row_sum", [P, TT], F32)
        cw = sb("cw", [P, TB], F32R)
        pick = sb("pick", [P, E], F32)
        pick_pair = sb("pick_pair", [P, 2, 2, EH], F32R)
        r_bias = sb("r_bias", [P, E], F32)
        b1, s_b1, s_b2 = sb("m_b1", [P, PAIRS], F32), sb("m_sb1", [P, SC], F32), sb("m_sb2", [P, 2, KC], F32)
        b2_sum = sb("m_b2_sum", [P, KC], F32)
        b2 = [sb(f"m_b2_{p}", [P, D], F32R) for p in ("hi", "lo")]
        turn_ps, h_ps, c_ps, y_ps = (ps(n, [P, 2, TB]) for n in ("m_turn", "m_h", "m_c", "m_y"))
        (consts, pick_set, b_cut, x_loaded, x_reloaded, logit_done, logit_ready, max_ready,
         cent_ready, exp_ready, best_ready, drop_ready, kept_ready, sum_ready, r_ready, cw_ready, cw_turned,
         cw_hi, cw_lo, h_done, spread, full_ready, hi_ready, lo_ready, h_free, x4_ready, out_turned,
         out_ready, out_stored, kept_weights, picked, dve_passed, pe_passed, passed) = (
            sem(n) for n in (
                "consts", "pick", "b_cut", "x_loaded", "x_reloaded", "logit_done",
                "logit_ready", "max", "cent", "exp", "best", "drop", "kept", "sum", "r", "cw", "cw_turned",
                "cw_hi", "cw_lo", "h_done", "spread", "full", "hi", "lo", "h_free", "x4", "out_turned",
                "out_ready", "out_stored", "kept_weights", "picked", "dve_passed", "pe_passed",
                "pool_passed"))
        sp_passed = sem("sp_passed")
        ln = LayerNorm("ln4", nc, sb, sem, K["ones"], [x], x_loaded, turn_ps[:, 0, :], turn_ps[:, 1, :])
        logits, dropped = (ln.xc[:, k, 0:TT * E].rearrange("p (t e) -> p t e", t=TT) for k in range(2))
        b2_raw = h_full[:, 2, 0:D]
        places = [v[:, 0:2, :].rearrange("p a n -> p (a n)") for v in (h_full, ln.sq, ln.xc, x)]
        weights = WeightCut(nc, sem, items, places)
        out_tok = ln.sq[:, :, :].rearrange("p k n -> p (k n)").rearrange("p (t f) -> p t f", t=TT)
        out_dram = d["out"].rearrange("a (t p) n -> p (a t) n", p=P)
        x3_dram = feature_major(d["X3T"])
        C = SC + PAIRS

        def heads_and_tails(eng, head, tail):
            head(0, False)
            with eng.Fori(0, NB - 1) as i:
                tail(i, True)
                head(i + 1, True)
            tail(NB - 1, False)

        sem.start()
        with nc.Block() as block:
            @block.sync
            def _(sp):
                def col(dst, src):
                    sp.dma_start(dst, src, allow_slow_non_contiguous=True).then_inc(consts, 16)

                sp.dma_start(r_bias[:, :], d["L1_ffn_router_b"].partition_broadcast(P)).then_inc(consts, 16)
                col(b1[:, :], column(d["L1_ffn_b1"].rearrange("e h -> (e h)")))
                col(s_b1[:, :], column(d["L1_ffn_sb1"].rearrange("e h -> (e h)")))
                for s in range(2):
                    col(s_b2[:, s, :], column(d["L1_ffn_sb2"][s]))
                    sp.dma_start(b2_raw[s * E:(s + 1) * E, :], d["L1_ffn_b2"]).then_inc(consts, 16)
                weights.load(sp)
                weights.ready(sp)
                sp.dma_start(x[:, :, :], x3_dram[:, :, 0:TB]).then_inc(x_loaded, 16)
                sp.wait_ge(ln.centred, count(1))
                with sp.Fori(0, NB - 1) as i:
                    sp.dma_start(x[:, :, :], x3_dram[:, :, ds(i + 1, TB)]).then_inc(x_loaded, 16)
                    sp.wait_ge(ln.centred, count(i + 2))
                    alone(sp, sp_passed)
                    sp.dma_start(x[:, :, :], x3_dram[:, :, ds(i, TB)]).then_inc(x_reloaded, 16)
                    sp.wait_ge(out_ready, count((i + 1) * 2))
                    sp.dma_start(out_dram[:, ds(i, TT), :], out_tok).then_inc(out_stored, 16)
                sp.dma_start(x[:, :, :], x3_dram[:, :, (NB - 1) * TB:]).then_inc(x_reloaded, 16)
                sp.wait_ge(out_ready, count(2 * NB))
                sp.dma_start(out_dram[:, (NB - 1) * TT:, :], out_tok).then_inc(out_stored, 16)
                sp.wait_ge(out_stored, count(16 * NB))

            @block.gpsimd
            def _(pool):
                nc.gpsimd.memset(pick[:, :], 0.0).then_inc(pick_set, 1)
                for n, base in enumerate((0, -E)):
                    pool.wait_ge(pick_set, count(n + 1))
                    nc.gpsimd.affine_select(out=pick[:, :], in_=pick[:, :], compare_op=ALU.not_equal,
                                            fill=1.0, base=base, pattern=[[-1, E]],
                                            channel_multiplier=1).then_inc(pick_set, 1)
                pool.wait_ge(pick_set, count(3))
                with pool.Fori(0, NB) as i:
                    for p in range(PAIRS):
                        pool.wait_ge(spread, count(i * PAIRS + max(p - 1, 0)))
                        alone(pool, passed)
                        nc.gpsimd.tensor_copy(pick_pair[:, p % 2, :, :],
                                              pick[:, 2 * p:2 * p + 2].unsqueeze(2).to_broadcast([P, 2, EH])
                                              ).then_inc(picked, 1)
                        pool.wait_ge(picked, count(i * PAIRS + (p + 1)))

            @block.tensor
            def _(pe):
                def hidden(i, c):
                    pe.wait_ge(full_ready, count(i * C + max(c - 1, 0)))
                    if c < SC:
                        w, cols = s1, slice(c * P, (c + 1) * P)
                    else:
                        w, cols = w1, slice((c - SC) * P, (c - SC + 1) * P)
                    project3(nc, h_ps[:, c % 2, :], w, ln.cut[0], cols).then_inc(h_done, 1)
                    if c >= SC:
                        p = c - SC
                        if p == 0:
                            pe.wait_ge(cw_lo, count(i + 1))
                            pe.wait_ge(out_ready, count(i * 2))
                        pe.wait_ge(kept_ready, count(i * PAIRS + max(p - 1, 0)))
                        pe.wait_ge(picked, count(i * PAIRS + (p + 1)))
                        nc.tensor.matmul(c_ps[:, c % 2, :],
                                         pick_pair[:, p % 2, :, :].rearrange("q a b -> q (a b)"),
                                         cw[:, :], start=True, stop=True).then_inc(spread, 1)

                def output(i, c):
                    w, k = (s2, c) if c < SC else (w2, c - SC)
                    pe.wait_ge(lo_ready, count(i * C + (c + 1)))
                    if c == 0:
                        pe.wait_ge(x4_ready, count(i))
                    for n in range(KC):
                        mm = product3(nc, y_ps[:, n, :], [v[:, k, n * P:(n + 1) * P] for v in w],
                                      [v[:, c % RING, :] for v in h], c == 0, c == C - 1)
                    mm.then_inc(h_free, 1)

                def second_bias():
                    for n in range(KC):
                        for p in range(2):
                            nc.tensor.matmul(y_ps[:, n, :], b2[p][:, n * P:(n + 1) * P], cw[:, :],
                                             start=False, stop=False)

                def turn_output(i):
                    pe.wait_ge(x4_ready, count(i + 1))
                    alone(pe, pe_passed)
                    for k in range(KC):
                        for t in range(TT):
                            mm = nc.tensor.transpose(
                                c_ps[:, t // 2, t % 2 * D + k * P:t % 2 * D + (k + 1) * P],
                                x[:, k, t * P:(t + 1) * P], K["ident"][:, :])
                    mm.then_inc(out_turned, 1)

                def head(i, finish):
                    pe.wait_ge(ln.lo_ready, count(i + 1))
                    for t in range(TT):
                        for k in range(KC):
                            mm = product3(nc, turn_ps[:, 0, t * E:(t + 1) * E],
                                          [v[:, k, t * P:(t + 1) * P] for v in ln.cut[0]],
                                          [v[:, k, :] for v in rw], k == 0, k == KC - 1)
                    mm.then_inc(logit_done, 1)
                    for c in range(HEAD):
                        hidden(i, c)
                        if c >= LAG:
                            output(i, c - LAG)
                    if finish:
                        turn_output(i - 1)

                def tail(i, following):
                    for c in range(HEAD, C):
                        hidden(i, c)
                        output(i, c - LAG)
                        if c == SC - 1:
                            pe.wait_ge(cw_ready, count(i + 1))
                            alone(pe, pe_passed)
                            for t in range(TT):
                                mm = nc.tensor.transpose(turn_ps[0:E, 1, t * P:(t + 1) * P], dropped[:, t, :],
                                                         K["ident"][:, :])
                            mm.then_inc(cw_turned, 1)
                        if following and c == 12:
                            pe.wait_ge(x_loaded, count((i + 2) * 16))
                            ln.tensor_mean_of_ready()
                        if following and c == 16:
                            ln.tensor_var(pe, i + 1)
                    output(i, C - 2)
                    second_bias()
                    output(i, C - 1)

                pe.wait_ge(b_cut, count(3))
                pe.wait_ge(x_loaded, count(16))
                ln.tensor_mean_of_ready()
                ln.tensor_var(pe, 0)
                weights.ready(pe)
                heads_and_tails(pe, head, tail)
                turn_output(NB - 1)

            @block.scalar
            def _(act):
                def chunk(i, c):
                    act.wait_ge(h_done, count(i * C + (c + 1)))
                    act.wait_ge(h_free, count(i * C + (c + 1)))
                    bias = s_b1[:, c:c + 1] if c < SC else b1[:, c - SC:c - SC + 1]
                    nc.scalar.activation(h_full[:, c % RING, :], h_ps[:, c % 2, :], ACT.Silu,
                                         bias=bias).then_inc(full_ready, 1)
                    if c < SC:
                        act.wait_ge(full_ready, count(i * C + (c + 1)))
                    else:
                        act.wait_ge(kept_ready, count(i * PAIRS + (c - SC + 1)))
                    nc.scalar.copy(h[0][:, c % RING, :], h_full[:, c % RING, :]).then_inc(hi_ready, 1)

                def copy_output(i):
                    act.wait_ge(out_turned, count(i + 1))
                    for t in range(2):
                        nc.scalar.copy(out_tok[:, 2 * t:2 * t + 2, :],
                                       c_ps[:, t, :].rearrange("p (a n) -> p a n", a=2)).then_inc(out_ready, 1)

                def head(i, finish):
                    for c in range(HEAD):
                        chunk(i, c)
                    if finish:
                        copy_output(i - 1)

                def tail(i, following):
                    for c in range(HEAD, C):
                        if c == HEAD + 1:
                            act.wait_ge(cent_ready, count(i + 1))
                            nc.scalar.activation(logits[:, :, :], logits[:, :, :], ACT.Exp).then_inc(exp_ready, 1)
                        if following and c == 14:
                            act.wait_ge(out_stored, count(i * 16))
                            ln.scalar_square(act, i + 1)
                        if following and c == 18:
                            ln.scalar_std(act, i + 1, K["eps"])
                        chunk(i, c)
                    if following:
                        ln.scalar_hi(act, i + 1)

                act.sem_inc(h_free, RING)
                act.wait_ge(consts, count(16 * 7))
                nc.scalar.copy(b2[0][:, :], b2_raw).then_inc(b_cut, 1)
                for n in range(len(items)):
                    weights.hi(act, n)
                ln.scalar_square(act, 0)
                ln.scalar_std(act, 0, K["eps"])
                ln.scalar_hi(act, 0)
                heads_and_tails(act, head, tail)
                copy_output(NB - 1)

            @block.vector
            def _(dve):
                def router(i, step):
                    if step == "centre":
                        dve.wait_ge(logit_done, count(i + 1))
                        nc.vector.tensor_tensor(
                            logits[:, :, :], turn_ps[:, 0, 0:TT * E].rearrange("p (t e) -> p t e", t=TT),
                            r_bias[:, :].unsqueeze(1).to_broadcast([P, TT, E]), ALU.add).then_inc(logit_ready, 1)
                        dve.wait_ge(logit_ready, count(i + 1))
                        nc.vector.tensor_reduce(row_max[:, :], logits[:, :, :], AX.X,
                                                ALU.max).then_inc(max_ready, 1)
                        dve.wait_ge(max_ready, count(i + 1))
                        nc.vector.tensor_tensor(logits[:, :, :], logits[:, :, :],
                                                row_max[:, :].unsqueeze(2).to_broadcast([P, TT, E]),
                                                ALU.subtract).then_inc(cent_ready, 1)
                    elif step == "best":
                        dve.wait_ge(exp_ready, count(i + 1))
                        alone(dve, dve_passed)
                        for t in range(TT):
                            nc.vector.max(best[:, t, :], logits[:, t, :]).then_inc(best_ready, 1)
                    elif step == "drop":
                        dve.wait_ge(best_ready, count((i + 1) * TT))
                        dve.wait_ge(cw_turned, count(i))
                        alone(dve, dve_passed)
                        for t in range(TT):
                            nc.vector.match_replace(dropped[:, t, :], best[:, t, :], logits[:, t, :],
                                                    0.0).then_inc(drop_ready, 1)
                        nc.vector.tensor_reduce(row_sum[:, :], best[:, :, :], AX.X, ALU.add).then_inc(sum_ready, 1)
                        dve.wait_ge(sum_ready, count(i + 1))
                        nc.vector.reciprocal(row_sum[:, :], row_sum[:, :]).then_inc(r_ready, 1)
                    elif step == "weights":
                        dve.wait_ge(drop_ready, count((i + 1) * TT))
                        nc.vector.tensor_tensor(logits[:, :, :], logits[:, :, :], dropped[:, :, :],
                                                ALU.subtract).then_inc(kept_weights, 1)
                        dve.wait_ge(r_ready, count(i + 1))
                        dve.wait_ge(kept_weights, count(i + 1))
                        nc.vector.tensor_tensor(dropped[:, :, :], logits[:, :, :],
                                                row_sum[:, :].unsqueeze(2).to_broadcast([P, TT, E]),
                                                ALU.mult).then_inc(cw_ready, 1)
                    elif step == "cut":
                        dve.wait_ge(cw_turned, count(i + 1))
                        dve.wait_ge(h_free, count(i * C + RING))
                        nc.vector.tensor_copy(cw[0:E, :], turn_ps[0:E, 1, :]).then_inc(cw_hi, 1)
                        dve.wait_ge(cw_hi, count(i + 1))
                        nc.vector.tensor_tensor(cw[E:2 * E, :], turn_ps[0:E, 1, :], cw[0:E, :].bitcast(F32),
                                                ALU.subtract).then_inc(cw_lo, 1)

                def chunk(i, c):
                    if c >= SC:
                        dve.wait_ge(full_ready, count(i * C + (c + 1)))
                        dve.wait_ge(spread, count(i * PAIRS + (c - SC + 1)))
                        nc.vector.tensor_tensor(h_full[:, c % RING, :], h_full[:, c % RING, :], c_ps[:, c % 2, :],
                                                ALU.mult).then_inc(kept_ready, 1)
                    dve.wait_ge(hi_ready, count(i * C + (c + 1)))
                    nc.vector.tensor_tensor(h[1][:, c % RING, :], h_full[:, c % RING, :],
                                            h[0][:, c % RING, :].bitcast(F32),
                                            ALU.subtract).then_inc(lo_ready, 1)

                def head(i, finish):
                    chunk(i, 0)
                    router(i, "centre")
                    for c in range(1, HEAD):
                        chunk(i, c)

                def tail(i, following):
                    for c in range(HEAD, C):
                        chunk(i, c)
                        router(i, {4: "best", 5: "drop", 6: "weights", 7: "cut"}.get(c))
                        if following and c == 13:
                            ln.vector_centre(dve, i + 1)
                        if following and c in (19, 21):
                            ln.vector_reciprocal(dve, i + 1, (c - 19) // 2)
                        if following and c == 22:
                            ln.vector_scale(dve, i + 1)
                    if following:
                        ln.vector_lo(dve, i + 1)
                    dve.wait_ge(h_free, count((i + 1) * C + RING))
                    dve.wait_ge(x_reloaded, count((i + 1) * 16))
                    for n in range(KC):
                        ins = nc.vector.scalar_tensor_tensor(
                            out=x[:, n, :], in0=y_ps[:, n, :], scalar=b2_sum[:, n:n + 1],
                            in1=x[:, n, :], op0=ALU.add, op1=ALU.add)
                    ins.then_inc(x4_ready, 1)

                dve.wait_ge(consts, count(16 * 7))
                nc.vector.tensor_tensor(b2_sum[:, :], s_b2[:, 0, :], s_b2[:, 1, :], ALU.add).then_inc(b_cut, 1)
                dve.wait_ge(b_cut, count(2))
                nc.vector.tensor_tensor(b2[1][:, :], b2_raw, b2[0][:, :].bitcast(F32),
                                        ALU.subtract).then_inc(b_cut, 1)
                for n in range(len(items)):
                    weights.lo(dve, n)
                weights.ready(dve)
                ln.vector_centre(dve, 0)
                for part in range(2):
                    ln.vector_reciprocal(dve, 0, part)
                ln.vector_scale(dve, 0)
                ln.vector_lo(dve, 0)
                heads_and_tails(dve, head, tail)



def scratch(nc):
    t = lambda n, s, dt: nc.dram_tensor(n, s, dt).ap()
    return {"X0T": t("X0T", (D, T), F32), "QS": t("QS", (PARTS, D, T), BF16),
            "KS": t("KS", (PARTS, D, T), BF16), "NUM": t("NUM", (D, T), F32), "DEN": t("DEN", (D, T), F32),
            "X2T": t("X2T", (D, T), F32), "X3T": t("X3T", (D, T), F32)}


def program(nc, d):
    d = {**d, **scratch(nc)}
    with ExitStack() as ctx:
        sb = lambda n, s, t: ctx.enter_context(nc.sbuf_tensor(n, s, t))
        K = {"ident": sb("ident", [P, P], F32), "ident_b": sb("ident_b", [P, P], BF16),
             "ones": sb("ones", [P, P], F32), "eps": sb("eps", [P, 1], F32)}
        with ExitStack() as weights:
            wsb = lambda n, s: weights.enter_context(nc.sbuf_tensor(n, s, F32R))
            K |= {f"wt_{p}": wsb(f"wt_{p}", [P, KC, CHUNKS * P]) for p in ("hi", "lo")}
            K |= {f"g1_{p}": wsb(f"g1_{p}", [P, KC, HD]) for p in ("hi", "lo")}
            K |= {f"g2_{p}": wsb(f"g2_{p}", [HD, D]) for p in ("hi", "lo")}
            setup_phase(nc, d, K)
            with ExitStack() as att:
                V_all = att.enter_context(nc.sbuf_tensor("V_all", [P, MC, D], F32))
                qkv0_phase(nc, d, K, V_all)
                attention_phase(nc, d, K, V_all)
            ffn0_phase(nc, d, K)
            with ExitStack() as layer1:
                rsb = lambda n, s, t: layer1.enter_context(nc.sbuf_tensor(n, s, t))
                R = {n: rsb(n, [P, KC, T], F32) for n in ("Q1", "G1")}
                R["kv"] = [rsb(f"kv_{p}", [P, KC, P], F32R) for p in ("hi", "lo")]
                with ExitStack() as keys_values:
                    ksb = lambda n, s: keys_values.enter_context(nc.sbuf_tensor(n, s, F32))
                    R["K1"], R["V1"] = ksb("K1", [P, KC, T]), ksb("V1", [P, MC, D])
                    qkv1_phase(nc, d, K, R)
                    kv1_phase(nc, d, K, R)
                out1_phase(nc, d, K, R)
        moe_phase(nc, d, K)



def kernel(**inputs):
    import numpy as np
    from concourse import bacc
    from concourse.bass_utils import run_bass_kernel_spmd

    nc = bacc.Bacc("TRN2", target_bir_lowering=False, num_devices=1)
    arrays, d = {}, {}
    for name, value in inputs.items():
        a = np.ascontiguousarray(value)
        arrays[f"in_{name}"] = a
        d[name] = nc.dram_tensor(f"in_{name}", a.shape, mybir.dt.from_np(a.dtype), kind="ExternalInput").ap()
    d["out"] = nc.dram_tensor("out_0", (1, T, D), F32, kind="ExternalOutput").ap()
    program(nc, d)
    r = run_bass_kernel_spmd(nc, [arrays], core_ids=[0])
    return r.results[0]["out_0"]
```
